# Optimizing a Trainium2 kernel written in Bass

```python
import numpy as np
import jax
import jax.numpy as jnp

def _softmax(x, axis=-1):
    return jax.nn.softmax(x, axis=axis)

def _gelu(x):
    return jax.nn.gelu(x, approximate=True)

def _silu(x):
    return jax.nn.silu(x)

def _sigmoid(x):
    return jax.nn.sigmoid(x)

def _layernorm(x, axis=-1, eps=1e-05):
    m = jnp.mean(x, axis=axis, keepdims=True)
    v = jnp.var(x, axis=axis, keepdims=True)
    return (x - m) / jnp.sqrt(v + eps)

def _scatter_add(tgt, idx, src, axis=0):
    return tgt.at[idx].add(src)

def _segment_sum(src, seg, n):
    return jax.ops.segment_sum(src, seg, n)
kernel_name = 'mk_perceiver_d2_seqx_r8_4d8f72'

def setup_inputs(seed: int=0):
    np.random.seed(seed)
    _w = jnp.asarray

    def _rec_inputs():
        import jax
        import jax.numpy as jnp
        _rk = jax.random.key(seed)
        x = -0.0002928 + 1 * jax.random.normal(jax.random.fold_in(_rk, 1), (32, 64, 128), jnp.float32)
        _lenS = 64 - jax.random.randint(jax.random.fold_in(_rk, 7), (32,), 0, max(1, 64 // 4) + 1, jnp.int32)
        _lenS2 = 128 - jax.random.randint(jax.random.fold_in(_rk, 8), (32,), 0, max(1, 128 // 4) + 1, jnp.int32)
        _ctx_1024P = jax.random.normal(jax.random.fold_in(_rk, 11), (32, 16, 128), jnp.float32)
        _ctx_1024c = jax.random.dirichlet(jax.random.fold_in(_rk, 511), 0.3 * jnp.ones((16,), jnp.float32), (32, 128))
        _ctx_1024t = jnp.einsum('bsk,bkd->bsd', _ctx_1024c, _ctx_1024P)
        _ctx_1024t = _ctx_1024t * jax.lax.rsqrt(jnp.mean(jnp.square(_ctx_1024t)) + 1e-12) * 0.953939
        ctx_1024 = -1.39393e-06 + 0.999914 * (_ctx_1024t + 0.3 * jax.random.normal(jax.random.fold_in(_rk, 611), (32, 128, 128), jnp.float32))
        _validS = jnp.arange(64)[None, :] < _lenS[:, None]
        _validS2 = jnp.arange(128)[None, :] < _lenS2[:, None]
        _causal = jnp.tril(jnp.ones((64, 64), dtype=bool))
        mask_Bx1xSxS2_ik1 = jnp.where(jnp.broadcast_to(_validS2[:, None, None, :], (32, 1, 64, 128)), 1, 0).astype(jnp.int32)
        return (x, ctx_1024, mask_Bx1xSxS2_ik1)
    x, ctx_1024, mask_Bx1xSxS2_ik1 = _rec_inputs()

    def _L0_xattn_setup():
        import jax, jax.numpy as jnp
        import numpy as np
        import math
        D_MODEL = 128
        HEADS = 16
        DK = 64
        DV = 64
        key = jax.random.key(seed)
        ks = jax.random.split(key, 8)
        N, QL, KL = (2, 256, 256)
        s = 1.0 / math.sqrt(D_MODEL)
        return {'Q': jax.random.normal(ks[0], (N, QL, D_MODEL), jnp.float32), 'K': jax.random.normal(ks[1], (N, KL, D_MODEL), jnp.float32), 'V': jax.random.normal(ks[2], (N, KL, D_MODEL), jnp.float32), 'WQ': jax.random.normal(ks[3], (D_MODEL, HEADS * DK), jnp.float32) * s, 'WK': jax.random.normal(ks[4], (D_MODEL, HEADS * DK), jnp.float32) * s, 'WV': jax.random.normal(ks[5], (D_MODEL, HEADS * DV), jnp.float32) * s, 'WO': jax.random.normal(ks[6], (HEADS * DV, D_MODEL), jnp.float32) * (1.0 / math.sqrt(HEADS * DV)), 'bO': jnp.zeros((D_MODEL,), jnp.float32)}
    _L0_xattn_all = _L0_xattn_setup()
    _L0_xattn_in = {k: v for k, v in _L0_xattn_all.items() if k in ('WQ', 'WK', 'WV', 'WO', 'bO')}
    del _L0_xattn_all

    def _L0_attn_setup():
        import jax, jax.numpy as jnp
        import numpy as np
        DIM = 128
        HEADS = 16
        HIDDEN = 256
        EPS = 1e-06

        def _rmsnorm(x, scale):
            norm = jnp.linalg.norm(x, axis=-1, keepdims=True)
            return x * (scale * (x.shape[-1] ** 0.5 + EPS) / norm)
        key = jax.random.key(seed)
        ks = jax.random.split(key, 8)
        B, N, C = (4, 512, DIM)
        s = 0.02
        return {'x': jax.random.normal(ks[0], (B, N, C), dtype=jnp.float32), 'scale1': jnp.ones((C,), jnp.float32), 'scale2': jnp.ones((C,), jnp.float32), 'gamma': jnp.ones((C,), jnp.float32), 'qkv_w': jax.random.normal(ks[1], (3 * C, C), jnp.float32) * s, 'proj_w': jax.random.normal(ks[2], (C, C), jnp.float32) * s, 'proj_b': jnp.zeros((C,), jnp.float32), 'conv1_w': jax.random.normal(ks[3], (HIDDEN, C), jnp.float32) * s, 'conv1_b': jnp.zeros((HIDDEN,), jnp.float32), 'conv2_w': jax.random.normal(ks[4], (C, HIDDEN), jnp.float32) * s, 'conv2_b': jnp.zeros((C,), jnp.float32)}
    _L0_attn_all = _L0_attn_setup()
    _L0_attn_in = {k: v for k, v in _L0_attn_all.items() if k in ('scale1', 'scale2', 'gamma', 'qkv_w', 'proj_w', 'proj_b', 'conv1_w', 'conv1_b', 'conv2_w', 'conv2_b')}
    del _L0_attn_all

    def _L0_ffn_setup():
        import jax, jax.numpy as jnp
        import numpy as np
        B, S, D, H, E = (4, 256, 128, 16, 4)
        key = jax.random.key(seed)
        ks = jax.random.split(key, 8)
        w = lambda k, shape: jax.random.normal(k, shape, jnp.float32) * 0.02
        return {'x': jax.random.normal(ks[0], (B, S, D), jnp.float32), 'router_w': w(ks[1], (D, E)), 'router_b': jnp.zeros((E,), jnp.float32), 'wq': w(ks[2], (E, D, D)), 'bq': jnp.zeros((E, D), jnp.float32), 'wk': w(ks[3], (E, D, D)), 'bk': jnp.zeros((E, D), jnp.float32), 'wv': w(ks[4], (E, D, D)), 'bv': jnp.zeros((E, D), jnp.float32), 'wo': w(ks[5], (E, D, D)), 'bo': jnp.zeros((E, D), jnp.float32)}
    _L0_ffn_all = _L0_ffn_setup()
    _L0_ffn_in = {k: v for k, v in _L0_ffn_all.items() if k in ('router_w', 'router_b', 'wq', 'bq', 'wk', 'bk', 'wv', 'bv', 'wo', 'bo')}
    del _L0_ffn_all

    def _L1_xattn_setup():
        import jax, jax.numpy as jnp
        import numpy as np
        EMBED = 128
        HEADS = 16
        HEAD_DIM = EMBED // HEADS
        key = jax.random.key(seed)
        k1, k2, k3, k4, k5, k6 = jax.random.split(key, 6)
        N, S = (4, 256)
        return {'values': jax.random.normal(k1, (N, S, EMBED), dtype=jnp.float32), 'keys': jax.random.normal(k2, (N, S, EMBED), dtype=jnp.float32), 'query': jax.random.normal(k3, (N, S, EMBED), dtype=jnp.float32), 'mask': jax.random.randint(k4, (N, 1, S, S), 0, 2, dtype=jnp.int32), 'W_out': jax.random.normal(k5, (EMBED, EMBED), dtype=jnp.float32) * (1.0 / np.sqrt(EMBED)), 'b_out': jax.random.normal(k6, (EMBED,), dtype=jnp.float32) * 0.01}
    _L1_xattn_all = _L1_xattn_setup()
    _L1_xattn_in = {k: v for k, v in _L1_xattn_all.items() if k in ('W_out', 'b_out')}
    del _L1_xattn_all

    def _L1_attn_setup():
        import jax, jax.numpy as jnp
        import numpy as np
        D_MODEL = 128
        N_HEADS = 16
        HEAD_DIM = D_MODEL // N_HEADS
        MAX_LEN = 256
        BATCH = 2
        SEQ = 256
        key = jax.random.key(seed)
        ks = jax.random.split(key, 10)
        s = 1.0 / np.sqrt(D_MODEL)
        inp = {'x': jax.random.normal(ks[0], (BATCH, SEQ, D_MODEL), dtype=jnp.float32), 'Wq': jax.random.uniform(ks[1], (D_MODEL, D_MODEL), jnp.float32, -s, s), 'bq': jax.random.uniform(ks[2], (D_MODEL,), jnp.float32, -s, s), 'Wk': jax.random.uniform(ks[3], (D_MODEL, D_MODEL), jnp.float32, -s, s), 'bk': jax.random.uniform(ks[4], (D_MODEL,), jnp.float32, -s, s), 'Wv': jax.random.uniform(ks[5], (D_MODEL, D_MODEL), jnp.float32, -s, s), 'bv': jax.random.uniform(ks[6], (D_MODEL,), jnp.float32, -s, s), 'Wo': jax.random.uniform(ks[7], (D_MODEL, D_MODEL), jnp.float32, -s, s), 'bo': jax.random.uniform(ks[8], (D_MODEL,), jnp.float32, -s, s), 'rel_emb': jax.random.normal(ks[9], (MAX_LEN * 2 - 1, HEAD_DIM), dtype=jnp.float32)}
        return inp
    _L1_attn_all = _L1_attn_setup()
    _L1_attn_in = {k: v for k, v in _L1_attn_all.items() if k in ('Wq', 'bq', 'Wk', 'bk', 'Wv', 'bv', 'Wo', 'bo', 'rel_emb')}
    del _L1_attn_all

    def _L1_ffn_setup():
        import jax, jax.numpy as jnp
        import numpy as np
        S_LEN, BATCH, HIDDEN = (256, 2, 128)
        N_HEADS, N_KV = (16, 8)
        N_EXP, TOP_K, CAP_F = (8, 2, 1.25)
        FFN = 512
        HEAD_DIM = HIDDEN // N_HEADS
        Q_PER_KV = N_HEADS // N_KV
        EPS = 1e-05
        NEG = -1000000000.0

        def _ln(x, w, b):
            mu = jnp.mean(x, -1, keepdims=True)
            var = jnp.var(x, -1, keepdims=True)
            return (x - mu) * jax.lax.rsqrt(var + EPS) * w + b

        def _forward(hidden_states, ln1_weight, ln1_bias, ln2_weight, ln2_bias, qkv_weight, proj_weight, router_weight, moe_w1, moe_w2):
            S, B, H = hidden_states.shape
            ln1 = _ln(hidden_states, ln1_weight, ln1_bias)
            qkv = (ln1 @ qkv_weight.T).reshape(S, B, N_KV, (Q_PER_KV + 2) * HEAD_DIM)
            q_dim = Q_PER_KV * HEAD_DIM
            q = qkv[..., :q_dim].reshape(S, B, N_HEADS, HEAD_DIM)
            k = jnp.repeat(qkv[..., q_dim:q_dim + HEAD_DIM], Q_PER_KV, axis=2)
            v = jnp.repeat(qkv[..., q_dim + HEAD_DIM:], Q_PER_KV, axis=2)
            scores = jnp.einsum('sbhd,tbhd->bhst', q, k) / jnp.sqrt(jnp.float32(HEAD_DIM))
            causal = jnp.tril(jnp.ones((S, S), bool))
            attn = jax.nn.softmax(jnp.where(causal[None, None], scores, NEG), axis=-1)
            attn_out = jnp.einsum('bhst,tbhd->sbhd', attn, v).reshape(S, B, H)
            hidden_after_attn = hidden_states + attn_out @ proj_weight.T
            x = _ln(hidden_after_attn, ln2_weight, ln2_bias).reshape(-1, H)
            N = S * B
            probs = jax.nn.softmax(x.astype(jnp.float32) @ router_weight, axis=-1)
            top_p, top_i = jax.lax.top_k(probs, TOP_K)
            top_p = top_p / jnp.sum(top_p, -1, keepdims=True)
            flat_exp = top_i.reshape(-1)
            order = jnp.argsort(flat_exp)
            sorted_exp = flat_exp[order]
            counts = jnp.bincount(sorted_exp, length=N_EXP)
            offsets = jnp.concatenate([jnp.zeros((1,), counts.dtype), jnp.cumsum(counts)])
            within = jnp.arange(N * TOP_K) - offsets[sorted_exp]
            cap = int(np.ceil(N * TOP_K / N_EXP * CAP_F))
            keep = within < cap
            slot = jnp.where(keep, sorted_exp * cap + within, N_EXP * cap)
            tok_id = order // TOP_K
            padded_tokens = jnp.zeros((N_EXP * cap + 1, H), x.dtype).at[slot].set(x[tok_id])[:-1]
            padded_probs = jnp.zeros((N_EXP * cap + 1,), jnp.float32).at[slot].set(top_p.reshape(-1)[order])[:-1]
            padded_ids = jnp.zeros((N_EXP * cap + 1,), jnp.int32).at[slot].set(tok_id.astype(jnp.int32))[:-1]
            exp_in = padded_tokens.reshape(N_EXP, cap, H)
            act = jax.nn.gelu(jnp.einsum('ech,ehf->ecf', exp_in, moe_w1), approximate=False)
            exp_out = jnp.einsum('ecf,efh->ech', act, moe_w2).reshape(N_EXP * cap, H)
            weighted = exp_out * padded_probs[:, None].astype(exp_out.dtype)
            moe = jnp.zeros((N, H), exp_out.dtype).at[padded_ids].add(weighted)
            return hidden_after_attn + moe.reshape(S, B, H)
        ks = jax.random.split(jax.random.key(seed), 6)
        qkv_out = N_KV * (Q_PER_KV + 2) * HEAD_DIM
        sc = 0.02
        return {'hidden_states': jax.random.normal(ks[0], (S_LEN, BATCH, HIDDEN), jnp.float32), 'ln1_weight': jnp.ones((HIDDEN,), jnp.float32), 'ln1_bias': jnp.zeros((HIDDEN,), jnp.float32), 'ln2_weight': jnp.ones((HIDDEN,), jnp.float32), 'ln2_bias': jnp.zeros((HIDDEN,), jnp.float32), 'qkv_weight': jax.random.normal(ks[1], (qkv_out, HIDDEN), jnp.float32) * sc, 'proj_weight': jax.random.normal(ks[2], (HIDDEN, HIDDEN), jnp.float32) * sc, 'router_weight': jax.random.normal(ks[3], (HIDDEN, N_EXP), jnp.float32) * sc, 'moe_w1': jax.random.normal(ks[4], (N_EXP, HIDDEN, FFN), jnp.float32) * sc, 'moe_w2': jax.random.normal(ks[5], (N_EXP, FFN, HIDDEN), jnp.float32) * sc}
    _L1_ffn_all = _L1_ffn_setup()
    _L1_ffn_in = {k: v for k, v in _L1_ffn_all.items() if k in ('ln1_weight', 'ln1_bias', 'ln2_weight', 'ln2_bias', 'qkv_weight', 'proj_weight', 'router_weight', 'moe_w1', 'moe_w2')}
    del _L1_ffn_all
    return {'x': x, 'ctx_1024': ctx_1024, 'mask_Bx1xSxS2_ik1': mask_Bx1xSxS2_ik1, 'L0_xattn_WQ': _L0_xattn_in['WQ'], 'L0_xattn_WK': _L0_xattn_in['WK'], 'L0_xattn_WV': _L0_xattn_in['WV'], 'L0_xattn_WO': _L0_xattn_in['WO'], 'L0_xattn_bO': _L0_xattn_in['bO'], 'L0_attn_scale1': _L0_attn_in['scale1'], 'L0_attn_scale2': _L0_attn_in['scale2'], 'L0_attn_gamma': _L0_attn_in['gamma'], 'L0_attn_qkv_w': _L0_attn_in['qkv_w'], 'L0_attn_proj_w': _L0_attn_in['proj_w'], 'L0_attn_proj_b': _L0_attn_in['proj_b'], 'L0_attn_conv1_w': _L0_attn_in['conv1_w'], 'L0_attn_conv1_b': _L0_attn_in['conv1_b'], 'L0_attn_conv2_w': _L0_attn_in['conv2_w'], 'L0_attn_conv2_b': _L0_attn_in['conv2_b'], 'L0_ffn_router_w': _L0_ffn_in['router_w'], 'L0_ffn_router_b': _L0_ffn_in['router_b'], 'L0_ffn_wq': _L0_ffn_in['wq'], 'L0_ffn_bq': _L0_ffn_in['bq'], 'L0_ffn_wk': _L0_ffn_in['wk'], 'L0_ffn_bk': _L0_ffn_in['bk'], 'L0_ffn_wv': _L0_ffn_in['wv'], 'L0_ffn_bv': _L0_ffn_in['bv'], 'L0_ffn_wo': _L0_ffn_in['wo'], 'L0_ffn_bo': _L0_ffn_in['bo'], 'L1_xattn_W_out': _L1_xattn_in['W_out'], 'L1_xattn_b_out': _L1_xattn_in['b_out'], 'L1_attn_Wq': _L1_attn_in['Wq'], 'L1_attn_bq': _L1_attn_in['bq'], 'L1_attn_Wk': _L1_attn_in['Wk'], 'L1_attn_bk': _L1_attn_in['bk'], 'L1_attn_Wv': _L1_attn_in['Wv'], 'L1_attn_bv': _L1_attn_in['bv'], 'L1_attn_Wo': _L1_attn_in['Wo'], 'L1_attn_bo': _L1_attn_in['bo'], 'L1_attn_rel_emb': _L1_attn_in['rel_emb'], 'L1_ffn_ln1_weight': _L1_ffn_in['ln1_weight'], 'L1_ffn_ln1_bias': _L1_ffn_in['ln1_bias'], 'L1_ffn_ln2_weight': _L1_ffn_in['ln2_weight'], 'L1_ffn_ln2_bias': _L1_ffn_in['ln2_bias'], 'L1_ffn_qkv_weight': _L1_ffn_in['qkv_weight'], 'L1_ffn_proj_weight': _L1_ffn_in['proj_weight'], 'L1_ffn_router_weight': _L1_ffn_in['router_weight'], 'L1_ffn_moe_w1': _L1_ffn_in['moe_w1'], 'L1_ffn_moe_w2': _L1_ffn_in['moe_w2']}

def reference(x, ctx_1024, mask_Bx1xSxS2_ik1, L0_xattn_WQ, L0_xattn_WK, L0_xattn_WV, L0_xattn_WO, L0_xattn_bO, L0_attn_scale1, L0_attn_scale2, L0_attn_gamma, L0_attn_qkv_w, L0_attn_proj_w, L0_attn_proj_b, L0_attn_conv1_w, L0_attn_conv1_b, L0_attn_conv2_w, L0_attn_conv2_b, L0_ffn_router_w, L0_ffn_router_b, L0_ffn_wq, L0_ffn_bq, L0_ffn_wk, L0_ffn_bk, L0_ffn_wv, L0_ffn_bv, L0_ffn_wo, L0_ffn_bo, L1_xattn_W_out, L1_xattn_b_out, L1_attn_Wq, L1_attn_bq, L1_attn_Wk, L1_attn_bk, L1_attn_Wv, L1_attn_bv, L1_attn_Wo, L1_attn_bo, L1_attn_rel_emb, L1_ffn_ln1_weight, L1_ffn_ln1_bias, L1_ffn_ln2_weight, L1_ffn_ln2_bias, L1_ffn_qkv_weight, L1_ffn_proj_weight, L1_ffn_router_weight, L1_ffn_moe_w1, L1_ffn_moe_w2):
    import jax
    import jax.numpy as jnp

    def _L0_xattn_ref(Q, K, V, WQ, WK, WV, WO, bO):
        import jax, jax.numpy as jnp
        import numpy as np
        import math
        D_MODEL = 128
        HEADS = 16
        DK = 64
        DV = 64
        N, ql, _ = Q.shape
        kl = K.shape[1]
        q = (Q @ WQ).reshape(N, ql, HEADS, DK)
        k = (K @ WK).reshape(N, kl, HEADS, DK)
        v = (V @ WV).reshape(N, kl, HEADS, DV)
        compat = jnp.einsum('nqhk,nlhk->nhql', q, k) / math.sqrt(DK)
        weights = jax.nn.softmax(compat, axis=3)
        attn = jnp.einsum('nhqk,nkhv->nqhv', weights, v).reshape(N, ql, HEADS * DV)
        return attn @ WO + bO

    def _L0_attn_ref(x, scale1, scale2, gamma, qkv_w, proj_w, proj_b, conv1_w, conv1_b, conv2_w, conv2_b):
        import jax, jax.numpy as jnp
        import numpy as np
        DIM = 128
        HEADS = 16
        HIDDEN = 256
        EPS = 1e-06

        def _rmsnorm(x, scale):
            norm = jnp.linalg.norm(x, axis=-1, keepdims=True)
            return x * (scale * (x.shape[-1] ** 0.5 + EPS) / norm)
        B, N, C = x.shape
        h, d = (HEADS, C // HEADS)
        xn = _rmsnorm(x, scale1)
        qkv = jnp.einsum('bnc,fc->bnf', xn, qkv_w)
        qkv = qkv.reshape(B, N, 3, h, d).transpose(2, 0, 3, 1, 4)
        q, k, v = (qkv[0], qkv[1], qkv[2])
        phi = lambda t: jnp.exp(-0.5 * t * t)
        q, k = (phi(q), phi(k))
        kv = jnp.einsum('bhnd,bhne->bhde', k, v)
        z = 1.0 / (jnp.einsum('bhnd,bhd->bhn', q, k.sum(2)) + 1e-06)
        out = jnp.einsum('bhnd,bhde,bhn->bhne', q, kv, z)
        out = out.transpose(0, 2, 1, 3).reshape(B, N, C)
        attn = jnp.einsum('bnc,oc->bno', out, proj_w) + proj_b
        x = x + gamma * attn
        xn2 = _rmsnorm(x, scale2)
        hdd = jax.nn.gelu(jnp.einsum('bnc,hc->bnh', xn2, conv1_w) + conv1_b, approximate=False)
        mlp = jnp.einsum('bnh,ch->bnc', hdd, conv2_w) + conv2_b
        return x + gamma * mlp

    def _L0_ffn_ref(x, router_w, router_b, wq, bq, wk, bk, wv, bv, wo, bo):
        import jax, jax.numpy as jnp
        import numpy as np
        B, S, D, H, E = (4, 256, 128, 16, 4)
        b, s, d = x.shape
        e_total = router_w.shape[-1]
        h = H
        hd = d // h
        sm_scale = 0.5
        logits = x @ router_w + router_b
        probs = jax.nn.softmax(logits, axis=-1)
        _, top2 = jax.lax.top_k(probs, 2)
        out = jnp.zeros_like(x)
        bidx = jnp.arange(b)[:, None]
        for e in range(e_total):
            member = (top2 == e).any(-1)
            w_tok = jnp.where(member, probs[..., e], 0.0)
            order = jnp.argsort((~member).astype(jnp.int32), axis=-1, stable=True)
            xg = jnp.take_along_axis(x, order[..., None], axis=1)
            validg = jnp.take_along_axis(member, order, axis=1)
            wg = jnp.take_along_axis(w_tok, order, axis=1)
            q = (xg @ wq[e] + bq[e]).reshape(b, s, h, hd)
            k = (xg @ wk[e] + bk[e]).reshape(b, s, h, hd)
            v = (xg @ wv[e] + bv[e]).reshape(b, s, h, hd)
            att = jnp.einsum('bqhd,bkhd->bhqk', q, k) * sm_scale
            att = jnp.where(validg[:, None, None, :], att, -1000000000.0)
            att = jax.nn.softmax(att, axis=-1)
            y = jnp.einsum('bhqk,bkhd->bqhd', att, v).reshape(b, s, d)
            y = y @ wo[e] + bo[e]
            out = out.at[bidx, order].add(wg[..., None] * y)
        return out

    def _L1_xattn_ref(values, keys, query, mask, W_out, b_out):
        import jax, jax.numpy as jnp
        import numpy as np
        EMBED = 128
        HEADS = 16
        HEAD_DIM = EMBED // HEADS
        N, Q = (query.shape[0], query.shape[1])
        K = keys.shape[1]
        v = values.reshape(N, K, HEADS, HEAD_DIM)
        k = keys.reshape(N, K, HEADS, HEAD_DIM)
        q = query.reshape(N, Q, HEADS, HEAD_DIM)
        energy = jnp.einsum('nqhd,nkhd->nhqk', q, k)
        energy = jnp.where(mask == 0, jnp.float32(-1e+20), energy)
        attn = jax.nn.softmax(energy / jnp.sqrt(jnp.float32(EMBED)), axis=3)
        out = jnp.einsum('nhqk,nkhd->nqhd', attn, v).reshape(N, Q, EMBED)
        return out @ W_out.T + b_out

    def _L1_attn_ref(x, Wq, bq, Wk, bk, Wv, bv, Wo, bo, rel_emb):
        import jax, jax.numpy as jnp
        import numpy as np
        D_MODEL = 128
        N_HEADS = 16
        HEAD_DIM = D_MODEL // N_HEADS
        MAX_LEN = 256
        BATCH = 2
        SEQ = 256
        B, L, _ = x.shape

        def lin(x, W, b):
            return jnp.einsum('bld,ed->ble', x, W) + b

        def split_heads(t):
            return t.reshape(B, L, N_HEADS, HEAD_DIM).transpose(0, 2, 1, 3)
        q = split_heads(lin(x, Wq, bq))
        k = split_heads(lin(x, Wk, bk))
        v = split_heads(lin(x, Wv, bv))
        r = jnp.arange(L)
        idx = r[None, :] - r[:, None] + (MAX_LEN - 1)
        rel = rel_emb[idx]
        qk = jnp.einsum('bhld,bhrd->bhlr', q, k) / np.sqrt(HEAD_DIM)
        qk = qk + jnp.einsum('bhld,lrd->bhlr', q, rel)
        att = jax.nn.softmax(qk, axis=-1)
        out = jnp.einsum('bhlr,bhrd->bhld', att, v)
        out = out.transpose(0, 2, 1, 3).reshape(B, L, D_MODEL)
        return lin(out, Wo, bo)

    def _L1_ffn_ref(hidden_states, ln1_weight, ln1_bias, ln2_weight, ln2_bias, qkv_weight, proj_weight, router_weight, moe_w1, moe_w2):
        import jax, jax.numpy as jnp
        import numpy as np
        S_LEN, BATCH, HIDDEN = (256, 2, 128)
        N_HEADS, N_KV = (16, 8)
        N_EXP, TOP_K, CAP_F = (8, 2, 1.25)
        FFN = 512
        HEAD_DIM = HIDDEN // N_HEADS
        Q_PER_KV = N_HEADS // N_KV
        EPS = 1e-05
        NEG = -1000000000.0

        def _ln(x, w, b):
            mu = jnp.mean(x, -1, keepdims=True)
            var = jnp.var(x, -1, keepdims=True)
            return (x - mu) * jax.lax.rsqrt(var + EPS) * w + b

        def _forward(hidden_states, ln1_weight, ln1_bias, ln2_weight, ln2_bias, qkv_weight, proj_weight, router_weight, moe_w1, moe_w2):
            S, B, H = hidden_states.shape
            ln1 = _ln(hidden_states, ln1_weight, ln1_bias)
            qkv = (ln1 @ qkv_weight.T).reshape(S, B, N_KV, (Q_PER_KV + 2) * HEAD_DIM)
            q_dim = Q_PER_KV * HEAD_DIM
            q = qkv[..., :q_dim].reshape(S, B, N_HEADS, HEAD_DIM)
            k = jnp.repeat(qkv[..., q_dim:q_dim + HEAD_DIM], Q_PER_KV, axis=2)
            v = jnp.repeat(qkv[..., q_dim + HEAD_DIM:], Q_PER_KV, axis=2)
            scores = jnp.einsum('sbhd,tbhd->bhst', q, k) / jnp.sqrt(jnp.float32(HEAD_DIM))
            causal = jnp.tril(jnp.ones((S, S), bool))
            attn = jax.nn.softmax(jnp.where(causal[None, None], scores, NEG), axis=-1)
            attn_out = jnp.einsum('bhst,tbhd->sbhd', attn, v).reshape(S, B, H)
            hidden_after_attn = hidden_states + attn_out @ proj_weight.T
            x = _ln(hidden_after_attn, ln2_weight, ln2_bias).reshape(-1, H)
            N = S * B
            probs = jax.nn.softmax(x.astype(jnp.float32) @ router_weight, axis=-1)
            top_p, top_i = jax.lax.top_k(probs, TOP_K)
            top_p = top_p / jnp.sum(top_p, -1, keepdims=True)
            flat_exp = top_i.reshape(-1)
            order = jnp.argsort(flat_exp)
            sorted_exp = flat_exp[order]
            counts = jnp.bincount(sorted_exp, length=N_EXP)
            offsets = jnp.concatenate([jnp.zeros((1,), counts.dtype), jnp.cumsum(counts)])
            within = jnp.arange(N * TOP_K) - offsets[sorted_exp]
            cap = int(np.ceil(N * TOP_K / N_EXP * CAP_F))
            keep = within < cap
            slot = jnp.where(keep, sorted_exp * cap + within, N_EXP * cap)
            tok_id = order // TOP_K
            padded_tokens = jnp.zeros((N_EXP * cap + 1, H), x.dtype).at[slot].set(x[tok_id])[:-1]
            padded_probs = jnp.zeros((N_EXP * cap + 1,), jnp.float32).at[slot].set(top_p.reshape(-1)[order])[:-1]
            padded_ids = jnp.zeros((N_EXP * cap + 1,), jnp.int32).at[slot].set(tok_id.astype(jnp.int32))[:-1]
            exp_in = padded_tokens.reshape(N_EXP, cap, H)
            act = jax.nn.gelu(jnp.einsum('ech,ehf->ecf', exp_in, moe_w1), approximate=False)
            exp_out = jnp.einsum('ecf,efh->ech', act, moe_w2).reshape(N_EXP * cap, H)
            weighted = exp_out * padded_probs[:, None].astype(exp_out.dtype)
            moe = jnp.zeros((N, H), exp_out.dtype).at[padded_ids].add(weighted)
            return hidden_after_attn + moe.reshape(S, B, H)
        return _forward(hidden_states, ln1_weight, ln1_bias, ln2_weight, ln2_bias, qkv_weight, proj_weight, router_weight, moe_w1, moe_w2)
    x = x + _L0_xattn_ref(_layernorm(x, axis=-1), ctx_1024, ctx_1024, L0_xattn_WQ, L0_xattn_WK, L0_xattn_WV, L0_xattn_WO, L0_xattn_bO)
    x = x + _L0_attn_ref(_layernorm(x, axis=-1), L0_attn_scale1, L0_attn_scale2, L0_attn_gamma, L0_attn_qkv_w, L0_attn_proj_w, L0_attn_proj_b, L0_attn_conv1_w, L0_attn_conv1_b, L0_attn_conv2_w, L0_attn_conv2_b)
    x = x + _L0_ffn_ref(_layernorm(x, axis=-1), L0_ffn_router_w, L0_ffn_router_b, L0_ffn_wq, L0_ffn_bq, L0_ffn_wk, L0_ffn_bk, L0_ffn_wv, L0_ffn_bv, L0_ffn_wo, L0_ffn_bo)
    x = x + _L1_xattn_ref(ctx_1024, ctx_1024, _layernorm(x, axis=-1), mask_Bx1xSxS2_ik1, L1_xattn_W_out, L1_xattn_b_out)
    x = x + _L1_attn_ref(_layernorm(x, axis=-1), L1_attn_Wq, L1_attn_bq, L1_attn_Wk, L1_attn_bk, L1_attn_Wv, L1_attn_bv, L1_attn_Wo, L1_attn_bo, L1_attn_rel_emb)
    x = x + _L1_ffn_ref(_layernorm(x, axis=-1), L1_ffn_ln1_weight, L1_ffn_ln1_bias, L1_ffn_ln2_weight, L1_ffn_ln2_bias, L1_ffn_qkv_weight, L1_ffn_proj_weight, L1_ffn_router_weight, L1_ffn_moe_w1, L1_ffn_moe_w2)
    return x

_drawn_inputs = setup_inputs


def setup_inputs(seed=0):
    import zlib

    import numpy as np

    out = dict(_drawn_inputs(seed))
    spreads = {'L0_xattn_bO': (0.0, 0.1),
     'L0_attn_scale1': (1.0, 0.6),
     'L0_attn_scale2': (1.0, 0.6),
     'L0_attn_gamma': (1.0, 0.6),
     'L0_attn_proj_b': (0.0, 0.1),
     'L0_attn_conv1_b': (0.0, 0.8),
     'L0_attn_conv2_b': (0.0, 0.1),
     'L0_ffn_router_b': (0.0, 0.8),
     'L0_ffn_bq': (0.0, 0.8),
     'L0_ffn_bk': (0.0, 0.8),
     'L0_ffn_bv': (0.0, 0.8),
     'L0_ffn_bo': (0.0, 0.414),
     'L1_ffn_ln1_weight': (1.0, 0.6),
     'L1_ffn_ln1_bias': (0.0, 0.8),
     'L1_ffn_ln2_weight': (1.0, 0.6),
     'L1_ffn_ln2_bias': (0.0, 0.8)}
    factors = {'L0_attn_qkv_w': 4.661,
     'L0_attn_proj_w': 4.752,
     'L0_attn_conv1_w': 2.979,
     'L0_attn_conv2_w': 2.778,
     'L0_ffn_router_w': 4.024,
     'L0_ffn_wq': 8.0,
     'L0_ffn_wk': 8.0,
     'L0_ffn_wv': 8.0,
     'L0_ffn_wo': 8.0,
     'L1_xattn_b_out': 8.0,
     'L1_attn_bq': 8.0,
     'L1_attn_Wk': 5.382,
     'L1_attn_bk': 8.0,
     'L1_attn_bv': 4.078,
     'L1_ffn_qkv_weight': 8.0,
     'L1_ffn_proj_weight': 8.0,
     'L1_ffn_router_weight': 5.471,
     'L1_ffn_moe_w1': 4.657,
     'L1_ffn_moe_w2': 4.615}
    for name, (base, spread) in spreads.items():
        noise = np.random.default_rng([zlib.crc32(name.encode()), seed]).standard_normal(out[name].shape)
        drawn = base * np.exp(spread * noise) if base else spread * noise
        out[name] = jnp.asarray(drawn.astype(out[name].dtype))
    for name, factor in factors.items():
        out[name] = (out[name] * factor).astype(out[name].dtype)
    return out
```

```python
from contextlib import ExitStack

import concourse.bass as bass
from concourse import mybir
from concourse.alu_op_type import AluOpType as ALU

ACT = mybir.ActivationFunctionType
AX = mybir.AxisListType
F32 = mybir.dt.float32
BF16 = mybir.dt.bfloat16
I32 = mybir.dt.int32
U32 = mybir.dt.uint32

B, S, D = 32, 64, 128
KEYS = 128
HEADS = 16
HD = D // HEADS
DK = 64
P = 128
TILES = B * S // P
TB = P // S
PAIRS = HEADS // 2
UCOL = 1024
LN_EPS = 1e-5
RMS_NUM = float(D) ** 0.5 + 1e-6
E0 = 4
E1, TOPK, FFN = 8, 2, 512
CAP = 640
SLOTS = E1 * CAP
S5, B5 = B, S
NEG0, NEG1 = -1e9, -1e20

PACK = [("WQT", 1024), ("WKT", 1024), ("WV", 1024), ("WO", 1024),
        ("ident", 128), ("headmask", 16), ("quadmask", 4), ("mask8", 8), ("tri", 128), ("ones", 128),
        ("half", 256), ("expert", 8), ("repq", 128), ("causal", 32), ("token", 16),
        ("qkvT", 384), ("projT", 128), ("conv1T", 256), ("conv2T", 256),
        ("scale1", 1), ("scale2", 1), ("conv1_b", 2), ("rw", 4),
        ("wq", 512), ("wk", 512), ("wv", 512), ("wo", 512), ("bq", 4), ("bk", 4),
        ("W_outT", 128), ("WqT", 128), ("WkT", 128), ("WvT", 128), ("WoT", 128), ("bq1", 1), ("bk1", 1),
        ("relT", 128), ("q5T", 128), ("k5T", 128), ("v5T", 128), ("proj5T", 128), ("rw5", 8)]
EARLY = 4 * 1024
OFF, _at = {}, 0
for _n, _w in PACK:
    OFF[_n] = (_at, _w)
    _at += _w
WCOLS = _at
ROWS = [("bO", 128), ("gamma", 128), ("proj_b", 128), ("conv2_b", 128), ("rb", 4), ("bv", 512), ("bo", 512),
        ("b_out", 128), ("bv1", 128), ("bo1", 128), ("ln1w", 128), ("ln1b", 128), ("ln2w", 128), ("ln2b", 128)]
ROFF, _at = {}, 0
for _n, _w in ROWS:
    ROFF[_n] = (_at, _w)
    _at += _w
RCOLS = _at


class At:

    def __init__(self, p, j, units):
        self.p, self.j, self.units = p, j, units
        body = 2 * units
        self.n = p * body + j
        self.t = p * 2 + j // units
        self.u = j % units
        self.par = (j // units) % 2
        self.up = j % 2
        self.round = p + (j // units) // 2

    def plus(self, k):
        return At(self.p, self.j + k, self.units)

    def inside(self, total):
        return not isinstance(self.n, int) or 0 <= self.n < total


def run_units(eng, units, tiles, step, lead=0, tail=3, peel=2):
    body = 2 * units
    turns = tiles // 2
    for p in range(peel):
        for j in range(body):
            step(At(p, j, units))
    with eng.Fori(peel, turns - 1) as p:
        for j in range(body):
            step(At(p, j, units))
    for j in range(body + tail):
        step(At(turns - 1, j, units))


def wait(eng, sem, value):
    if isinstance(value, int):
        if value <= 0:
            return
    else:
        assert value.min_val > 0, "a wait in a loop has to be on a count above zero"
    eng.wait_ge(sem, value)


class Chain:

    def __init__(self, sem):
        self.sem, self.n, self.base = sem, 0, 0

    def link(self, eng, ins):
        ins.then_inc(self.sem, 1)
        self.n += 1
        eng.wait_ge(self.sem, self.base + self.n)

    def loop(self, eng, start, end, body):
        before = self.n
        body(start)
        per, first = self.n - before, self.n
        if end - start > 1:
            with eng.Fori(start + 1, end) as i:
                self.base, self.n = (i - (start + 1)) * per + first, 0
                body(i)
            self.base, self.n = 0, first + per * (end - start - 1)


def bc(ap, shape):
    return ap.broadcast_to(shape)


def build(nc, A, out):
    es = ExitStack()
    with es:
        def sb(name, shape, dt=F32):
            return es.enter_context(nc.sbuf_tensor(name, shape, dt))

        held = []

        def sems(st, prefix, names):
            got = {x: nc.alloc_semaphore(prefix + x) for x in names.split()}
            held.extend(got.values())
            return got

        def clear_semaphores():
            nc.clear_and_free_semaphores(held)
            nc.all_engine_barrier()
            held.clear()

        W = sb("W", [P, WCOLS])
        R = sb("R", [P, RCOLS])
        X = sb("X", [P, TILES, D])
        XnT = sb("XnT", [D, TILES * P])
        ctxT = sb("ctxT", [D, B, KEYS])
        nhalf = sb("nhalf", [P, TILES])

        def w(name, lo=0, n=None):
            o, width = OFF[name]
            return W[:, o + lo:o + (lo + n if n is not None else width)]

        def row(name, lo=0, n=None):
            o, width = ROFF[name]
            return R[:, o + lo:o + (lo + n if n is not None else width)]

        ident = w("ident")

        psS = [es.enter_context(nc.psum_tensor(f"scores{i}", [P, UCOL], F32)) for i in range(2)]
        psT = es.enter_context(nc.psum_tensor("probsT", [P, UCOL], F32))
        psO = es.enter_context(nc.psum_tensor("mixed", [P, 512], F32))
        psM = es.enter_context(nc.psum_tensor("misc", [P, 512], F32))

        def dram(name, shape, dt=F32):
            return nc.dram_tensor(name, shape, dt, kind="Internal").ap()

        shared = dict(nc=nc, A=A, out=out, es=es, sb=sb, sems=sems, W=W, R=R, X=X, XnT=XnT, ctxT=ctxT, nhalf=nhalf, w=w, row=row,
                     ident=ident, psS=psS, psT=psT, psO=psO, psM=psM, dram=dram)
        K = type("K", (), shared)
        load(K)
        stages = [stage_cross_wide, stage_linear, stage_mlp, stage_expert_attention, stage_cross_masked,
                  stage_relative, stage_causal, stage_moe]
        for f in stages:
            f(K)
            if f in (stage_expert_attention, stage_relative):
                clear_semaphores()


def load(K):
    nc = K.nc
    with ExitStack() as st:
        s = K.sems(st, "load_", "done const")
        with nc.Block() as block:
            @block.sync
            def _(sp):
                sp.dma_start(K.W[:, 0:EARLY], K.A["wpack"][:, 0:EARLY]).then_inc(s["done"], 16)
                sp.dma_start(K.X[:, :, :], K.A["x"].rearrange("t p d -> p t d")).then_inc(s["done"], 16)
                sp.dma_start(K.R[:, :], K.A["rpack"].partition_broadcast(P)).then_inc(s["done"], 16)
                sp.dma_start(K.ctxT[:, :, :], K.A["ctxT"].rearrange("b d k -> d b k")).then_inc(s["done"], 16)
                sp.dma_start(K.W[:, EARLY:], K.A["wpack"][:, EARLY:]).then_inc(s["done"], 16)
                sp.wait_ge(s["done"], 80)

            @block.gpsimd
            def _(pool):
                pool.memset(K.nhalf[:, :], -0.5).then_inc(s["const"], 1)
                pool.wait_ge(s["const"], 1)


def norm_stats(dve, ch, st6, mv, src, n, var_ready):
    for i in range(n):
        last = dve.bn_stats(st6[:, i, :], src[:, i, :])
    ch.link(dve, last)
    for i in range(n):
        last = dve.bn_aggr(mv[:, i, :], st6[:, i, :])
    last.then_inc(var_ready, 1)


def layer_norm(K, tag, router=None, keep=None, src=None, affine=None):
    nc = K.nc
    G = 4
    src = K.X if src is None else src
    with ExitStack() as st:
        s = K.sems(st, tag, "chain scaled var vareps rstd normed kept turned copied logits logitsout xT")
        st6 = st.enter_context(nc.sbuf_tensor(tag + "st6", [P, G, 6], F32))
        mv = st.enter_context(nc.sbuf_tensor(tag + "mv", [P, G, 2], F32))
        rstd = st.enter_context(nc.sbuf_tensor(tag + "rstd", [P, G], F32))
        xn = st.enter_context(nc.sbuf_tensor(tag + "xn", [P, 2, G, D], F32))
        xT = st.enter_context(nc.sbuf_tensor(tag + "xT", [P, 2, G * P], F32))
        groups = TILES // G
        with nc.Block() as block:
            @block.vector
            def _(dve):
                ch = Chain(s["chain"])

                def group(g, par):
                    rows = src[:, bass.ds(g * G, G), :]
                    norm_stats(dve, ch, st6, mv, rows, G, s["var"])
                    dve.wait_ge(s["rstd"], g + 1)
                    wait(dve, s["turned"], g - 1)
                    if keep is not None:
                        wait(dve, s["kept"], g - 1)
                    for i in range(G):
                        last = dve.tensor_scalar(xn[:, par, i, :], src[:, g * G + i, :], mv[:, i, 0:1], rstd[:, i:i + 1],
                                                 ALU.subtract, ALU.mult)
                    if affine is not None:
                        last.then_inc(s["scaled"], 1)
                        for op, v in ((ALU.mult, affine[0]), (ALU.add, affine[1])):
                            dve.wait_ge(s["scaled"], 2 * g + (1 if op == ALU.mult else 2))
                            last = dve.tensor_tensor(xn[:, par, :, :], xn[:, par, :, :],
                                                     bc(K.row(v).unsqueeze(1), [P, G, D]), op)
                            if op == ALU.mult:
                                last.then_inc(s["scaled"], 1)
                    last.then_inc(s["normed"], 1)
                    if router is not None:
                        wait(dve, s["logits"], g + 1)
                        dve.tensor_copy(router[2][:, bass.ds(g * G, G), :],
                                        K.psO[:, 0:G * router[1]].rearrange("p (g e) -> p g e", g=G)).then_inc(s["logitsout"], 1)

                ch.loop(dve, 0, groups // 2, lambda p: (group(p * 2, 0), group(p * 2 + 1, 1)))

            @block.tensor
            def _(pe):
                def group(g, par):
                    pe.wait_ge(s["normed"], g + 1)
                    wait(pe, s["copied"], g - 1)
                    for i in range(G):
                        last = pe.transpose(K.psS[par][:, i * P:(i + 1) * P], xn[:, par, i, :], K.ident)
                    last.then_inc(s["turned"], 1)
                    if router is not None:
                        pe.wait_ge(s["xT"], g + 1)
                        wait(pe, s["logitsout"], g)
                        for i in range(G):
                            last = pe.matmul(K.psO[:, i * router[1]:(i + 1) * router[1]], xT[:, par, i * P:(i + 1) * P],
                                             router[0], start=True, stop=True)
                        last.then_inc(s["logits"], 1)

                group(0, 0)
                group(1, 1)
                with pe.Fori(1, groups // 2) as p:
                    group(p * 2, 0)
                    group(p * 2 + 1, 1)

            @block.scalar
            def _(act):
                def group(g, par):
                    act.wait_ge(s["turned"], g + 1)
                    if router is not None:
                        wait(act, s["logits"], g - 1)
                        act.copy(xT[:, par, :], K.psS[par][:, 0:G * P]).then_inc(s["xT"], 1)
                    act.copy(K.XnT[:, bass.ds(g * G * P, G * P)], K.psS[par][:, 0:G * P]).then_inc(s["copied"], 1)

                group(0, 0)
                group(1, 1)
                with act.Fori(1, groups // 2) as p:
                    group(p * 2, 0)
                    group(p * 2 + 1, 1)

            @block.gpsimd
            def _(pool):
                def group(g, par):
                    pool.wait_ge(s["var"], g + 1)
                    pool.tensor_scalar(rstd[:, :], mv[:, :, 1], LN_EPS, None, ALU.add).then_inc(s["vareps"], 1)
                    pool.wait_ge(s["vareps"], g + 1)
                    pool.tensor_tensor(rstd[:, :], rstd[:, :], K.nhalf[:, 0:G], ALU.pow).then_inc(s["rstd"], 1)
                    if keep is not None:
                        pool.wait_ge(s["normed"], g + 1)
                        pool.tensor_copy(keep[:, bass.ds(g * G, G), :], xn[:, par, :, :]).then_inc(s["kept"], 1)

                group(0, 0)
                group(1, 1)
                with pool.Fori(1, groups // 2) as p:
                    group(p * 2, 0)
                    group(p * 2 + 1, 1)


UNIT_SEMS = "scored tiled maxed shifted exped turned tcopied mixed recip normed "


class Attention:

    def __init__(self, K, st, s, tag, total, keys, scale, cols=UCOL, split=1):
        self.K, self.s, self.total, self.keys, self.scale, self.cols = K, s, total, keys, scale, cols
        self.groups = cols // keys
        self.split = split
        nc = K.nc
        self.P = st.enter_context(nc.sbuf_tensor(tag + "P", [P, 2, cols], F32))
        self.PT = st.enter_context(nc.sbuf_tensor(tag + "PT", [P, 2, cols], F32))
        self.mx = st.enter_context(nc.sbuf_tensor(tag + "mx", [P, 2, self.groups], F32))
        self.banks = (cols + 511) // 512

    def scores_free(self, pe, a):
        wait(pe, self.s["shifted" if self.bias is None else "biased"], a.n - 1)

    def shift(self, dve, a):
        if not a.inside(self.total):
            return
        s, g = self.s, self.groups
        if self.split == 1:
            sc = self.K.psS[a.up][:, 0:self.cols].rearrange("p (g k) -> p g k", g=g)
        else:
            sc = self.K.psS[a.up][:, :].rearrange("p (a g k) -> p a g k", a=2, k=self.keys)[:, :, 0:g // 2, :]
        pr = self.P[:, a.up, :].rearrange("p (g k) -> p g k", g=g)
        mx = self.mx[:, a.up, :]
        out, top, wide = pr, bc(mx.unsqueeze(2), [P, g, self.keys]), mx
        if self.split == 2:
            out = pr.rearrange("p (a g) k -> p a g k", a=2)
            wide = mx.rearrange("p (a g) -> p a g", a=2)
            top = bc(wide.unsqueeze(3), [P, 2, g // 2, self.keys])
        dve.wait_ge(s["scored"], a.n + 1)
        if self.bias is not None:
            wait(dve, s["turned"], (a.n - 1) * self.banks)
            self.bias(dve, a, out, sc).then_inc(s["biased"], 1)
            dve.wait_ge(s["biased"], a.n + 1)
            sc = out
        wait(dve, s["shifted"], a.n - 1)
        dve.tensor_reduce(wide, sc, AX.X, ALU.max).then_inc(s["maxed"], 1)
        wait(dve, s["turned"], (a.n - 1) * self.banks)
        if self.summed is not None:
            wait(dve, self.summed, a.n - 1)
        dve.wait_ge(s["maxed"], a.n + 1)
        dve.tensor_tensor(out, sc, top, ALU.subtract).then_inc(s["shifted"], 1)

    def exp(self, act, a):
        if not a.inside(self.total):
            return
        act.wait_ge(self.s["shifted"], a.n + 1)
        act.activation(self.P[:, a.up, :], self.P[:, a.up, :], ACT.Exp, scale=self.scale).then_inc(self.s["exped"], 1)

    def turn(self, pe, a):
        if not a.inside(self.total):
            return
        pe.wait_ge(self.s["exped"], a.n + 1)
        for b in range(self.banks):
            wait(pe, self.s["tcopied"], (a.n - 1) * self.banks + b + 1)
            for c in range(4):
                i = 4 * b + c
                last = pe.transpose(self.K.psT[:, i * P:(i + 1) * P], self.P[:, a.up, i * P:(i + 1) * P], self.K.ident)
            last.then_inc(self.s["turned"], 1)

    def tcopy(self, act, a):
        if not a.inside(self.total):
            return
        for b in range(self.banks):
            act.wait_ge(self.s["turned"], a.n * self.banks + b + 1)
            wait(act, self.s["mixed"], (a.n - 1) * self.mixes)
            act.copy(self.PT[:, a.up, b * 512:(b + 1) * 512], self.K.psT[:, b * 512:(b + 1) * 512]).then_inc(
                self.s["tcopied"], 1)

    bias = None
    summed = None
    mixes = 1


def row_tile_wait(pe, s, a, g):
    if g:
        pe.wait_ge(s["tiled"], 3 * a.n + g)


def quad_order():
    return [(g % 2, (g // 2) * 2 + cc, g, cc) for g in range(4) for cc in range(2)]


def pair_slot(c):
    g, cc = c // 2, c % 2
    return (g % 2) * 4 + (g // 2) * 2 + cc


def stage_cross_wide(K):
    layer_norm(K, "n1_")
    nc, w = K.nc, K.w
    with ExitStack() as st:
        s = K.sems(st, "c1_", UNIT_SEMS + "chain cin cinT pre preout gt gtout v vout summed oT oTout y yout xin")
        sb = lambda n, sh, dt=F32: st.enter_context(nc.sbuf_tensor("c1_" + n, sh, dt))
        AQ = sb("AQ", [P, HEADS, D])
        xs = sb("xs", [P, 2, P])
        GT = sb("GT", [P, 2, TB, HEADS, S])
        ctxT = sb("ctxT", [P, 4, KEYS])
        Vb = sb("Vb", [P, 2, HEADS, DK])
        o = sb("o", [P, 2, HEADS, DK])
        oT = sb("oT", [P, 8, P])
        rl = sb("rl", [P, 2, PAIRS])
        yb = sb("yb", [P, 2, D])
        U, TOTAL = TB, TILES * TB
        at = Attention(K, st, s, "c1_", TOTAL, KEYS, 1.0 / DK ** 0.5)
        at.summed = s["summed"]
        M = K.psM

        with nc.Block() as block:
            @block.gpsimd
            def _(pool):
                def step(a):
                    if not a.inside(TOTAL):
                        return
                    if a.u == 0:
                        wait(pool, s["gt"], 4 * (a.t - 1))
                        pool.tensor_copy(xs[:, a.par, :], K.XnT[:, bass.ds(a.t * P, P)]).then_inc(s["xin"], 1)
                    wait(pool, s["scored"], a.n - 3)
                    wait(pool, s["v"], 2 * (a.n - 3))
                    pool.tensor_copy(ctxT[:, a.j % 4, :], K.ctxT[:, a.n, :]).then_inc(s["cin"], 1)

                run_units(pool, U, TILES, step, 0, 0)

            @block.tensor
            def _(pe):
                for r in range(2):
                    wait(pe, s["preout"], 2 * r)
                    for hh in range(2):
                        for c in range(4):
                            pr = 4 * r + c
                            q = w("WQT", pr * P, P)[hh * 64:hh * 64 + 64, :]
                            k = w("WKT", pr * P, P)[hh * 64:hh * 64 + 64, :]
                            last = pe.matmul(K.psS[hh][:, c * P:(c + 1) * P], q, k, start=True, stop=True)
                        last.then_inc(s["pre"], 1)
                pe.wait_ge(s["preout"], 4)

                def misc_free(a_t, used):
                    pass

                def gt(a, r):
                    if not a.inside(TOTAL):
                        return
                    pe.wait_ge(s["xin"], a.t + 1)
                    for h in range(4 * r, 4 * r + 4):
                        last = pe.matmul(M[:, (h % 4) * P:(h % 4 + 1) * P], AQ[:, h, :], xs[:, a.par, :],
                                         start=True, stop=True)
                    last.then_inc(s["gt"], 1)
                    pe.wait_ge(s["gtout"], 4 * a.t + r + 1)

                def values(a, r):
                    if not a.inside(TOTAL):
                        return
                    pe.wait_ge(s["cin"], a.n + 1)
                    pe.matmul(M[:, :], ctxT[:, a.j % 4, :], w("WV", r * 512, 512), start=True, stop=True).then_inc(s["v"], 1)
                    pe.wait_ge(s["vout"], 2 * a.n + r + 1)

                def score(a):
                    if not a.inside(TOTAL):
                        return
                    at.scores_free(pe, a)
                    pe.wait_ge(s["gtout"], 4 * (a.t + 1))
                    pe.wait_ge(s["cin"], a.n + 1)
                    for c in range(PAIRS):
                        last = pe.matmul(K.psS[a.up][:, c * KEYS:(c + 1) * KEYS],
                                         GT[:, a.par, a.u, 2 * c:2 * c + 2, :].rearrange("p h q -> p (h q)"),
                                         ctxT[:, a.j % 4, :], start=True, stop=True)
                    last.then_inc(s["scored"], 1)

                def mix(a, half):
                    if not a.inside(TOTAL):
                        return
                    pe.wait_ge(s["tcopied"], 2 * a.n + half + 1)
                    pe.wait_ge(s["vout"], 2 * (a.n + 1))
                    wait(pe, s["normed"], a.n)
                    for c in range(4 * half, 4 * half + 4):
                        for hh in range(2):
                            last = pe.matmul(K.psO[64 * hh:64 * hh + 64, c * DK:(c + 1) * DK],
                                             at.PT[:, a.up, c * P + 64 * hh:c * P + 64 * hh + 64],
                                             Vb[:, a.up, 2 * c + hh, :], start=True, stop=True)
                    if half:
                        last.then_inc(s["mixed"], 1)

                def finish(a, part):
                    if not a.inside(TOTAL):
                        return
                    if part < 2:
                        pe.wait_ge(s["normed"], 2 * (a.t + 1))
                        for c in range(4):
                            i = 4 * part + c
                            last = pe.transpose(M[:, c * P:(c + 1) * P],
                                                o[:, a.par, 2 * i:2 * i + 2, :].rearrange("p h d -> p (h d)"), K.ident)
                        last.then_inc(s["oT"], 1)
                        pe.wait_ge(s["oTout"], 2 * a.t + part + 1)
                    else:
                        for i in range(8):
                            last = pe.matmul(M[:, 0:D], oT[:, i, :], w("WO", i * D, D), start=(i == 0), stop=(i == 7))
                        last.then_inc(s["y"], 1)

                def step(a):
                    if a.u == 0:
                        wait(pe, s["yout"], a.t - 1)
                    n1, p1 = a.plus(1), a.plus(-1)
                    nt = a.plus(2)
                    gt(nt, 2 * a.u)
                    if a.u == 0:
                        score(n1)
                    gt(nt, 2 * a.u + 1)
                    if a.u == 1:
                        score(n1)
                    at.turn(pe, a)
                    values(a, 0)
                    mix(p1, 0)
                    values(a, 1)
                    mix(p1, 1)
                    if a.u == 1:
                        for part in range(3):
                            finish(a.plus(-2), part)

                first = At(0, 0, U)
                for r in range(4):
                    gt(first, r)
                score(first)
                run_units(pe, U, TILES, step, 0, 2)

            @block.scalar
            def _(act):
                for r in range(2):
                    for hh in range(2):
                        act.wait_ge(s["pre"], 2 * r + hh + 1)
                        act.copy(AQ[:, bass.ds(8 * r + hh, 4, 2), :],
                                 K.psS[hh][:, 0:512].rearrange("p (c d) -> p c d", c=4)).then_inc(s["preout"], 1)

                def gt(a, r):
                    if not a.inside(TOTAL):
                        return
                    act.wait_ge(s["gt"], 4 * a.t + r + 1)
                    wait(act, s["scored"], 2 * (a.t - 1))
                    for b in range(TB):
                        last = act.copy(GT[:, a.par, b, 4 * r:4 * r + 4, :],
                                        M[:, :].rearrange("p (h b q) -> p h b q", h=4, b=TB)[:, :, b, :])
                    last.then_inc(s["gtout"], 1)

                def values(a, r):
                    if not a.inside(TOTAL):
                        return
                    act.wait_ge(s["v"], 2 * a.n + r + 1)
                    wait(act, s["mixed"], a.n - 1)
                    act.copy(Vb[:, a.up, 8 * r:8 * r + 8, 0:DK],
                             M[:, :].rearrange("p (h d) -> p h d", h=8)).then_inc(s["vout"], 1)

                def finish(a):
                    if not a.inside(TOTAL):
                        return
                    for part in range(2):
                        act.wait_ge(s["oT"], 2 * a.t + part + 1)
                        wait(act, s["y"], a.t)
                        act.copy(oT[:, 4 * part:4 * part + 4, :],
                                 M[:, :].rearrange("p (c q) -> p c q", c=4)).then_inc(s["oTout"], 1)

                def step(a):
                    p1, nt = a.plus(-1), a.plus(2)
                    gt(nt, 2 * a.u)
                    at.exp(act, a)
                    gt(nt, 2 * a.u + 1)
                    at.tcopy(act, p1)
                    values(a, 0)
                    values(a, 1)
                    if a.u == 1:
                        finish(a.plus(-2))

                first = At(0, 0, U)
                for r in range(4):
                    gt(first, r)
                run_units(act, U, TILES, step, 0, 2)

            @block.vector
            def _(dve):
                ch = Chain(s["chain"])

                def sums(a):
                    if not a.inside(TOTAL):
                        return
                    dve.wait_ge(s["exped"], a.n + 1)
                    wait(dve, s["normed"], a.n - 1)
                    dve.tensor_reduce(rl[:, a.up, :], at.P[:, a.up, :].rearrange("p (g k) -> p g k", g=PAIRS),
                                      AX.X, ALU.add).then_inc(s["summed"], 1)
                    dve.wait_ge(s["summed"], a.n + 1)
                    dve.reciprocal(rl[:, a.up, :], rl[:, a.up, :]).then_inc(s["recip"], 1)

                def normalise(a):
                    if not a.inside(TOTAL):
                        return
                    dve.wait_ge(s["mixed"], a.n + 1)
                    dve.wait_ge(s["recip"], a.n + 1)
                    wait(dve, s["oT"], 2 * (a.t - 1))
                    ps = K.psO[:, :].rearrange("p (c e) -> p c e", c=PAIRS)
                    for hh in range(2):
                        rows = slice(64 * hh, 64 * hh + 64)
                        last = dve.tensor_tensor(o[64 * a.u:64 * a.u + 64, a.par, hh::2, :], ps[rows, :, :],
                                                 bc(rl[rows, a.up, :].unsqueeze(2), [64, PAIRS, DK]), ALU.mult)
                    last.then_inc(s["normed"], 1)

                def finish(a):
                    if not a.inside(TOTAL):
                        return
                    dve.wait_ge(s["y"], a.t + 1)
                    dve.tensor_tensor(yb[:, a.par, :], M[:, 0:D], K.row("bO"), ALU.add).then_inc(s["yout"], 1)
                    dve.wait_ge(s["yout"], a.t + 1)
                    dve.tensor_tensor(K.X[:, a.t, :], K.X[:, a.t, :], yb[:, a.par, :], ALU.add)

                def step(a):
                    at.shift(dve, a)
                    sums(a.plus(-1))
                    normalise(a.plus(-2))
                    if a.u == 0:
                        finish(a.plus(-3))

                run_units(dve, U, TILES, step, 0, 3)


def bank_views(K):
    return [K.psS[0][:, 0:512], K.psS[0][:, 512:1024], K.psS[1][:, 0:512], K.psS[1][:, 512:1024],
            K.psT[:, 0:512], K.psT[:, 512:1024], K.psO[:, :], K.psM[:, :]]


def stage_linear(K):
    nc, w, row = K.nc, K.w, K.row
    G, GROUPS = 2, TILES // 2
    N = G * P
    K.Xmid = K.es.enter_context(nc.sbuf_tensor("Xmid", [P, TILES, D], F32))
    with ExitStack() as st:
        s = K.sems(st, "l2_", "weights chain var scaled rs xn turned xnT q kv squared phi v kvm KV num rden rdenok o oT oTc y "
                              "ya yg xm")
        sb = lambda n, sh, dt=F32: st.enter_context(nc.sbuf_tensor("l2_" + n, sh, dt))
        Wqkv = sb("Wqkv", [D, 3 * D])
        st6, mv = sb("st6", [P, G, 6]), sb("mv", [P, G, 2])
        rs = sb("rs", [P, 2, G])
        xn = sb("xn", [P, 2, G, D])
        xnT, sqq, sqk = sb("xnT", [D, 2, N]), sb("sqq", [D, N]), sb("sqk", [P, G, D])
        phq, phk = sb("phq", [D, 2, N]), sb("phk", [P, 2, G, D])
        vb = sb("vb", [P, 2, G, TB * D + TB])
        KV = sb("KV", [P, 2, G, TB, D + HEADS])
        den, o, oT = sb("den", [P, G, HEADS]), sb("o", [P, 2, G, D]), sb("oT", [D, 2, N])
        ya = sb("ya", [P, 2, G, D])
        pT, pQ, pKV, pS0, pS1, pN, pO, pY = bank_views(K)
        inside = lambda a: a.inside(GROUPS)

        with nc.Block() as block:
            @block.vector
            def _(dve):
                ch = Chain(s["chain"])
                dve.tensor_scalar(Wqkv[:, :], w("qkvT"), w("scale1"), None, ALU.mult).then_inc(s["weights"], 1)
                ch.link(dve, dve.memset(vb[:, :, :, :], 0.0))
                for b in range(TB):
                    dve.memset(vb[64 * b:64 * b + 64, :, :, TB * D + b:TB * D + b + 1], 1.0).then_inc(s["weights"], 1)

                def xnorm(a):
                    if not inside(a):
                        return
                    src = K.X[:, bass.ds(a.n * G, G), :]
                    wait(dve, s["rs"], a.n)
                    for i in range(G):
                        dve.bn_stats(st6[:, i, :], K.X[:, a.n * G + i, :]).then_inc(s["chain"], 1)
                    dve.wait_ge(s["chain"], 1 + G * (a.n + 1))
                    wait(dve, s["xn"], a.n)
                    for i in range(G):
                        last = dve.bn_aggr(mv[:, i, :], st6[:, i, :])
                    last.then_inc(s["var"], 1)
                    dve.wait_ge(s["rs"], a.n + 1)
                    dve.wait_ge(s["var"], a.n + 1)
                    wait(dve, s["turned"], a.n - 1)
                    for i in range(G):
                        dve.tensor_scalar(K.Xmid[:, a.n * G + i, :], K.X[:, a.n * G + i, :], mv[:, i, 0:1], rs[:, 0, i:i + 1],
                                          ALU.subtract, ALU.mult)
                        last = dve.tensor_scalar(xn[:, a.par, i, :], K.X[:, a.n * G + i, :], mv[:, i, 0:1],
                                                 rs[:, 1, i:i + 1], ALU.subtract, ALU.mult)
                    last.then_inc(s["xn"], 1)

                def mask(a):
                    if not inside(a):
                        return
                    dve.wait_ge(s["KV"], a.n + 1)
                    wait(dve, s["num"], a.n - 1)
                    for i, ps in enumerate((pS0, pS1)):
                        dve.tensor_tensor(KV[:, a.par, i, :, 0:D].rearrange("p b (h e) -> p b h e", h=HEADS),
                                          ps[:, 0:TB * D].rearrange("p (b h e) -> p b h e", b=TB, h=HEADS),
                                          bc(w("headmask").unsqueeze(1).unsqueeze(3), [P, TB, HEADS, HD]), ALU.mult)
                        for b in range(TB):
                            last = dve.tensor_scalar(KV[:, a.par, i, b, D:], w("headmask"),
                                                     ps[:, TB * D + b:TB * D + b + 1], None, ALU.mult)
                    last.then_inc(s["kvm"], 1)

                def values(a):
                    if not inside(a):
                        return
                    dve.wait_ge(s["kv"], a.n + 1)
                    wait(dve, s["KV"], a.n - 1)
                    for b in range(TB):
                        last = dve.tensor_copy(vb[64 * b:64 * b + 64, a.par, :, b * D:(b + 1) * D],
                                               pKV[64 * b:64 * b + 64, :].rearrange("p (i c) -> p i c", i=G)[:, :, D:])
                    last.then_inc(s["v"], 1)

                def divide(a):
                    if not inside(a):
                        return
                    dve.wait_ge(s["num"], a.n + 1)
                    wait(dve, s["o"], a.n)
                    ps = pN[:, 0:G * (D + HEADS)].rearrange("p (i c) -> p i c", i=G)
                    dve.tensor_scalar(den[:, :, :], ps[:, :, D:], 1e-6, None, ALU.add).then_inc(s["rden"], 1)
                    dve.wait_ge(s["rden"], a.n + 1)
                    dve.reciprocal(den[:, :, :], den[:, :, :]).then_inc(s["rdenok"], 1)
                    dve.wait_ge(s["rdenok"], a.n + 1)
                    wait(dve, s["oT"], a.n - 1)
                    for i in range(G):
                        last = dve.tensor_tensor(o[:, a.par, i, :].rearrange("p (h e) -> p h e", h=HEADS),
                                                 ps[:, i, 0:D].rearrange("p (h e) -> p h e", h=HEADS),
                                                 bc(den[:, i, :].unsqueeze(2), [P, HEADS, HD]), ALU.mult)
                    last.then_inc(s["o"], 1)

                def bias(a):
                    if not inside(a):
                        return
                    dve.wait_ge(s["y"], a.n + 1)
                    wait(dve, s["xm"], a.n - 1)
                    dve.tensor_tensor(ya[:, a.par, :, :], pY[:, 0:N].rearrange("p (i d) -> p i d", i=G),
                                      bc(row("proj_b").unsqueeze(1), [P, G, D]), ALU.add).then_inc(s["ya"], 1)

                def step(a):
                    xnorm(a)
                    mask(a.plus(-1))
                    values(a)
                    divide(a.plus(-1))
                    bias(a.plus(-2))

                run_units(dve, 1, GROUPS, step, 0, 2)

            @block.gpsimd
            def _(pool):
                def scales(a):
                    if not inside(a):
                        return
                    pool.wait_ge(s["var"], a.n + 1)
                    wait(pool, s["xn"], a.n)
                    pool.tensor_scalar(rs[:, 0, :], mv[:, :, 1], LN_EPS, None, ALU.add)
                    pool.tensor_scalar(rs[:, 1, :], mv[:, :, 1], D / RMS_NUM ** 2, None, ALU.mult).then_inc(s["scaled"], 1)
                    pool.wait_ge(s["scaled"], a.n + 1)
                    pool.tensor_tensor(rs[:, :, :], rs[:, :, :], K.nhalf[:, 0:2 * G].rearrange("p (a b) -> p a b", a=2),
                                       ALU.pow).then_inc(s["rs"], 1)

                def mid(a):
                    if not inside(a):
                        return
                    pool.wait_ge(s["ya"], a.n + 1)
                    y = ya[:, a.par, :, :]
                    pool.tensor_tensor(y, y, bc(row("gamma").unsqueeze(1), [P, G, D]), ALU.mult).then_inc(s["yg"], 1)
                    pool.wait_ge(s["yg"], a.n + 1)
                    xl = K.Xmid[:, bass.ds(a.n * G, G), :]
                    pool.tensor_tensor(xl, xl, y, ALU.add).then_inc(s["xm"], 1)

                def step(a):
                    scales(a)
                    mid(a.plus(-2))

                run_units(pool, 1, GROUPS, step, 0, 2)

            @block.scalar
            def _(act):
                def xT(a):
                    if not inside(a):
                        return
                    act.wait_ge(s["turned"], a.n + 1)
                    wait(act, s["kv"], a.n - 1)
                    act.copy(xnT[:, a.par, :], pT[:, 0:N]).then_inc(s["xnT"], 1)

                def outT(a):
                    if not inside(a):
                        return
                    act.wait_ge(s["oT"], a.n + 1)
                    wait(act, s["y"], a.n - 1)
                    act.copy(oT[:, a.par, :], pO[:, 0:N]).then_inc(s["oTc"], 1)

                def phi(a):
                    if not inside(a):
                        return
                    act.wait_ge(s["q"], a.n + 1)
                    wait(act, s["phi"], a.n)
                    act.activation(sqq[:, :], pQ[:, 0:N], ACT.Square)
                    act.wait_ge(s["v"], a.n + 1)
                    act.activation(sqk[:, :, :], pKV[:, :].rearrange("p (i c) -> p i c", i=G)[:, :, 0:D],
                                   ACT.Square).then_inc(s["squared"], 1)
                    act.wait_ge(s["squared"], a.n + 1)
                    wait(act, s["num"], a.n - 1)
                    act.activation(phq[:, a.par, :], sqq[:, :], ACT.Exp, scale=-0.5)
                    act.activation(phk[:, a.par, :, :], sqk[:, :, :], ACT.Exp, scale=-0.5).then_inc(s["phi"], 1)

                def step(a):
                    xT(a)
                    outT(a.plus(-2))
                    phi(a)

                run_units(act, 1, GROUPS, step, 0, 2)

            @block.tensor
            def _(pe):
                def turn(a):
                    if not inside(a):
                        return
                    pe.wait_ge(s["xn"], a.n + 1)
                    wait(pe, s["xnT"], a.n)
                    for i in range(G):
                        last = pe.transpose(pT[:, i * P:(i + 1) * P], xn[:, a.par, i, :], K.ident)
                    last.then_inc(s["turned"], 1)

                def sums(a):
                    if not inside(a):
                        return
                    pe.wait_ge(s["phi"], a.n + 1)
                    pe.wait_ge(s["v"], a.n + 1)
                    wait(pe, s["kvm"], a.n)
                    for i, ps in enumerate((pS0, pS1)):
                        last = pe.matmul(ps[:, 0:TB * D + TB], phk[:, a.par, i, :], vb[:, a.par, i, :], start=True, stop=True)
                    last.then_inc(s["KV"], 1)

                def oturn(a):
                    if not inside(a):
                        return
                    pe.wait_ge(s["o"], a.n + 1)
                    wait(pe, s["oTc"], a.n)
                    for i in range(G):
                        last = pe.transpose(pO[:, i * P:(i + 1) * P], o[:, a.par, i, :], K.ident)
                    last.then_inc(s["oT"], 1)

                def qkv(a):
                    if not inside(a):
                        return
                    pe.wait_ge(s["xnT"], a.n + 1)
                    wait(pe, s["phi"], a.n)
                    wait(pe, s["v"], a.n)
                    pe.matmul(pQ[:, 0:N], Wqkv[:, 0:D], xnT[:, a.par, :], start=True, stop=True).then_inc(s["q"], 1)
                    for i in range(G):
                        last = pe.matmul(pKV[:, i * 2 * D:(i + 1) * 2 * D], xnT[:, a.par, i * P:(i + 1) * P],
                                         Wqkv[:, D:], start=True, stop=True)
                    last.then_inc(s["kv"], 1)

                def numer(a):
                    if not inside(a):
                        return
                    pe.wait_ge(s["kvm"], a.n + 1)
                    wait(pe, s["o"], a.n)
                    c = D + HEADS
                    for i in range(G):
                        for b in range(TB):
                            last = pe.matmul(pN[64 * b:64 * b + 64, i * c:(i + 1) * c],
                                             phq[:, a.par, i * P + 64 * b:i * P + 64 * b + 64],
                                             KV[:, a.par, i, b, :], start=True, stop=True)
                    last.then_inc(s["num"], 1)

                def proj(a):
                    if not inside(a):
                        return
                    pe.wait_ge(s["oTc"], a.n + 1)
                    wait(pe, s["ya"], a.n)
                    for i in range(G):
                        last = pe.matmul(pY[:, i * D:(i + 1) * D], oT[:, a.par, i * P:(i + 1) * P], w("projT"),
                                         start=True, stop=True)
                    last.then_inc(s["y"], 1)

                def step(a):
                    turn(a)
                    sums(a.plus(-1))
                    oturn(a.plus(-2))
                    qkv(a)
                    numer(a.plus(-1))
                    proj(a.plus(-2))

                pe.wait_ge(s["weights"], 3)
                run_units(pe, 1, GROUPS, step, 0, 2)


def stage_mlp(K):
    nc, w, row = K.nc, K.w, K.row
    G, GROUPS = 2, TILES // 2
    N = G * P
    with ExitStack() as st:
        s = K.sems(st, "m2_", "weights ss scaled rs xn turned xnT h gelu y ya yg ym")
        sb = lambda n, sh, dt=F32: st.enter_context(nc.sbuf_tensor("m2_" + n, sh, dt))
        W1 = sb("W1", [D, 2 * D])
        sq, ss, rs = sb("sq", [P, G, D]), sb("ss", [P, G]), sb("rs", [P, G])
        xn, xnT, hT = sb("xn", [P, 2, G, D]), sb("xnT", [D, 2, N]), sb("hT", [P, 2, 2, N])
        ya = sb("ya", [P, 2, G, D])
        banks = bank_views(K)
        pT, pH, pY = banks[0:2], banks[2:4], banks[4:6]
        inside = lambda a: a.inside(GROUPS)

        with nc.Block() as block:
            @block.vector
            def _(dve):
                dve.tensor_scalar(W1[:, :], w("conv1T"), w("scale2"), None, ALU.mult).then_inc(s["weights"], 1)

                def xnorm(a):
                    if not inside(a):
                        return
                    wait(dve, s["scaled"], a.n)
                    wait(dve, s["ss"], G * a.n)
                    for i in range(G):
                        x = K.Xmid[:, a.n * G + i, :]
                        dve.tensor_tensor_reduce(sq[:, i, :], x, x, 1.0, 0.0, ALU.mult, ALU.add,
                                                 ss[:, i:i + 1]).then_inc(s["ss"], 1)
                    dve.wait_ge(s["rs"], a.n + 1)
                    wait(dve, s["turned"], a.n - 1)
                    for i in range(G):
                        last = dve.tensor_scalar(xn[:, a.par, i, :], K.Xmid[:, a.n * G + i, :], rs[:, i:i + 1], None, ALU.mult)
                    last.then_inc(s["xn"], 1)

                def bias(a):
                    if not inside(a):
                        return
                    dve.wait_ge(s["y"], a.n + 1)
                    wait(dve, s["ym"], a.n - 1)
                    dve.tensor_tensor(ya[:, a.par, :, :], pY[a.par][:, 0:N].rearrange("p (i d) -> p i d", i=G),
                                      bc(row("conv2_b").unsqueeze(1), [P, G, D]), ALU.add).then_inc(s["ya"], 1)

                def step(a):
                    xnorm(a)
                    bias(a.plus(-1))

                run_units(dve, 1, GROUPS, step, 0, 1)

            @block.gpsimd
            def _(pool):
                def scales(a):
                    if not inside(a):
                        return
                    pool.wait_ge(s["ss"], G * (a.n + 1))
                    wait(pool, s["xn"], a.n)
                    pool.tensor_scalar(rs[:, :], ss[:, :], 1.0 / RMS_NUM ** 2, None, ALU.mult).then_inc(s["scaled"], 1)
                    pool.wait_ge(s["scaled"], a.n + 1)
                    pool.tensor_tensor(rs[:, :], rs[:, :], K.nhalf[:, 0:G], ALU.pow).then_inc(s["rs"], 1)

                def residual(a):
                    if not inside(a):
                        return
                    pool.wait_ge(s["ya"], a.n + 1)
                    y = ya[:, a.par, :, :]
                    at = bass.ds(a.n * G, G)
                    pool.tensor_tensor(y, y, bc(row("gamma").unsqueeze(1), [P, G, D]), ALU.mult).then_inc(s["yg"], 1)
                    pool.tensor_tensor(K.X[:, at, :], K.X[:, at, :], K.Xmid[:, at, :], ALU.add).then_inc(s["yg"], 1)
                    pool.wait_ge(s["yg"], 2 * a.n + 2)
                    pool.tensor_tensor(K.X[:, at, :], K.X[:, at, :], y, ALU.add).then_inc(s["ym"], 1)

                def step(a):
                    scales(a)
                    residual(a.plus(-1))

                run_units(pool, 1, GROUPS, step, 0, 1)

            @block.scalar
            def _(act):
                def xT(a):
                    if not inside(a):
                        return
                    act.wait_ge(s["turned"], a.n + 1)
                    wait(act, s["h"], 2 * (a.n - 1))
                    act.copy(xnT[:, a.par, :], pT[a.par][:, 0:N]).then_inc(s["xnT"], 1)

                def gelu(a):
                    if not inside(a):
                        return
                    wait(act, s["y"], a.n - 1)
                    for c in range(2):
                        act.wait_ge(s["h"], 2 * a.n + c + 1)
                        act.activation(hT[:, a.par, c, :], pH[c][:, 0:N], ACT.Gelu, bias=w("conv1_b", c, 1)).then_inc(s["gelu"], 1)

                def step(a):
                    xT(a)
                    gelu(a)

                run_units(act, 1, GROUPS, step, 0, 0)

            @block.tensor
            def _(pe):
                def turn(a):
                    if not inside(a):
                        return
                    pe.wait_ge(s["xn"], a.n + 1)
                    wait(pe, s["xnT"], a.n - 1)
                    for i in range(G):
                        last = pe.transpose(pT[a.par][:, i * P:(i + 1) * P], xn[:, a.par, i, :], K.ident)
                    last.then_inc(s["turned"], 1)

                def up(a):
                    if not inside(a):
                        return
                    pe.wait_ge(s["xnT"], a.n + 1)
                    for c in range(2):
                        wait(pe, s["gelu"], 2 * (a.n - 1) + c + 1)
                        pe.matmul(pH[c][:, 0:N], W1[:, c * P:(c + 1) * P], xnT[:, a.par, :], start=True,
                                  stop=True).then_inc(s["h"], 1)

                def down(a):
                    if not inside(a):
                        return
                    pe.wait_ge(s["gelu"], 2 * (a.n + 1))
                    wait(pe, s["ya"], a.n - 1)
                    for i in range(G):
                        for c in range(2):
                            last = pe.matmul(pY[a.par][:, i * D:(i + 1) * D], hT[:, a.par, c, i * P:(i + 1) * P],
                                             w("conv2T", c * P, P), start=(c == 0), stop=(c == 1))
                    last.then_inc(s["y"], 1)

                def step(a):
                    turn(a)
                    down(a.plus(-1))
                    up(a)

                pe.wait_ge(s["weights"], 1)
                run_units(pe, 1, GROUPS, step, 0, 1)


def rank_columns(dve, ch, rank, less, l, E):
    ch.link(dve, dve.memset(less[:, :, :, :], 0.0))
    shape = [P, TILES, E]
    for e in range(E):
        le = l[:, :, e:e + 1]
        if e + 1 < E:
            last = dve.tensor_tensor(less[:, :, e + 1:, e], l[:, :, e + 1:], bc(le, [P, TILES, E - e - 1]), ALU.is_le)
        if e:
            last = dve.tensor_tensor(less[:, :, 0:e, e], l[:, :, 0:e], bc(le, [P, TILES, e]), ALU.is_lt)
    ch.link(dve, last)
    ch.link(dve, dve.tensor_reduce(rank, less[:, :, :, :], AX.X, ALU.add))


def stage_expert_attention(K):
    nc, w, row = K.nc, K.w, K.row
    with ExitStack() as keep:
        rt = lambda n, sh, dt=F32: keep.enter_context(nc.sbuf_tensor("e3_" + n, sh, dt))
        logits = rt("logits", [P, TILES, E0])
        layer_norm(K, "n3_", router=(w("rw"), E0, logits))
        wtok = rt("wtok", [P, TILES, E0])
        neg = rt("neg", [P, TILES * E0, S], BF16)

        with ExitStack() as st:
            s = K.sems(st, "r3_", "chain shifted exped negated turned copied stored row")
            sb = lambda n, sh, dt=F32: st.enter_context(nc.sbuf_tensor("r3_" + n, sh, dt))
            mx, ex, rank = sb("mx", [P, TILES]), sb("ex", [P, TILES, E0]), sb("rank", [P, TILES, E0])
            less, negm = sb("less", [P, TILES, E0, E0]), sb("negm", [P, TILES * E0])
            negT = sb("negT", [TILES * E0, P], BF16)
            scratch = K.dram("hbm_negT", (TB, TILES * E0, S), BF16)
            with nc.Block() as block:
                @block.vector
                def _(dve):
                    ch = Chain(s["chain"])
                    ch.link(dve, dve.tensor_tensor(logits[:, :, :], logits[:, :, :],
                                                   bc(row("rb").unsqueeze(1), [P, TILES, E0]), ALU.add))
                    ch.link(dve, dve.tensor_reduce(mx[:, :], logits[:, :, :], AX.X, ALU.max))
                    dve.tensor_tensor(ex[:, :, :], logits[:, :, :], bc(mx[:, :].unsqueeze(2), [P, TILES, E0]),
                                      ALU.subtract).then_inc(s["shifted"], 1)
                    rank_columns(dve, ch, rank[:, :, :], less, logits, E0)
                    ch.link(dve, dve.tensor_scalar(rank[:, :, :], rank[:, :, :], float(TOPK), None, ALU.is_lt))
                    dve.tensor_scalar(negm[:, :], rank[:, :, :].rearrange("p t e -> p (t e)"), 1.0, -NEG0, ALU.subtract,
                                      ALU.mult).then_inc(s["negated"], 1)
                    dve.wait_ge(s["exped"], 1)
                    ch.link(dve, dve.tensor_reduce(mx[:, :], ex[:, :, :], AX.X, ALU.add))
                    ch.link(dve, dve.reciprocal(mx[:, :], mx[:, :]))
                    ch.link(dve, dve.tensor_tensor(ex[:, :, :], ex[:, :, :], rank[:, :, :], ALU.mult))
                    ch.link(dve, dve.tensor_tensor(wtok[:, :, :], ex[:, :, :], bc(mx[:, :].unsqueeze(2), [P, TILES, E0]),
                                                   ALU.mult))

                @block.tensor
                def _(pe):
                    pe.wait_ge(s["negated"], 1)
                    pe.transpose(K.psM[0:TILES * E0, 0:P], negm[:, :], K.ident).then_inc(s["turned"], 1)

                @block.scalar
                def _(act):
                    act.wait_ge(s["shifted"], 1)
                    act.activation(ex[:, :, :], ex[:, :, :], ACT.Exp).then_inc(s["exped"], 1)
                    act.wait_ge(s["turned"], 1)
                    act.copy(negT[:, :], K.psM[0:TILES * E0, 0:P]).then_inc(s["copied"], 1)

                @block.sync
                def _(sp):
                    sp.wait_ge(s["copied"], 1)
                    sp.dma_start(scratch.rearrange("b r k -> r b k"), negT[:, :].rearrange("r (b k) -> r b k", b=TB)).then_inc(
                        s["stored"], 16)
                    sp.wait_ge(s["stored"], 16)
                    for b in range(TB):
                        sp.dma_start(neg[64 * b:64 * b + 64, :, :], scratch[b, :, :].partition_broadcast(64)).then_inc(
                            s["row"], 16)
                    sp.wait_ge(s["row"], 16 * TB)

        with ExitStack() as st:
            s = K.sems(st, "e3_", UNIT_SEMS + "biased init xin q qout k kout v vout kbd weighted oT oTc ysum xsum")
            sb = lambda n, sh, dt=F32: st.enter_context(nc.sbuf_tensor("e3_" + n, sh, dt))
            U, TOTAL = E0, TILES * E0
            xs = sb("xs", [D, 2, P])
            LQ = sb("LQ", [P, 2, E0, 2, P])
            Ks = sb("Ks", [P, 2, E0, 2, S])
            RK = sb("RK", [P, 2, 2, 8, S])
            Vbd = sb("Vbd", [P, 2, E0, PAIRS, TB, 2, HD + 1])
            rl, o = sb("rl", [P, 2, PAIRS, 2]), sb("o", [P, 2, E0, D])
            oT, ya = sb("oT", [D, E0, P]), sb("ya", [P, D])
            at = Attention(K, st, s, "e3_", TOTAL, S, 0.5)
            at.bias = lambda dve, a, out, sc: dve.tensor_tensor(out, sc, bc(neg[:, a.t * E0 + a.u, :].unsqueeze(1),
                                                                           [P, HEADS, S]), ALU.add)
            M = K.psM

            with nc.Block() as block:
                @block.gpsimd
                def _(pool):
                    pool.memset(Vbd[:, :, :, :, :, :, :], 0.0).then_inc(s["init"], 1)
                    pool.memset(LQ[:, :, :, :, :], 0.0).then_inc(s["init"], 1)
                    pool.wait_ge(s["init"], 2)
                    for hh in range(2):
                        pool.memset(Vbd[64 * hh:64 * hh + 64, :, :, :, :, hh, HD].rearrange("p x e c b -> p (x e c b)"),
                                    1.0).then_inc(s["init"], 1)
                    pool.wait_ge(s["init"], 4)

                    def tile_in(a):
                        if not a.inside(TOTAL):
                            return
                        wait(pool, s["v"], a.t - 1)
                        pool.tensor_copy(xs[:, a.par, :], K.XnT[:, bass.ds(a.t * P, P)]).then_inc(s["xin"], 1)

                    def keys(a):
                        if not a.inside(TOTAL):
                            return
                        pool.wait_ge(s["kout"], a.t + 1)
                        wait(pool, s["scored"], a.n - 1)
                        pool.tensor_tensor(RK[:, a.up, :, :, :], bc(Ks[:, a.par, a.u, :, :].unsqueeze(2), [P, 2, 8, S]),
                                           bc(w("mask8").unsqueeze(1).unsqueeze(3), [P, 2, 8, S]), ALU.mult).then_inc(
                                               s["kbd"], 1)

                    def weigh(a):
                        if not a.inside(TOTAL):
                            return
                        pool.wait_ge(s["normed"], U * (a.t + 1))
                        ob = o[:, a.par, :, :]
                        pool.tensor_tensor(ob, ob, bc(wtok[:, a.t, :].unsqueeze(2), [P, E0, D]), ALU.mult).then_inc(
                            s["weighted"], 1)

                    def step(a):
                        if a.u == 0:
                            tile_in(a.plus(2 * U))
                        keys(a.plus(1))
                        if a.u == 1:
                            weigh(a.plus(-U))

                    first = At(0, 0, U)
                    tile_in(first)
                    tile_in(first.plus(U))
                    keys(first)
                    run_units(pool, U, TILES, step, 0, U)

                @block.tensor
                def _(pe):
                    def queries(a):
                        if not a.inside(TOTAL):
                            return
                        pe.wait_ge(s["xin"], a.t + 1)
                        wait(pe, s["oTc"], a.t - 2)
                        for e in range(E0):
                            last = pe.matmul(M[:, e * P:(e + 1) * P], w("wq", e * D, D), xs[:, a.par, :], start=True, stop=True)
                        last.then_inc(s["q"], 1)

                    def keys(a):
                        if not a.inside(TOTAL):
                            return
                        pe.wait_ge(s["qout"], a.t + 1)
                        for e in range(E0):
                            last = pe.matmul(M[:, e * P:(e + 1) * P], w("wk", e * D, D), xs[:, a.par, :], start=True, stop=True)
                        last.then_inc(s["k"], 1)

                    def values(a):
                        if not a.inside(TOTAL):
                            return
                        pe.wait_ge(s["kout"], a.t + 1)
                        pe.matmul(M[:, :], xs[:, a.par, :], w("wv"), start=True, stop=True).then_inc(s["v"], 1)

                    def score(a):
                        if not a.inside(TOTAL):
                            return
                        at.scores_free(pe, a)
                        pe.wait_ge(s["qout"], a.t + 1)
                        pe.wait_ge(s["kbd"], a.n + 1)
                        for half in range(2):
                            last = pe.matmul(K.psS[a.up][:, half * 512:(half + 1) * 512], LQ[:, a.par, a.u, half, :],
                                             RK[:, a.up, half, :, :].rearrange("p h k -> p (h k)"), start=True, stop=True)
                        last.then_inc(s["scored"], 1)

                    def mix(a):
                        if a.inside(TOTAL):
                            pe.wait_ge(s["tcopied"], 2 * (a.n + 1))
                            pe.wait_ge(s["vout"], a.t + 1)
                            wait(pe, s["normed"], a.n)
                            for c in range(PAIRS):
                                last = pe.matmul(K.psO[:, c * 36:(c + 1) * 36], at.PT[:, a.up, c * P:(c + 1) * P],
                                                 Vbd[:, a.par, a.u, c, :, :, :], start=True, stop=True)
                        done = a.plus(-U)
                        if a.u == U - 1 and done.inside(TOTAL):
                            pe.wait_ge(s["oTc"], done.t + 1)
                            if not a.inside(TOTAL):
                                pe.wait_ge(s["normed"], TOTAL)
                            for e in range(E0):
                                last = pe.matmul(K.psO[:, 384:384 + D], oT[:, e, :], w("wo", e * D, D), start=(e == 0),
                                                 stop=(e == E0 - 1))
                            last.then_inc(s["mixed"], 1)
                        elif a.inside(TOTAL):
                            last.then_inc(s["mixed"], 1)

                    def oturn(a):
                        if not a.inside(TOTAL):
                            return
                        pe.wait_ge(s["weighted"], a.t + 1)
                        if not isinstance(a.t, int) or a.t + 2 < TILES:
                            pe.wait_ge(s["vout"], a.t + 3)
                        for e in range(E0):
                            last = pe.transpose(M[:, e * P:(e + 1) * P], o[:, a.par, e, :], K.ident)
                        last.then_inc(s["oT"], 1)

                    def step(a):
                        score(a.plus(1))
                        at.turn(pe, a)
                        mix(a.plus(-1))
                        if a.u == 0:
                            queries(a.plus(U))
                        if a.u == 1:
                            keys(a.plus(U - 1))
                        if a.u == 2:
                            values(a.plus(U - 2))
                        if a.u == 3:
                            oturn(a.plus(-U - 3))

                    pe.wait_ge(s["init"], 4)
                    first = At(0, 0, U)
                    queries(first)
                    keys(first)
                    values(first)
                    score(first)
                    run_units(pe, U, TILES, step, 0, U + 1)

                @block.scalar
                def _(act):
                    def outT(a):
                        if not a.inside(TOTAL):
                            return
                        act.wait_ge(s["oT"], a.t + 1)
                        wait(act, s["mixed"], U * (a.t + 1))
                        act.copy(oT[:, :, :], M[:, :].rearrange("p (e q) -> p e q", e=E0)).then_inc(s["oTc"], 1)

                    def step(a):
                        at.exp(act, a)
                        at.tcopy(act, a.plus(-1))
                        if a.u == 3:
                            outT(a.plus(-U - 3))

                    run_units(act, U, TILES, step, 0, U)

                @block.vector
                def _(dve):
                    def queries(a):
                        if not a.inside(TOTAL):
                            return
                        dve.wait_ge(s["q"], a.t + 1)
                        wait(dve, s["scored"], U * (a.t - 1))
                        for half in range(2):
                            rows = slice(64 * half, 64 * half + 64)
                            for b in range(TB):
                                last = dve.tensor_tensor(LQ[64 * b:64 * b + 64, a.par, :, half, b * S:(b + 1) * S],
                                                         M[rows, :].rearrange("p (e b q) -> p e b q", e=E0, b=TB)[:, :, b, :],
                                                         bc(w("bq")[rows, :].unsqueeze(2), [64, E0, S]), ALU.add)
                        last.then_inc(s["qout"], 1)

                    def keys(a):
                        if not a.inside(TOTAL):
                            return
                        dve.wait_ge(s["k"], a.t + 1)
                        wait(dve, s["kbd"], U * (a.t - 1))
                        for half in range(2):
                            rows = slice(64 * half, 64 * half + 64)
                            for b in range(TB):
                                last = dve.tensor_tensor(Ks[64 * b:64 * b + 64, a.par, :, half, :],
                                                         M[rows, :].rearrange("p (e b q) -> p e b q", e=E0, b=TB)[:, :, b, :],
                                                         bc(w("bk")[rows, :].unsqueeze(2), [64, E0, S]), ALU.add)
                        last.then_inc(s["kout"], 1)

                    def values(a):
                        if not a.inside(TOTAL):
                            return
                        dve.wait_ge(s["v"], a.t + 1)
                        wait(dve, s["mixed"], U * (a.t - 1))
                        for b in range(TB):
                            rows = slice(64 * b, 64 * b + 64)
                            for hh in range(2):
                                split = lambda x: x.rearrange("p (e c h d) -> p e c h d", e=E0, c=PAIRS, h=2)[:, :, :, hh, :]
                                last = dve.tensor_tensor(Vbd[64 * hh:64 * hh + 64, a.par, :, :, b, hh, 0:HD],
                                                         split(M[rows, :]), split(row("bv")[rows, :]), ALU.add)
                        last.then_inc(s["vout"], 1)

                    def finish(a):
                        wait(dve, s["xsum"], 4 * a.t)
                        dve.scalar_tensor_tensor(ya[:, :], row("bo", 0, D), wtok[:, a.t, 0:1], K.psO[:, 384:384 + D], ALU.mult,
                                                 ALU.add).then_inc(s["ysum"], 1)
                        dve.wait_ge(s["ysum"], a.t + 1)
                        for e in range(1, E0):
                            dve.scalar_tensor_tensor(ya[:, :], row("bo", e * D, D), wtok[:, a.t, e:e + 1], ya[:, :],
                                                     ALU.mult, ALU.add).then_inc(s["xsum"], 1)
                            dve.wait_ge(s["xsum"], a.t * 4 + e)
                        dve.tensor_tensor(K.X[:, a.t, :], K.X[:, a.t, :], ya[:, :], ALU.add).then_inc(s["xsum"], 1)

                    def normalise(a):
                        done = a.plus(-U)
                        if a.inside(TOTAL):
                            dve.wait_ge(s["mixed"], a.n + 1)
                        elif a.u == U - 1 and done.inside(TOTAL):
                            dve.wait_ge(s["mixed"], TOTAL + 1)
                        if a.u == U - 1 and done.inside(TOTAL):
                            finish(done)
                        if not a.inside(TOTAL):
                            return
                        wait(dve, s["normed"], a.n - 1)
                        ps = K.psO[:, 0:288].rearrange("p (c b h e) -> p c b h e", c=PAIRS, b=TB, h=2)
                        for b in range(TB):
                            rows = slice(64 * b, 64 * b + 64)
                            last = dve.reciprocal(rl[rows, a.up, :, :], ps[rows, :, b, :, HD])
                        last.then_inc(s["recip"], 1)
                        dve.wait_ge(s["recip"], a.n + 1)
                        wait(dve, s["oT"], a.t - 1)
                        for b in range(TB):
                            rows = slice(64 * b, 64 * b + 64)
                            last = dve.tensor_tensor(o[rows, a.par, a.u, :].rearrange("p (c h d) -> p c h d", c=PAIRS, h=2),
                                                     ps[rows, :, b, :, 0:HD],
                                                     bc(rl[rows, a.up, :, :].unsqueeze(3), [64, PAIRS, 2, HD]), ALU.mult)
                        last.then_inc(s["normed"], 1)

                    def step(a):
                        at.shift(dve, a)
                        if a.u == 1:
                            queries(a.plus(U - 1))
                        if a.u == 2:
                            keys(a.plus(U - 2))
                        if a.u == 3:
                            values(a.plus(U - 3))
                        normalise(a.plus(-2))

                    dve.wait_ge(s["init"], 4)
                    first = At(0, 0, U)
                    queries(first)
                    keys(first)
                    values(first)
                    run_units(dve, U, TILES, step, 0, U + 2)


def stage_cross_masked(K):
    layer_norm(K, "n4_")
    nc, w, row = K.nc, K.w, K.row
    with ExitStack() as st:
        s = K.sems(st, "x4_", UNIT_SEMS + "loaded masked half ones qbd kin vin oT oTc y ysum")
        sb = lambda n, sh, dt=F32: st.enter_context(nc.sbuf_tensor("x4_" + n, sh, dt))
        U, TOTAL = TB, TILES * TB
        maski, neg = sb("maski", [P, TILES, KEYS], I32), sb("neg", [P, TILES, KEYS], BF16)
        half = sb("half", [P, TB, P], BF16)
        ctx = sb("ctx", [KEYS, B, D])
        Qbd, kT = sb("Qbd", [D, 2, TB, 4, S]), sb("kT", [D, 2, KEYS])
        V1 = sb("V1", [KEYS, 2, HEADS, HD + 1])
        rl, o = sb("rl", [P, 2, PAIRS]), sb("o", [P, 2, D])
        oT, ya = sb("oT", [D, P]), sb("ya", [P, 2, D])
        at = Attention(K, st, s, "x4_", TOTAL, KEYS, 1.0 / float(D) ** 0.5)
        M = K.psM

        with nc.Block() as block:
            @block.sync
            def _(sp):
                sp.dma_start(maski[:, :, :], K.A["mask"].rearrange("t p k -> p t k")).then_inc(s["loaded"], 16)
                sp.dma_start(ctx[:, :, :], K.A["ctx"].rearrange("b k d -> k b d")).then_inc(s["loaded"], 16)

            @block.gpsimd
            def _(pool):
                pool.memset(V1[:, :, :, HD:HD + 1], 1.0).then_inc(s["ones"], 1)
                pool.wait_ge(s["loaded"], 32)

                def queries(a):
                    if not a.inside(TOTAL):
                        return
                    wait(pool, s["scored"], U * (a.t - 1))
                    pool.tensor_tensor(Qbd[:, a.par, :, :, :],
                                       bc(K.XnT[:, bass.ds(a.t * P, P)].rearrange("p (b q) -> p b q", b=TB).unsqueeze(2),
                                          [D, TB, 4, S]),
                                       bc(w("quadmask").unsqueeze(1).unsqueeze(3), [D, TB, 4, S]), ALU.mult).then_inc(s["qbd"], 1)

                def context(a):
                    if not a.inside(TOTAL):
                        return
                    wait(pool, s["scored"], a.n - 1)
                    pool.tensor_copy(kT[:, a.up, :], K.ctxT[:, a.n, :]).then_inc(s["kin"], 1)
                    wait(pool, s["mixed"], a.n - 1)
                    pool.tensor_copy(V1[:, a.up, :, 0:HD], ctx[:, a.n, :].rearrange("p (h d) -> p h d", h=HEADS)).then_inc(
                        s["vin"], 1)

                def step(a):
                    if a.u == 0:
                        queries(a)
                    context(a)

                run_units(pool, U, TILES, step, 0, 0)

            @block.tensor
            def _(pe):
                def score(a):
                    if not a.inside(TOTAL):
                        return
                    at.scores_free(pe, a)
                    pe.wait_ge(s["masked"], 1)
                    pe.wait_ge(s["half"], 1)
                    pe.wait_ge(s["qbd"], a.t + 1)
                    pe.wait_ge(s["kin"], a.n + 1)
                    ps = K.psS[a.up]
                    for bank in range(2):
                        last = pe.matmul(ps[:, bank * 512:(bank + 1) * 512].rearrange("p (c k) -> p c k", c=4),
                                         half[:, a.u, :], bc(neg[:, a.t, :].unsqueeze(1), [P, 4, KEYS]),
                                         start=True, stop=False, skip_group_check=True)
                    last.then_inc(s["tiled"], 1)
                    for bank, slot, g, cc in quad_order():
                        if cc == 0:
                            row_tile_wait(pe, s, a, g)
                        col, rows = bank * 512 + slot * KEYS, slice(32 * g, 32 * g + 32)
                        last = pe.matmul(ps[:, col:col + KEYS],
                                         Qbd[rows, a.par, a.u, 2 * cc:2 * cc + 2, :].rearrange("p h q -> p (h q)"),
                                         kT[rows, a.up, :], start=False, stop=True, skip_group_check=True)
                        if cc == 1 and g < 2:
                            last.then_inc(s["tiled"], 1)
                    last.then_inc(s["scored"], 1)

                def mix(a):
                    if not a.inside(TOTAL):
                        return
                    pe.wait_ge(s["tcopied"], 2 * (a.n + 1))
                    pe.wait_ge(s["vin"], a.n + 1)
                    pe.wait_ge(s["ones"], 1)
                    wait(pe, s["normed"], a.n)
                    for c in range(PAIRS):
                        i = pair_slot(c)
                        last = pe.matmul(K.psO[:, c * 18:(c + 1) * 18], at.PT[:, a.up, i * P:(i + 1) * P],
                                         V1[:, a.up, 2 * c:2 * c + 2, :].rearrange("p h e -> p (h e)"), start=True, stop=True)
                    last.then_inc(s["mixed"], 1)

                def finish(a):
                    if not a.inside(TOTAL):
                        return
                    pe.wait_ge(s["normed"], U * (a.t + 1))
                    wait(pe, s["ysum"], 2 * a.t)
                    pe.transpose(M[:, 0:P], o[:, a.par, :], K.ident).then_inc(s["oT"], 1)
                    pe.wait_ge(s["oTc"], a.t + 1)
                    pe.matmul(M[:, 0:D], oT[:, :], w("W_outT"), start=True, stop=True).then_inc(s["y"], 1)

                def step(a):
                    score(a.plus(1))
                    at.turn(pe, a)
                    mix(a.plus(-1))
                    if a.u == 1:
                        finish(a.plus(-U))

                score(At(0, 0, U))
                run_units(pe, U, TILES, step, 0, 2)

            @block.scalar
            def _(act):
                act.copy(half[:, :, :], w("half").rearrange("p (b m) -> p b m", b=TB)).then_inc(s["half"], 1)

                def outT(a):
                    if not a.inside(TOTAL):
                        return
                    act.wait_ge(s["oT"], a.t + 1)
                    wait(act, s["y"], a.t)
                    act.copy(oT[:, :], M[:, 0:P]).then_inc(s["oTc"], 1)

                def step(a):
                    at.exp(act, a)
                    at.tcopy(act, a.plus(-1))
                    if a.u == 1:
                        outT(a.plus(-U))

                run_units(act, U, TILES, step, 0, 2)

            @block.vector
            def _(dve):
                dve.wait_ge(s["loaded"], 32)
                dve.tensor_scalar(neg[:, :, :], maski[:, :, :], 0.0, NEG1, ALU.is_equal, ALU.mult).then_inc(s["masked"], 1)

                def normalise(a):
                    if not a.inside(TOTAL):
                        return
                    dve.wait_ge(s["mixed"], a.n + 1)
                    wait(dve, s["normed"], a.n - 1)
                    ps = K.psO[:, 0:144].rearrange("p (c h e) -> p c h e", c=PAIRS, h=2)
                    for hh in range(2):
                        rows = slice(64 * hh, 64 * hh + 64)
                        last = dve.reciprocal(rl[rows, a.up, :], ps[rows, :, hh, HD])
                    last.then_inc(s["recip"], 1)
                    dve.wait_ge(s["recip"], a.n + 1)
                    wait(dve, s["oT"], a.t - 1)
                    for hh in range(2):
                        rows = slice(64 * hh, 64 * hh + 64)
                        last = dve.tensor_tensor(
                            o[64 * a.u:64 * a.u + 64, a.par, :].rearrange("p (c h d) -> p c h d", c=PAIRS, h=2)[:, :, hh, :],
                            ps[rows, :, hh, 0:HD], bc(rl[rows, a.up, :].unsqueeze(2), [64, PAIRS, HD]), ALU.mult)
                    last.then_inc(s["normed"], 1)

                def finish(a):
                    if not a.inside(TOTAL):
                        return
                    dve.wait_ge(s["y"], a.t + 1)
                    wait(dve, s["ysum"], 2 * (a.t - 1))
                    dve.tensor_tensor(ya[:, a.par, :], M[:, 0:D], row("b_out"), ALU.add).then_inc(s["ysum"], 1)
                    dve.wait_ge(s["ysum"], 2 * a.t + 1)
                    dve.tensor_tensor(K.X[:, a.t, :], K.X[:, a.t, :], ya[:, a.par, :], ALU.add).then_inc(s["ysum"], 1)

                def step(a):
                    at.shift(dve, a)
                    normalise(a.plus(-2))
                    if a.u == 0:
                        finish(a.plus(-U - 1))

                run_units(dve, U, TILES, step, 0, 3)


def project(K, tag, QT, KT, V, wq, wk, wv, bq=None, bk=None, bv=None):
    nc, w = K.nc, K.w
    G, GROUPS = 4, TILES // 4
    N = G * P
    with ExitStack() as st:
        s = K.sems(st, tag, "xin q k v qout kout vout")
        xs = st.enter_context(nc.sbuf_tensor(tag + "xs", [D, 2, N], F32))
        banks = bank_views(K)

        def groups(eng, group):
            group(0, 0)
            group(1, 1)
            with eng.Fori(1, GROUPS // 2) as p:
                group(p * 2, 0)
                group(p * 2 + 1, 1)

        with nc.Block() as block:
            @block.gpsimd
            def _(pool):
                def group(g, par):
                    wait(pool, s["v"], g - 1)
                    pool.tensor_copy(xs[:, par, :], K.XnT[:, bass.ds(g * N, N)]).then_inc(s["xin"], 1)

                groups(pool, group)

            @block.tensor
            def _(pe):
                def group(g, par):
                    pe.wait_ge(s["xin"], g + 1)
                    wait(pe, s["qout"], g - 1)
                    pe.matmul(banks[par], w(wq), xs[:, par, :], start=True, stop=True).then_inc(s["q"], 1)
                    wait(pe, s["kout"], g - 1)
                    pe.matmul(banks[2 + par], w(wk), xs[:, par, :], start=True, stop=True).then_inc(s["k"], 1)
                    wait(pe, s["vout"], g - 1)
                    for i in range(G):
                        last = pe.matmul(banks[4 + par][:, i * D:(i + 1) * D], xs[:, par, i * P:(i + 1) * P], w(wv),
                                         start=True, stop=True)
                    last.then_inc(s["v"], 1)

                groups(pe, group)

            @block.scalar
            def _(act):
                def group(g, par):
                    for ready, out, dst, bank, bias in (("q", "qout", QT, par, bq), ("k", "kout", KT, 2 + par, bk)):
                        act.wait_ge(s[ready], g + 1)
                        view = dst[:, bass.ds(g * N, N)]
                        if bias is None:
                            act.copy(view, banks[bank]).then_inc(s[out], 1)
                        else:
                            act.activation(view, banks[bank], ACT.Identity, bias=w(bias)).then_inc(s[out], 1)

                groups(act, group)

            @block.vector
            def _(dve):
                def group(g, par):
                    dve.wait_ge(s["v"], g + 1)
                    ps = banks[4 + par].rearrange("p (i d) -> p i d", i=G)
                    dst = V[:, bass.ds(g * G, G), :]
                    if bv is None:
                        dve.tensor_copy(dst, ps).then_inc(s["vout"], 1)
                    else:
                        dve.tensor_tensor(dst, ps, bc(K.row(bv).unsqueeze(1), [P, G, D]), ALU.add).then_inc(s["vout"], 1)

                groups(dve, group)


def spread_queries(K, dst, src, nb, n):
    return K.nc.gpsimd.tensor_tensor(dst, bc(src.rearrange("p (b q) -> p b q", b=nb).unsqueeze(2), [D, nb, 4, n]),
                                     bc(K.w("quadmask").unsqueeze(1).unsqueeze(3), [D, nb, 4, n]), ALU.mult)


def stage_relative(K):
    layer_norm(K, "n5_")
    nc, w, row = K.nc, K.w, K.row
    with ExitStack() as keep:
        rt = lambda n, sh, dt=F32: keep.enter_context(nc.sbuf_tensor("a5_" + n, sh, dt))
        QT, KT, V = rt("QT", [D, TILES * P]), rt("KTall", [D, TILES * P]), rt("V", [P, TILES, D])
        project(K, "p5_", QT, KT, V, "WqT", "WkT", "WvT", "bq1", "bk1", "bv1")
        dist = K.dram("hbm_dist", (TILES, P, 2 * UCOL))

        with ExitStack() as st:
            s = K.sems(st, "z5_", "rel relbd qin z zout stored0 stored1")
            sb = lambda n, sh, dt=F32: st.enter_context(nc.sbuf_tensor("z5_" + n, sh, dt))
            rel, relbd = sb("rel", [D, P]), sb("relbd", [D, HEADS, P])
            qs, Z = sb("qs", [D, 2, P]), sb("Z", [P, 2, 2, 8, P])
            with nc.Block() as block:
                @block.gpsimd
                def _(pool):
                    pool.wait_ge(s["rel"], 1)
                    pool.tensor_tensor(relbd[:, :, :], bc(rel[:, :].unsqueeze(1), [D, HEADS, P]),
                                       bc(w("headmask").unsqueeze(2), [D, HEADS, P]), ALU.mult).then_inc(s["relbd"], 1)

                    def step(a):
                        wait(pool, s["z"], 2 * (a.t - 1))
                        pool.tensor_copy(qs[:, a.par, :], QT[:, bass.ds(a.t * P, P)]).then_inc(s["qin"], 1)

                    run_units(pool, 1, TILES, step, 0, 0)

                @block.tensor
                def _(pe):
                    pe.wait_ge(s["relbd"], 1)
                    rb = relbd[:, :, :].rearrange("p h j -> p (h j)")

                    def step(a):
                        pe.wait_ge(s["qin"], a.t + 1)
                        for half in range(2):
                            wait(pe, s["zout"], 2 * (a.t - 1) + half + 1)
                            for c in range(2):
                                last = pe.matmul(K.psS[half][:, c * 512:(c + 1) * 512], qs[:, a.par, :],
                                                 rb[:, half * UCOL + c * 512:half * UCOL + (c + 1) * 512], start=True, stop=True)
                            last.then_inc(s["z"], 1)

                    run_units(pe, 1, TILES, step, 0, 0)

                @block.scalar
                def _(act):
                    def step(a):
                        for half in range(2):
                            act.wait_ge(s["z"], 2 * a.t + half + 1)
                            wait(act, s[f"stored{a.par}"], 16 * a.round)
                            act.copy(Z[:, a.par, half, :, :],
                                     K.psS[half][:, :].rearrange("p (h j) -> p h j", h=8)).then_inc(s["zout"], 1)

                    run_units(act, 1, TILES, step, 0, 0)

                @block.vector
                def _(dve):
                    dve.tensor_scalar(rel[:, :], w("relT"), float(HD) ** 0.5, None, ALU.mult).then_inc(s["rel"], 1)

                @block.sync
                def _(sp):
                    def step(a):
                        dst = dist[a.t, :, :]
                        if not isinstance(a.t, int):
                            ready, at = sp.snap(2 * (a.t + 1)), sp.snap(a.t * (P * 2 * UCOL))
                            dst = bass.AP(dist.tensor, at, [[2 * UCOL, P], [1, 2 * UCOL]])
                            sp.wait_ge(s["zout"], ready)
                        else:
                            sp.wait_ge(s["zout"], 2 * (a.t + 1))
                        sp.dma_start(dst, Z[:, a.par, :, :, :].rearrange("p i h j -> p (i h j)")).then_inc(
                            s[f"stored{a.par}"], 16)

                    run_units(sp, 1, TILES, step, 0, 0)
                    for par in range(2):
                        sp.wait_ge(s[f"stored{par}"], 16 * TILES // 2)

        with ExitStack() as st:
            s = K.sems(st, "a5_", UNIT_SEMS + "biased zero init din0 din1 qin kout kin vin oT oTc ysum xsum")
            sb = lambda n, sh, dt=F32: st.enter_context(nc.sbuf_tensor("u5_" + n, sh, dt))
            U, TOTAL = 1, TILES
            S2 = sb("S2", [P, 2, UCOL])
            LQ = sb("LQ", [P, 2, 2, P])
            Ks, RK = sb("Ks", [P, 2, 2, S]), sb("RK", [P, 2, 2, 8, S])
            Vbd = sb("Vbd", [P, 2, PAIRS, TB, 2, HD + 1])
            rl, o = sb("rl", [P, 2, PAIRS, 2]), sb("o", [P, 2, D])
            oT, ya = sb("oT", [D, P]), sb("ya", [P, D])
            at = Attention(K, st, s, "a5_", TOTAL, S, 1.0 / float(HD) ** 0.5)
            M = K.psM

            def add_distances(dve, a, out, sc):
                dve.wait_ge(s[f"din{a.par}"], 16 * TB * (a.round + 1))
                return dve.tensor_tensor(out, sc, S2[:, a.par, :].rearrange("p (g k) -> p g k", g=HEADS), ALU.add)

            at.bias = add_distances

            with nc.Block() as block:
                @block.sync
                def _(sp):
                    def step(a):
                        base = a.t * (P * 2 * UCOL) + (S - 1)
                        if not isinstance(a.t, int):
                            rows = [sp.snap(base), sp.snap(base + S * 2 * UCOL)]
                            sp.wait_ge(s["biased"], sp.snap(a.n - 1))
                        else:
                            rows = [base, base + S * 2 * UCOL]
                            wait(sp, s["biased"], a.n - 1)
                        for b in range(TB):
                            src = bass.AP(dist.tensor, rows[b], [[2 * UCOL - 1, S], [P, HEADS], [1, S]])
                            sp.dma_start(S2[64 * b:64 * b + 64, a.par, :].rearrange("p (h k) -> p h k", h=HEADS),
                                         src).then_inc(s[f"din{a.par}"], 16)

                    run_units(sp, 1, TILES, step, 0, 0)

                @block.gpsimd
                def _(pool):
                    pool.memset(LQ[:, :, :, :], 0.0).then_inc(s["zero"], 1)
                    pool.memset(Vbd[:, :, :, :, :, :], 0.0).then_inc(s["zero"], 1)
                    pool.wait_ge(s["zero"], 2)

                    def step(a):
                        pool.wait_ge(s["kout"], a.n + 1)
                        wait(pool, s["scored"], a.n - 1)
                        last = pool.tensor_tensor(RK[:, a.par, :, :, :], bc(Ks[:, a.par, :, :].unsqueeze(2), [P, 2, 8, S]),
                                                  bc(w("mask8").unsqueeze(1).unsqueeze(3), [P, 2, 8, S]), ALU.mult)
                        last.then_inc(s["kin"], 1)

                    run_units(pool, U, TILES, step, 0, 0)

                @block.tensor
                def _(pe):
                    def score(a):
                        if not a.inside(TOTAL):
                            return
                        at.scores_free(pe, a)
                        pe.wait_ge(s["qin"], a.n + 1)
                        pe.wait_ge(s["kin"], a.n + 1)
                        for half in range(2):
                            last = pe.matmul(K.psS[a.up][:, half * 512:(half + 1) * 512], LQ[:, a.par, half, :],
                                             RK[:, a.par, half, :, :].rearrange("p h k -> p (h k)"), start=True, stop=True)
                        last.then_inc(s["scored"], 1)

                    def mix(a):
                        done = a.plus(-2)
                        if a.inside(TOTAL):
                            pe.wait_ge(s["tcopied"], 2 * (a.n + 1))
                            pe.wait_ge(s["vin"], a.n + 1)
                            wait(pe, s["normed"], a.n)
                            for c in range(PAIRS):
                                last = pe.matmul(K.psO[:, c * 36:(c + 1) * 36], at.PT[:, a.up, c * P:(c + 1) * P],
                                                 Vbd[:, a.par, c, :, :, :], start=True, stop=True)
                        if done.inside(TOTAL):
                            pe.wait_ge(s["oTc"], done.n + 1)
                            if not a.inside(TOTAL):
                                pe.wait_ge(s["normed"], TOTAL)
                                pe.wait_ge(s["ysum"], done.n)
                            last = pe.matmul(K.psO[:, 384:384 + D], oT[:, :], w("WoT"), start=True, stop=True)
                        if a.inside(TOTAL) or done.inside(TOTAL):
                            last.then_inc(s["mixed"], 1)

                    def oturn(a):
                        if not a.inside(TOTAL):
                            return
                        pe.wait_ge(s["normed"], a.n + 1)
                        wait(pe, s["oTc"], a.n)
                        pe.transpose(M[:, 0:P], o[:, a.par, :], K.ident).then_inc(s["oT"], 1)

                    def step(a):
                        score(a.plus(1))
                        at.turn(pe, a)
                        mix(a.plus(-1))
                        oturn(a.plus(-2))

                    score(At(0, 0, U))
                    run_units(pe, U, TILES, step, 0, 3)

                @block.scalar
                def _(act):
                    act.wait_ge(s["zero"], 2)
                    for hh in range(2):
                        ones = Vbd[64 * hh:64 * hh + 64, :, :, :, hh, HD].rearrange("p x c b -> p (x c b)")
                        act.activation(ones, ones, ACT.Identity, bias=1.0).then_inc(s["init"], 1)

                    def queries(a):
                        if not a.inside(TOTAL):
                            return
                        wait(act, s["scored"], a.n - 1)
                        for half in range(2):
                            for b in range(TB):
                                last = act.copy(LQ[64 * b:64 * b + 64, a.par, half, b * S:(b + 1) * S],
                                                QT[64 * half:64 * half + 64, bass.ds(a.t * P + b * S, S)])
                        last.then_inc(s["qin"], 1)
                        wait(act, s["kin"], a.n - 1)
                        for half in range(2):
                            for b in range(TB):
                                last = act.copy(Ks[64 * b:64 * b + 64, a.par, half, :],
                                                KT[64 * half:64 * half + 64, bass.ds(a.t * P + b * S, S)])
                        last.then_inc(s["kout"], 1)

                    def values(a):
                        if not a.inside(TOTAL):
                            return
                        act.wait_ge(s["init"], 2)
                        wait(act, s["mixed"], a.n - 1)
                        for b in range(TB):
                            for hh in range(2):
                                src = V[64 * b:64 * b + 64, a.t, :].rearrange("p (c h d) -> p c h d", c=PAIRS, h=2)
                                last = act.copy(Vbd[64 * hh:64 * hh + 64, a.par, :, b, hh, 0:HD], src[:, :, hh, :])
                        last.then_inc(s["vin"], 1)

                    def outT(a):
                        if not a.inside(TOTAL):
                            return
                        act.wait_ge(s["oT"], a.n + 1)
                        wait(act, s["mixed"], a.n + 2)
                        act.copy(oT[:, :], M[:, 0:P]).then_inc(s["oTc"], 1)

                    def step(a):
                        at.exp(act, a)
                        at.tcopy(act, a.plus(-1))
                        queries(a.plus(2))
                        values(a.plus(1))
                        outT(a.plus(-2))

                    first = At(0, 0, U)
                    queries(first)
                    queries(first.plus(1))
                    values(first)
                    run_units(act, U, TILES, step, 0, 2)

                @block.vector
                def _(dve):
                    def finish(a):
                        wait(dve, s["xsum"], a.n)
                        dve.tensor_tensor(ya[:, :], K.psO[:, 384:384 + D], row("bo1"), ALU.add).then_inc(s["ysum"], 1)
                        dve.wait_ge(s["ysum"], a.n + 1)
                        dve.tensor_tensor(K.X[:, a.t, :], K.X[:, a.t, :], ya[:, :], ALU.add).then_inc(s["xsum"], 1)

                    def normalise(a):
                        done = a.plus(-2)
                        if a.inside(TOTAL) or done.inside(TOTAL):
                            dve.wait_ge(s["mixed"], a.n + 1)
                        if done.inside(TOTAL):
                            finish(done)
                        if not a.inside(TOTAL):
                            return
                        wait(dve, s["normed"], a.n - 1)
                        ps = K.psO[:, 0:288].rearrange("p (c b h e) -> p c b h e", c=PAIRS, b=TB, h=2)
                        for b in range(TB):
                            rows = slice(64 * b, 64 * b + 64)
                            last = dve.reciprocal(rl[rows, a.up, :, :], ps[rows, :, b, :, HD])
                        last.then_inc(s["recip"], 1)
                        dve.wait_ge(s["recip"], a.n + 1)
                        wait(dve, s["oT"], a.n - 1)
                        for b in range(TB):
                            rows = slice(64 * b, 64 * b + 64)
                            last = dve.tensor_tensor(o[rows, a.par, :].rearrange("p (c h d) -> p c h d", c=PAIRS, h=2),
                                                     ps[rows, :, b, :, 0:HD],
                                                     bc(rl[rows, a.up, :, :].unsqueeze(3), [64, PAIRS, 2, HD]), ALU.mult)
                        last.then_inc(s["normed"], 1)

                    def step(a):
                        at.shift(dve, a)
                        normalise(a.plus(-2))

                    run_units(dve, U, TILES, step, 0, 4, peel=3)


def regroup(K, tag, pairs, back):
    nc = K.nc
    with ExitStack() as st:
        s = K.sems(st, tag, "out in")
        mem = [K.dram(f"hbm_{tag}{i}", (TILES * P, D)) for i in range(len(pairs))]
        with nc.Block() as block:
            @block.sync
            def _(sp):
                def natural(m):
                    return m.rearrange("(t p) d -> p t d", p=P)

                def grouped(m, b5):
                    return m.rearrange("(s u b) d -> b s u d", s=S5, b=4)[b5, :, :, :]

                def grouped_sb(x, b5):
                    return x[32 * b5:32 * b5 + 32, :, :]

                n = 0
                for m, (src, _) in zip(mem, pairs):
                    if back:
                        for b5 in range(4):
                            sp.dma_start(grouped(m, b5), grouped_sb(src, b5)).then_inc(s["out"], 16)
                            n += 16
                    else:
                        sp.dma_start(natural(m), src[:, :, :]).then_inc(s["out"], 16)
                        n += 16
                sp.wait_ge(s["out"], n)
                n = 0
                for m, (_, dst) in zip(mem, pairs):
                    if back:
                        sp.dma_start(dst[:, :, :], natural(m)).then_inc(s["in"], 16)
                        n += 16
                    else:
                        for b5 in range(4):
                            sp.dma_start(grouped_sb(dst, b5), grouped(m, b5)).then_inc(s["in"], 16)
                            n += 16
                sp.wait_ge(s["in"], n)


def plain_norm(K, tag, dst):
    nc = K.nc
    with ExitStack() as st:
        s = K.sems(st, tag, "stats var vareps rstd")
        sb = lambda n, sh, dt=F32: st.enter_context(nc.sbuf_tensor(tag + n, sh, dt))
        st6, mv, rstd = sb("st6", [P, TILES, 6]), sb("mv", [P, TILES, 2]), sb("rstd", [P, TILES])
        with nc.Block() as block:
            @block.vector
            def _(dve):
                with dve.Fori(0, TILES) as t:
                    dve.bn_stats(st6[:, t, :], K.X[:, t, :]).then_inc(s["stats"], 1)
                for t in range(TILES):
                    dve.wait_ge(s["stats"], t + 1)
                    last = dve.bn_aggr(mv[:, t, :], st6[:, t, :])
                last.then_inc(s["var"], 1)
                dve.wait_ge(s["rstd"], 1)
                dve.wait_ge(s["var"], 1)
                with dve.Fori(0, TILES) as t:
                    dve.tensor_scalar(dst[:, t, :], K.X[:, t, :], mv[:, t, 0:1], rstd[:, bass.ds(t, 1)], ALU.subtract, ALU.mult)

            @block.gpsimd
            def _(pool):
                pool.wait_ge(s["var"], 1)
                pool.tensor_scalar(rstd[:, :], mv[:, :, 1], LN_EPS, None, ALU.add).then_inc(s["vareps"], 1)
                pool.wait_ge(s["vareps"], 1)
                pool.tensor_tensor(rstd[:, :], rstd[:, :], K.nhalf[:, :], ALU.pow).then_inc(s["rstd"], 1)


def stage_causal(K):
    nc, w, row = K.nc, K.w, K.row
    K.H = K.es.enter_context(nc.sbuf_tensor("H", [P, TILES, D], F32))
    regroup(K, "g6_", [(K.X, K.X)], False)
    plain_norm(K, "h6_", K.H)
    layer_norm(K, "n6_", src=K.H, affine=("ln1w", "ln1b"))
    with ExitStack() as keep:
        rt = lambda n, sh, dt=F32: keep.enter_context(nc.sbuf_tensor("a6_" + n, sh, dt))
        QT, KT, V = rt("QT", [D, TILES * P]), rt("KTall", [D, TILES * P]), rt("V", [P, TILES, D])
        project(K, "p6_", QT, KT, V, "q5T", "k5T", "v5T")
        with ExitStack() as st:
            s = K.sems(st, "a6_", UNIT_SEMS + "const zero init qbd kin vin oT oTc y ysum")
            sb = lambda n, sh, dt=F32: st.enter_context(nc.sbuf_tensor("u6_" + n, sh, dt))
            U, TOTAL, NB = 1, TILES, 4
            Qbd, kt = sb("Qbd", [D, 2, NB, 4, S5]), sb("kt", [D, 2, P])
            Vbd = sb("Vbd", [P, 2, NB, HEADS, HD + 1])
            rep, tri = sb("rep", [S5, P], BF16), sb("tri", [S5, S5], BF16)
            rl, o = sb("rl", [P, 2, 4, NB]), sb("o", [P, 2, D])
            oT, ya = sb("oT", [D, P]), sb("ya", [P, D])
            at = Attention(K, st, s, "a6_", TOTAL, S5, 1.0 / float(HD) ** 0.5, cols=512, split=2)
            M = K.psM

            with nc.Block() as block:
                @block.gpsimd
                def _(pool):
                    pool.memset(Vbd[:, :, :, :, :], 0.0).then_inc(s["zero"], 1)

                    def step(a):
                        wait(pool, s["scored"], a.n - 1)
                        spread_queries(K, Qbd[:, a.par, :, :, :], QT[:, bass.ds(a.t * P, P)], NB, S5).then_inc(s["qbd"], 1)
                        pool.tensor_copy(kt[:, a.par, :], KT[:, bass.ds(a.t * P, P)]).then_inc(s["kin"], 1)

                    run_units(pool, U, TILES, step, 0, 0)

                @block.tensor
                def _(pe):
                    pe.wait_ge(s["const"], 2)

                    def score(a):
                        if not a.inside(TOTAL):
                            return
                        at.scores_free(pe, a)
                        pe.wait_ge(s["qbd"], a.n + 1)
                        pe.wait_ge(s["kin"], a.n + 1)
                        ps = K.psS[a.up]
                        for bank in range(2):
                            last = pe.matmul(ps[:, bank * 512:bank * 512 + 256].rearrange("p (c k) -> p c k", c=8), rep[:, :],
                                             bc(tri[:, :].unsqueeze(1), [S5, 8, S5]), start=True, stop=False,
                                             skip_group_check=True)
                        last.then_inc(s["tiled"], 1)
                        for g in range(4):
                            row_tile_wait(pe, s, a, g)
                            for b in range(NB):
                                col = (g % 2) * 512 + (g // 2) * 128 + b * S5
                                rows = slice(32 * g, 32 * g + 32)
                                last = pe.matmul(ps[:, col:col + S5], Qbd[rows, a.par, b, :, :].rearrange("p j q -> p (j q)"),
                                                 kt[rows, a.par, b * S5:(b + 1) * S5], start=False, stop=True,
                                                 skip_group_check=True)
                            if g < 2:
                                last.then_inc(s["tiled"], 1)
                        last.then_inc(s["scored"], 1)

                    def mix(a):
                        if not a.inside(TOTAL):
                            return
                        pe.wait_ge(s["tcopied"], a.n + 1)
                        pe.wait_ge(s["vin"], a.n + 1)
                        wait(pe, s["normed"], a.n)
                        for g in range(4):
                            i = (g % 2) * 2 + g // 2
                            for j in range(4):
                                last = pe.matmul(K.psO[32 * j:32 * j + 32, g * 36:(g + 1) * 36],
                                                 at.PT[:, a.up, i * P + 32 * j:i * P + 32 * j + 32],
                                                 Vbd[:, a.par, :, 4 * g + j, :], start=True, stop=True)
                        last.then_inc(s["mixed"], 1)

                    def finish(a):
                        if not a.inside(TOTAL):
                            return
                        pe.wait_ge(s["normed"], a.n + 1)
                        wait(pe, s["ysum"], 2 * a.n)
                        pe.transpose(M[:, 0:P], o[:, a.par, :], K.ident).then_inc(s["oT"], 1)
                        pe.wait_ge(s["oTc"], a.n + 1)
                        pe.matmul(M[:, 0:D], oT[:, :], w("proj5T"), start=True, stop=True).then_inc(s["y"], 1)

                    def step(a):
                        score(a.plus(1))
                        at.turn(pe, a)
                        mix(a.plus(-1))
                        finish(a.plus(-2))

                    score(At(0, 0, U))
                    run_units(pe, U, TILES, step, 0, 2)

                @block.scalar
                def _(act):
                    act.copy(rep[:, :], w("repq")[0:S5, :]).then_inc(s["const"], 1)
                    act.mul(tri[:, :], w("causal")[0:S5, :], NEG0).then_inc(s["const"], 1)
                    act.wait_ge(s["zero"], 1)
                    for b in range(NB):
                        act.activation(Vbd[32 * b:32 * b + 32, :, b, :, HD], Vbd[32 * b:32 * b + 32, :, b, :, HD],
                                       ACT.Identity, bias=1.0).then_inc(s["init"], 1)

                    def values(a):
                        if not a.inside(TOTAL):
                            return
                        act.wait_ge(s["init"], NB)
                        wait(act, s["mixed"], a.n - 1)
                        for b in range(NB):
                            rows = slice(32 * b, 32 * b + 32)
                            last = act.copy(Vbd[rows, a.par, b, :, 0:HD],
                                            V[rows, a.t, :].rearrange("p (h d) -> p h d", h=HEADS))
                        last.then_inc(s["vin"], 1)

                    def outT(a):
                        if not a.inside(TOTAL):
                            return
                        act.wait_ge(s["oT"], a.n + 1)
                        wait(act, s["y"], a.n)
                        act.copy(oT[:, :], M[:, 0:P]).then_inc(s["oTc"], 1)

                    def step(a):
                        values(a)
                        at.exp(act, a)
                        at.tcopy(act, a.plus(-1))
                        outT(a.plus(-2))

                    run_units(act, U, TILES, step, 0, 2)

                @block.vector
                def _(dve):
                    def normalise(a):
                        if not a.inside(TOTAL):
                            return
                        dve.wait_ge(s["mixed"], a.n + 1)
                        wait(dve, s["normed"], a.n - 1)
                        ps = K.psO[:, 0:144].rearrange("p (g b e) -> p g b e", g=4, b=NB)
                        dve.reciprocal(rl[:, a.up, :, :], ps[:, :, :, HD]).then_inc(s["recip"], 1)
                        dve.wait_ge(s["recip"], a.n + 1)
                        wait(dve, s["oT"], a.n - 1)
                        for b in range(NB):
                            for j in range(4):
                                rows = slice(32 * j, 32 * j + 32)
                                last = dve.tensor_tensor(
                                    o[32 * b:32 * b + 32, a.par, :].rearrange("p (g j d) -> p g j d", g=4, j=4)[:, :, j, :],
                                    ps[rows, :, b, 0:HD], bc(rl[rows, a.up, :, b].unsqueeze(2), [32, 4, HD]), ALU.mult)
                        last.then_inc(s["normed"], 1)

                    def finish(a):
                        if not a.inside(TOTAL):
                            return
                        dve.wait_ge(s["y"], a.n + 1)
                        wait(dve, s["ysum"], 2 * a.n)
                        dve.tensor_tensor(K.H[:, a.t, :], M[:, 0:D], K.H[:, a.t, :], ALU.add).then_inc(s["ysum"], 1)
                        dve.wait_ge(s["ysum"], 2 * a.n + 1)
                        dve.tensor_tensor(K.X[:, a.t, :], K.X[:, a.t, :], K.H[:, a.t, :], ALU.add).then_inc(s["ysum"], 1)

                    def step(a):
                        at.shift(dve, a)
                        normalise(a.plus(-2))
                        finish(a.plus(-3))

                    run_units(dve, U, TILES, step, 0, 3)
    regroup(K, "b6_", [(K.X, K.X), (K.H, K.H)], True)


def stage_moe(K):
    nc, w, row = K.nc, K.w, K.row
    SPARE = SLOTS
    xe = K.dram("hbm_slots", (SLOTS + TOPK * TILES * P, D))
    ye = K.dram("hbm_results", (SLOTS, D))
    with ExitStack() as keep:
        rt = lambda n, sh, dt=F32: keep.enter_context(nc.sbuf_tensor("f7_" + n, sh, dt))
        logits, X2 = rt("logits", [P, TILES, E1]), rt("X2", [P, TILES, D])
        layer_norm(K, "n7_", router=(w("rw5"), E1, logits), keep=X2, src=K.H, affine=("ln2w", "ln2b"))
        weight = rt("weight", [P, TOPK, TILES])
        into, back = rt("into", [P, TOPK, TILES], U32), rt("back", [P, TOPK, TILES], U32)

        with ExitStack() as st:
            s = K.sems(st, "r7_", "chain shifted exped counted summed zeroed zstored placed scattered")
            sb = lambda n, sh, dt=F32: st.enter_context(nc.sbuf_tensor("r7_" + n, sh, dt))
            mx, ex, rank = sb("mx", [P, TILES]), sb("ex", [P, TILES, E1]), sb("rank", [P, TILES, E1])
            less, pick = sb("less", [P, TILES, E1, E1]), sb("pick", [P, TOPK, TILES, E1])
            count, run = sb("count", [P, TILES, E1]), sb("run", [P, 2, TILES, E1])
            pos, tmp = sb("pos", [P, 2, TILES, E1]), sb("tmp", [P, TOPK, 3, TILES, E1])
            picked, fits = sb("picked", [P, TOPK, 3, TILES]), sb("fits", [P, TOPK, TILES])
            idx, zero = sb("idx", [P, TOPK, 2, TILES]), sb("zero", [P, D])
            TE = [P, TILES, E1]
            with nc.Block() as block:
                @block.vector
                def _(dve):
                    ch = Chain(s["chain"])
                    dve.memset(zero[:, :], 0.0).then_inc(s["zeroed"], 1)
                    ch.link(dve, dve.tensor_reduce(mx[:, :], logits[:, :, :], AX.X, ALU.max))
                    dve.tensor_tensor(ex[:, :, :], logits[:, :, :], bc(mx[:, :].unsqueeze(2), TE), ALU.subtract).then_inc(
                        s["shifted"], 1)
                    rank_columns(dve, ch, rank[:, :, :], less, logits, E1)
                    for k in range(TOPK):
                        last = dve.tensor_scalar(pick[:, k, :, :], rank[:, :, :], float(k), None, ALU.is_equal)
                    ch.link(dve, last)
                    dve.tensor_tensor(count[:, :, :], pick[:, 0, :, :], pick[:, 1, :, :], ALU.add).then_inc(s["counted"], 1)
                    dve.wait_ge(s["summed"], 1)
                    total = K.psM[:, 0:P].rearrange("p (t e) -> p t e", t=TILES)
                    ch.link(dve, dve.tensor_copy(run[:, 0, :, :], total))
                    half = 0
                    for d in (1, 2, 4, 8):
                        dve.tensor_tensor(run[:, 1 - half, d:, :], run[:, half, d:, :], run[:, half, 0:TILES - d, :], ALU.add)
                        ch.link(dve, dve.tensor_copy(run[:, 1 - half, 0:d, :], run[:, half, 0:d, :]))
                        half = 1 - half
                    ch.link(dve, dve.tensor_tensor(run[:, half, :, :], run[:, half, :, :], total, ALU.subtract))
                    before = K.psO[:, 0:P].rearrange("p (t e) -> p t e", t=TILES)
                    ch.link(dve, dve.tensor_tensor(pos[:, 0, :, :], run[:, half, :, :], before, ALU.add))
                    ch.link(dve, dve.tensor_scalar(run[:, half, 0, :], w("expert"), float(CAP), None, ALU.mult))
                    ch.link(dve, dve.tensor_tensor(pos[:, 1, :, :], pos[:, 0, :, :],
                                                   bc(run[:, half, 0, :].unsqueeze(1), TE), ALU.add))
                    dve.wait_ge(s["exped"], 1)
                    for k in range(TOPK):
                        for i, v in enumerate((pos[:, 0, :, :], pos[:, 1, :, :], ex[:, :, :])):
                            last = dve.tensor_tensor(tmp[:, k, i, :, :], pick[:, k, :, :], v, ALU.mult)
                    ch.link(dve, last)
                    ch.link(dve, dve.tensor_reduce(picked[:, :, :, :], tmp[:, :, :, :, :], AX.X, ALU.add))
                    ch.link(dve, dve.tensor_scalar(fits[:, :, :], picked[:, :, 0, :], float(CAP), None, ALU.is_lt))
                    ch.link(dve, dve.tensor_tensor(idx[:, :, 1, :], picked[:, :, 1, :], fits[:, :, :], ALU.mult))
                    for k in range(TOPK):
                        last = dve.tensor_scalar(idx[:, k, 0, :], w("token"), float(SPARE + k * TILES * P), None, ALU.add)
                    ch.link(dve, last)
                    ch.link(dve, dve.tensor_scalar(tmp[:, :, 0, :, 0], fits[:, :, :], -1.0, 1.0, ALU.mult, ALU.add))
                    ch.link(dve, dve.tensor_tensor(idx[:, :, 0, :], idx[:, :, 0, :], tmp[:, :, 0, :, 0], ALU.mult))
                    ch.link(dve, dve.tensor_tensor(idx[:, :, 0, :], idx[:, :, 0, :], idx[:, :, 1, :], ALU.add))
                    dve.tensor_copy(back[:, :, :], idx[:, :, 1, :])
                    dve.tensor_copy(into[:, :, :], idx[:, :, 0, :]).then_inc(s["placed"], 1)
                    ch.link(dve, dve.tensor_tensor(mx[:, :], picked[:, 0, 2, :], picked[:, 1, 2, :], ALU.add))
                    ch.link(dve, dve.reciprocal(mx[:, :], mx[:, :]))
                    ch.link(dve, dve.tensor_tensor(weight[:, :, :], picked[:, :, 2, :],
                                                   bc(mx[:, :].unsqueeze(1), [P, TOPK, TILES]), ALU.mult))
                    ch.link(dve, dve.tensor_tensor(weight[:, :, :], weight[:, :, :], fits[:, :, :], ALU.mult))

                @block.scalar
                def _(act):
                    act.wait_ge(s["shifted"], 1)
                    act.activation(ex[:, :, :], ex[:, :, :], ACT.Exp).then_inc(s["exped"], 1)

                @block.tensor
                def _(pe):
                    pe.wait_ge(s["counted"], 1)
                    cnt = count[:, :, :].rearrange("p t e -> p (t e)")
                    pe.matmul(K.psO[:, 0:P], w("tri"), cnt, start=True, stop=True)
                    pe.matmul(K.psM[:, 0:P], w("ones"), cnt, start=True, stop=True).then_inc(s["summed"], 1)

                @block.sync
                def _(sp):
                    sp.wait_ge(s["zeroed"], 1)
                    sp.dma_start(xe[0:SLOTS, :].rearrange("(p r) d -> p r d", p=P),
                                 bc(zero[:, :].unsqueeze(1), [P, SLOTS // P, D])).then_inc(s["zstored"], 16)

                @block.gpsimd
                def _(pool):
                    pool.wait_ge(s["placed"], 1)
                    pool.wait_ge(s["zstored"], 16)
                    for t in range(TILES):
                        for k in range(TOPK):
                            pool.indirect_dma_start(xe, bass.IndirectOffsetOnAxis(ap=into[:, k, t:t + 1], axis=0),
                                                    X2[:, t, :], None).then_inc(s["scattered"], 16)
                    pool.wait_ge(s["scattered"], 16 * TILES * TOPK)

        with ExitStack() as st:
            s = K.sems(st, "e7_", "xin0 xin1 w1in0 w1in1 w2in0 w2in1 turned xT h gelu y yout stored0 stored1")
            sb = lambda n, sh, dt=F32: st.enter_context(nc.sbuf_tensor("e7_" + n, sh, dt))
            R, FC = CAP // P, FFN // P
            xin, xT = sb("xin", [P, 2, R, D]), sb("xT", [D, 2, CAP])
            w1, w2 = sb("w1", [D, 2, FFN]), sb("w2", [P, 2, FC, D])
            hT, yo = sb("hT", [P, 2, FC, CAP]), sb("yo", [P, 2, R, D])
            psH = [K.psS[1], K.psT]

            def experts(eng, step):
                for e in range(2):
                    step(e, e, 0)
                with eng.Fori(1, E1 // 2) as p:
                    for j in range(2):
                        step(p * 2 + j, j, p)

            with nc.Block() as block:
                @block.sync
                def _(sp):
                    def value(x):
                        return x if isinstance(x, int) else sp.snap(x)

                    def load(e, par):
                        used = [value(e - 1), value(FC * (e - 1)), value(e - 1)]
                        src = [value(e * (CAP * D)), value(e * (D * FFN)), value(e * (FFN * D))]
                        wait(sp, s["turned"], used[0])
                        sp.dma_start(xin[:, par, :, :], bass.AP(xe.tensor, src[0], [[D, P], [P * D, R], [1, D]])).then_inc(
                            s[f"xin{par}"], 16)
                        wait(sp, s["h"], used[1])
                        sp.dma_start(w1[:, par, :], bass.AP(K.A["w1"].tensor, src[1], [[FFN, D], [1, FFN]])).then_inc(
                            s[f"w1in{par}"], 16)
                        wait(sp, s["y"], used[2])
                        sp.dma_start(w2[:, par, :, :], bass.AP(K.A["w2"].tensor, src[2], [[FC * D, P], [D, FC], [1, D]])).then_inc(
                            s[f"w2in{par}"], 16)

                    def store(e, par):
                        ready, dst = value(e + 1), value(e * (CAP * D))
                        sp.wait_ge(s["yout"], ready)
                        sp.dma_start(bass.AP(ye.tensor, dst, [[D, P], [P * D, R], [1, D]]), yo[:, par, :, :]).then_inc(
                            s[f"stored{par}"], 16)

                    load(0, 0)
                    load(1, 1)
                    store(0, 0)
                    with sp.Fori(1, E1 // 2) as p:
                        load(p * 2, 0)
                        store(p * 2 - 1, 1)
                        load(p * 2 + 1, 1)
                        store(p * 2, 0)
                    store(E1 - 1, 1)
                    for par in range(2):
                        sp.wait_ge(s[f"stored{par}"], 16 * E1 // 2)

                @block.tensor
                def _(pe):
                    def step(e, par, used):
                        pe.wait_ge(s[f"xin{par}"], 16 * (used + 1))
                        wait(pe, s["xT"], e)
                        for r in range(R):
                            last = pe.transpose(K.psS[0][:, r * P:(r + 1) * P], xin[:, par, r, :], K.ident)
                        last.then_inc(s["turned"], 1)
                        pe.wait_ge(s["xT"], e + 1)
                        pe.wait_ge(s[f"w1in{par}"], 16 * (used + 1))
                        for f in range(FC):
                            wait(pe, s["gelu"], FC * e + f - 1)
                            for lo, n in ((0, 512), (512, CAP - 512)):
                                last = pe.matmul(psH[f % 2][:, lo:lo + n], w1[:, par, f * P:(f + 1) * P],
                                                 xT[:, par, lo:lo + n], start=True, stop=True)
                            last.then_inc(s["h"], 1)
                        pe.wait_ge(s["gelu"], FC * (e + 1))
                        pe.wait_ge(s[f"w2in{par}"], 16 * (used + 1))
                        wait(pe, s["yout"], e)
                        for r in range(R):
                            dst = K.psO[:, r * D:(r + 1) * D] if r < 4 else K.psM[:, 0:D]
                            for f in range(FC):
                                last = pe.matmul(dst, hT[:, par, f, r * P:(r + 1) * P], w2[:, par, f, :],
                                                 start=(f == 0), stop=(f == FC - 1))
                        last.then_inc(s["y"], 1)

                    experts(pe, step)

                @block.scalar
                def _(act):
                    def step(e, par, used):
                        wait(act, s["y"], e - 1)
                        for f in range(FC):
                            act.wait_ge(s["h"], FC * e + f + 1)
                            act.activation(hT[:, par, f, :], psH[f % 2][:, 0:CAP], ACT.Gelu).then_inc(s["gelu"], 1)

                    experts(act, step)

                @block.vector
                def _(dve):
                    def step(e, par, used):
                        dve.wait_ge(s["turned"], e + 1)
                        wait(dve, s["h"], FC * (e - 1))
                        dve.tensor_copy(xT[:, par, :], K.psS[0][:, 0:CAP]).then_inc(s["xT"], 1)
                        dve.wait_ge(s["y"], e + 1)
                        wait(dve, s[f"stored{par}"], 16 * used)
                        dve.tensor_copy(yo[:, par, 0:4, :], K.psO[:, :].rearrange("p (r d) -> p r d", r=4))
                        dve.tensor_copy(yo[:, par, 4, :], K.psM[:, 0:D]).then_inc(s["yout"], 1)

                    experts(dve, step)

        with ExitStack() as st:
            s = K.sems(st, "f7_", "gathered added stored")
            got = st.enter_context(nc.sbuf_tensor("f7_got", [P, TOPK, TILES, D], F32))
            with nc.Block() as block:
                @block.gpsimd
                def _(pool):
                    for t in range(TILES):
                        for k in range(TOPK):
                            pool.indirect_dma_start(got[:, k, t, :], None, ye,
                                                    bass.IndirectOffsetOnAxis(ap=back[:, k, t:t + 1], axis=0)).then_inc(
                                                        s["gathered"], 16)

                @block.vector
                def _(dve):
                    dve.wait_ge(s["gathered"], 16 * TILES * TOPK)
                    for k in range(TOPK):
                        with dve.Fori(0, TILES) as t:
                            if k:
                                dve.wait_ge(s["added"], t + 1)
                            dve.scalar_tensor_tensor(K.X[:, t, :], got[:, k, t, :], weight[:, k, bass.ds(t, 1)], K.X[:, t, :],
                                                     ALU.mult, ALU.add).then_inc(s["added"], 1)

                @block.sync
                def _(sp):
                    sp.wait_ge(s["added"], TOPK * TILES)
                    sp.dma_start(K.out.rearrange("(t b) q d -> (b q) t d", b=TB), K.X[:, :, :]).then_inc(s["stored"], 16)
                    sp.wait_ge(s["stored"], 16)






def kernel(**inputs):
    import numpy as np
    import concourse.bacc as bacc
    from concourse.bass_utils import run_bass_kernel_spmd as run

    I = {k: np.asarray(v) for k, v in inputs.items()}
    f = np.float32

    def chunked(a, n):
        return a.reshape(n, P, -1).transpose(1, 0, 2).reshape(P, -1)

    def experts(a):
        return a.transpose(1, 0, 2).reshape(P, -1)

    p = np.arange(P)
    qkv5 = I["L1_ffn_qkv_weight"].reshape(8, 32, D)
    pack = {
        "WQT": chunked(I["L0_xattn_WQ"].T, 8), "WKT": chunked(I["L0_xattn_WK"].T, 8), "WV": I["L0_xattn_WV"],
        "WO": chunked(I["L0_xattn_WO"], 8),
        "ident": np.eye(P, dtype=f), "headmask": (p[:, None] // HD == np.arange(HEADS)).astype(f),
        "quadmask": (p[:, None] % 32 // HD == np.arange(4)).astype(f), "mask8": (p[:, None] % 64 // HD == np.arange(8)).astype(f),
        "tri": (p[:, None] < p[None, :]).astype(f),
        "ones": np.ones((P, P), f),
        "half": np.concatenate([(p[:, None] == 64 * b + p[None, :] % 64).astype(f) for b in range(2)], 1),
        "expert": np.broadcast_to(np.arange(8, dtype=f), (P, 8)),
        "repq": (p[:, None] == p[None, :] % 32).astype(f),
        "causal": np.where(np.arange(32)[None, :] > p[:, None], 1.0, 0.0).astype(f),
        "token": (p[:, None] + P * np.arange(16)[None, :]).astype(f),
        "qkvT": I["L0_attn_qkv_w"].T, "projT": I["L0_attn_proj_w"].T, "conv1T": I["L0_attn_conv1_w"].T,
        "conv2T": chunked(I["L0_attn_conv2_w"].T, 2), "scale1": I["L0_attn_scale1"][:, None],
        "scale2": I["L0_attn_scale2"][:, None], "conv1_b": I["L0_attn_conv1_b"].reshape(2, P).T,
        "rw": I["L0_ffn_router_w"], "wq": experts(I["L0_ffn_wq"]), "wk": experts(I["L0_ffn_wk"]),
        "wv": experts(I["L0_ffn_wv"]), "wo": experts(I["L0_ffn_wo"]), "bq": I["L0_ffn_bq"].T, "bk": I["L0_ffn_bk"].T,
        "W_outT": I["L1_xattn_W_out"].T, "WqT": I["L1_attn_Wq"].T, "WkT": I["L1_attn_Wk"].T,
        "WvT": I["L1_attn_Wv"].T, "WoT": I["L1_attn_Wo"].T, "bq1": I["L1_attn_bq"][:, None],
        "bk1": I["L1_attn_bk"][:, None], "relT": np.tile(I["L1_attn_rel_emb"][192:320].T, (16, 1)),
        "q5T": qkv5[:, 0:16].reshape(P, D).T, "k5T": np.repeat(qkv5[:, 16:24], 2, axis=0).reshape(P, D).T,
        "v5T": np.repeat(qkv5[:, 24:32], 2, axis=0).reshape(P, D).T, "proj5T": I["L1_ffn_proj_weight"].T,
        "rw5": I["L1_ffn_router_weight"],
    }
    for n, width in PACK:
        assert pack[n].shape == (P, width), (n, pack[n].shape)
    rows = {"bO": "L0_xattn_bO", "gamma": "L0_attn_gamma", "proj_b": "L0_attn_proj_b", "conv2_b": "L0_attn_conv2_b",
            "rb": "L0_ffn_router_b", "bv": "L0_ffn_bv", "bo": "L0_ffn_bo", "b_out": "L1_xattn_b_out",
            "bv1": "L1_attn_bv", "bo1": "L1_attn_bo", "ln1w": "L1_ffn_ln1_weight", "ln1b": "L1_ffn_ln1_bias",
            "ln2w": "L1_ffn_ln2_weight", "ln2b": "L1_ffn_ln2_bias"}
    arrays = {
        "x": I["x"].reshape(TILES, P, D), "ctx": I["ctx_1024"], "ctxT": I["ctx_1024"].transpose(0, 2, 1),
        "mask": I["mask_Bx1xSxS2_ik1"].reshape(TILES, P, KEYS),
        "w1": I["L1_ffn_moe_w1"], "w2": I["L1_ffn_moe_w2"].reshape(E1, FFN // P, P, D).transpose(0, 2, 1, 3),
        "wpack": np.concatenate([pack[n] for n, _ in PACK], 1),
        "rpack": np.concatenate([I[rows[n]].reshape(-1) for n, _ in ROWS]),
    }
    arrays = {k: np.ascontiguousarray(v) for k, v in arrays.items()}
    nc = bacc.Bacc("TRN2", target_bir_lowering=False, num_devices=1)
    aps = {k: nc.dram_tensor(f"in_{k}", v.shape, mybir.dt.from_np(v.dtype), kind="ExternalInput").ap()
           for k, v in arrays.items()}
    out = nc.dram_tensor("out_x", (B, S, D), F32, kind="ExternalOutput").ap()
    build(nc, aps, out)
    r = run(nc, [{f"in_{k}": v for k, v in arrays.items()}], core_ids=[0])
    return r.results[0]["out_x"]
```

```python
from contextlib import ExitStack

import concourse.bass as bass
from concourse import mybir
from concourse.alu_op_type import AluOpType as ALU

ACT = mybir.ActivationFunctionType
AX = mybir.AxisListType
F32 = mybir.dt.float32
BF16 = mybir.dt.bfloat16
I32 = mybir.dt.int32
U32 = mybir.dt.uint32

B, S, D = 32, 64, 128
KEYS = 128
HEADS = 16
HD = D // HEADS
DK = 64
P = 128
TILES = B * S // P
TB = P // S
PAIRS = HEADS // 2
UCOL = 1024
LN_EPS = 1e-5
RMS_NUM = float(D) ** 0.5 + 1e-6
E0 = 4
E1, TOPK, FFN = 8, 2, 512
CAP = 640
SLOTS = E1 * CAP
S5, B5 = B, S
NEG0, NEG1 = -1e9, -1e20

PACK = [("WQT", 1024), ("WKT", 1024), ("WVT", 1024), ("WO", 1024),
        ("ident", 128), ("headmask", 16), ("quadmask", 4), ("mask8", 8), ("batch", 128), ("tri", 128), ("ones", 128),
        ("expert", 8), ("repq", 128), ("causal", 32), ("token", 16),
        ("qkvT", 384), ("projT", 128), ("conv1T", 256), ("conv2T", 256),
        ("scale1", 1), ("scale2", 1), ("conv1_b", 2), ("rw", 4),
        ("wq", 512), ("wk", 512), ("wv", 512), ("wo", 512), ("bq", 4), ("bk", 4),
        ("W_outT", 128), ("WqT", 128), ("WkT", 128), ("WvT", 128), ("WoT", 128), ("bq1", 1), ("bk1", 1),
        ("relT", 128), ("q5T", 128), ("k5T", 128), ("v5T", 128), ("proj5T", 128), ("rw5", 8)]
EARLY = 4 * 1024
OFF, _at = {}, 0
for _n, _w in PACK:
    OFF[_n] = (_at, _w)
    _at += _w
WCOLS = _at
ROWS = [("bO", 128), ("gamma", 128), ("proj_b", 128), ("conv2_b", 128), ("rb", 4), ("bv", 512), ("bo", 512),
        ("b_out", 128), ("bv1", 128), ("bo1", 128), ("ln1w", 128), ("ln1b", 128), ("ln2w", 128), ("ln2b", 128)]
ROFF, _at = {}, 0
for _n, _w in ROWS:
    ROFF[_n] = (_at, _w)
    _at += _w
RCOLS = _at


class At:

    def __init__(self, p, j, units):
        self.p, self.j, self.units = p, j, units
        body = 2 * units
        self.n = p * body + j
        self.t = p * 2 + j // units
        self.u = j % units
        self.par = (j // units) % 2
        self.up = j % 2
        self.round = p + (j // units) // 2

    def plus(self, k):
        return At(self.p, self.j + k, self.units)

    def inside(self, total):
        return not isinstance(self.n, int) or 0 <= self.n < total


def run_units(eng, units, tiles, step, lead=0, tail=3, peel=2):
    body = 2 * units
    turns = tiles // 2
    for p in range(peel):
        for j in range(body):
            step(At(p, j, units))
    with eng.Fori(peel, turns - 1) as p:
        for j in range(body):
            step(At(p, j, units))
    for j in range(body + tail):
        step(At(turns - 1, j, units))


def wait(eng, sem, value):
    if isinstance(value, int):
        if value <= 0:
            return
    else:
        assert value.min_val > 0, "a wait in a loop has to be on a count above zero"
    eng.wait_ge(sem, value)


class Chain:

    def __init__(self, sem):
        self.sem, self.n, self.base = sem, 0, 0

    def link(self, eng, ins):
        ins.then_inc(self.sem, 1)
        self.n += 1
        eng.wait_ge(self.sem, self.base + self.n)

    def loop(self, eng, start, end, body):
        before = self.n
        body(start)
        per, first = self.n - before, self.n
        if end - start > 1:
            with eng.Fori(start + 1, end) as i:
                self.base, self.n = (i - (start + 1)) * per + first, 0
                body(i)
            self.base, self.n = 0, first + per * (end - start - 1)


def bc(ap, shape):
    return ap.broadcast_to(shape)


def build(nc, A, out):
    es = ExitStack()
    with es:
        def sb(name, shape, dt=F32):
            return es.enter_context(nc.sbuf_tensor(name, shape, dt))

        held = []

        def sems(st, prefix, names):
            got = {x: nc.alloc_semaphore(prefix + x) for x in names.split()}
            held.extend(got.values())
            return got

        def clear_semaphores():
            nc.clear_and_free_semaphores(held)
            nc.all_engine_barrier()
            held.clear()

        W = sb("W", [P, WCOLS])
        R = sb("R", [P, RCOLS])
        X = sb("X", [P, TILES, D])
        XnT = sb("XnT", [D, TILES * P])
        ctx = sb("ctx", [KEYS, B, D])
        ctxT = sb("ctxT", [D, B, KEYS])
        nhalf = sb("nhalf", [P, TILES])

        def w(name, lo=0, n=None):
            o, width = OFF[name]
            return W[:, o + lo:o + (lo + n if n is not None else width)]

        def row(name, lo=0, n=None):
            o, width = ROFF[name]
            return R[:, o + lo:o + (lo + n if n is not None else width)]

        ident = w("ident")

        psS = [es.enter_context(nc.psum_tensor(f"scores{i}", [P, UCOL], F32)) for i in range(2)]
        psT = es.enter_context(nc.psum_tensor("probsT", [P, UCOL], F32))
        psO = es.enter_context(nc.psum_tensor("mixed", [P, 512], F32))
        psM = es.enter_context(nc.psum_tensor("misc", [P, 512], F32))

        def dram(name, shape, dt=F32):
            return nc.dram_tensor(name, shape, dt, kind="Internal").ap()

        shared = dict(nc=nc, A=A, out=out, es=es, sb=sb, sems=sems, W=W, R=R, X=X, XnT=XnT, ctx=ctx, ctxT=ctxT, nhalf=nhalf, w=w, row=row,
                     ident=ident, psS=psS, psT=psT, psO=psO, psM=psM, dram=dram)
        K = type("K", (), shared)
        load(K)
        stages = [stage_cross_wide, stage_linear, stage_mlp, stage_expert_attention, stage_cross_masked,
                  stage_relative, stage_causal, stage_moe]
        for f in stages:
            f(K)
            if f in (stage_mlp, stage_relative):
                clear_semaphores()


def load(K):
    nc = K.nc
    with ExitStack() as st:
        s = K.sems(st, "load_", "done const")
        with nc.Block() as block:
            @block.sync
            def _(sp):
                sp.dma_start(K.W[:, 0:EARLY], K.A["wpack"][:, 0:EARLY]).then_inc(s["done"], 16)
                sp.dma_start(K.X[:, :, :], K.A["x"].rearrange("t p d -> p t d")).then_inc(s["done"], 16)
                sp.dma_start(K.R[:, :], K.A["rpack"].partition_broadcast(P)).then_inc(s["done"], 16)
                sp.dma_start(K.ctxT[:, :, :], K.A["ctxT"].rearrange("b d k -> d b k")).then_inc(s["done"], 16)
                sp.dma_start(K.W[:, EARLY:], K.A["wpack"][:, EARLY:]).then_inc(s["done"], 16)
                sp.dma_start(K.ctx[:, :, :], K.A["ctx"].rearrange("b k d -> k b d")).then_inc(s["done"], 16)
                sp.wait_ge(s["done"], 96)

            @block.gpsimd
            def _(pool):
                pool.memset(K.nhalf[:, :], -0.5).then_inc(s["const"], 1)
                pool.wait_ge(s["const"], 1)


def norm_stats(dve, ch, st6, mv, src, n, var_ready):
    for i in range(n):
        last = dve.bn_stats(st6[:, i, :], src[:, i, :])
    ch.link(dve, last)
    for i in range(n):
        last = dve.bn_aggr(mv[:, i, :], st6[:, i, :])
    last.then_inc(var_ready, 1)


def layer_norm(K, tag, router=None, keep=None, src=None, affine=None):
    nc = K.nc
    G = 4
    src = K.X if src is None else src
    with ExitStack() as st:
        s = K.sems(st, tag, "chain scaled var vareps rstd normed kept turned copied logits logitsout xT")
        st6 = st.enter_context(nc.sbuf_tensor(tag + "st6", [P, G, 6], F32))
        mv = st.enter_context(nc.sbuf_tensor(tag + "mv", [P, G, 2], F32))
        rstd = st.enter_context(nc.sbuf_tensor(tag + "rstd", [P, G], F32))
        xn = st.enter_context(nc.sbuf_tensor(tag + "xn", [P, 2, G, D], F32))
        xT = st.enter_context(nc.sbuf_tensor(tag + "xT", [P, 2, G * P], F32))
        groups = TILES // G
        with nc.Block() as block:
            @block.vector
            def _(dve):
                ch = Chain(s["chain"])

                def group(g, par):
                    rows = src[:, bass.ds(g * G, G), :]
                    norm_stats(dve, ch, st6, mv, rows, G, s["var"])
                    dve.wait_ge(s["rstd"], g + 1)
                    wait(dve, s["turned"], g - 1)
                    if keep is not None:
                        wait(dve, s["kept"], g - 1)
                    for i in range(G):
                        last = dve.tensor_scalar(xn[:, par, i, :], src[:, g * G + i, :], mv[:, i, 0:1], rstd[:, i:i + 1],
                                                 ALU.subtract, ALU.mult)
                    if affine is not None:
                        last.then_inc(s["scaled"], 1)
                        for op, v in ((ALU.mult, affine[0]), (ALU.add, affine[1])):
                            dve.wait_ge(s["scaled"], 2 * g + (1 if op == ALU.mult else 2))
                            last = dve.tensor_tensor(xn[:, par, :, :], xn[:, par, :, :],
                                                     bc(K.row(v).unsqueeze(1), [P, G, D]), op)
                            if op == ALU.mult:
                                last.then_inc(s["scaled"], 1)
                    last.then_inc(s["normed"], 1)
                    if router is not None:
                        wait(dve, s["logits"], g + 1)
                        dve.tensor_copy(router[2][:, bass.ds(g * G, G), :],
                                        K.psO[:, 0:G * router[1]].rearrange("p (g e) -> p g e", g=G)).then_inc(s["logitsout"], 1)

                ch.loop(dve, 0, groups // 2, lambda p: (group(p * 2, 0), group(p * 2 + 1, 1)))

            @block.tensor
            def _(pe):
                def group(g, par):
                    pe.wait_ge(s["normed"], g + 1)
                    wait(pe, s["copied"], g - 1)
                    for i in range(G):
                        last = pe.transpose(K.psS[par][:, i * P:(i + 1) * P], xn[:, par, i, :], K.ident)
                    last.then_inc(s["turned"], 1)
                    if router is not None:
                        pe.wait_ge(s["xT"], g + 1)
                        wait(pe, s["logitsout"], g)
                        for i in range(G):
                            last = pe.matmul(K.psO[:, i * router[1]:(i + 1) * router[1]], xT[:, par, i * P:(i + 1) * P],
                                             router[0], start=True, stop=True)
                        last.then_inc(s["logits"], 1)

                group(0, 0)
                group(1, 1)
                with pe.Fori(1, groups // 2) as p:
                    group(p * 2, 0)
                    group(p * 2 + 1, 1)

            @block.scalar
            def _(act):
                def group(g, par):
                    act.wait_ge(s["turned"], g + 1)
                    if router is not None:
                        wait(act, s["logits"], g - 1)
                        act.copy(xT[:, par, :], K.psS[par][:, 0:G * P]).then_inc(s["xT"], 1)
                    act.copy(K.XnT[:, bass.ds(g * G * P, G * P)], K.psS[par][:, 0:G * P]).then_inc(s["copied"], 1)

                group(0, 0)
                group(1, 1)
                with act.Fori(1, groups // 2) as p:
                    group(p * 2, 0)
                    group(p * 2 + 1, 1)

            @block.gpsimd
            def _(pool):
                def group(g, par):
                    pool.wait_ge(s["var"], g + 1)
                    pool.tensor_scalar(rstd[:, :], mv[:, :, 1], LN_EPS, None, ALU.add).then_inc(s["vareps"], 1)
                    pool.wait_ge(s["vareps"], g + 1)
                    pool.tensor_tensor(rstd[:, :], rstd[:, :], K.nhalf[:, 0:G], ALU.pow).then_inc(s["rstd"], 1)
                    if keep is not None:
                        pool.wait_ge(s["normed"], g + 1)
                        pool.tensor_copy(keep[:, bass.ds(g * G, G), :], xn[:, par, :, :]).then_inc(s["kept"], 1)

                group(0, 0)
                group(1, 1)
                with pool.Fori(1, groups // 2) as p:
                    group(p * 2, 0)
                    group(p * 2 + 1, 1)


UNIT_SEMS = "scored tiled maxed shifted exped turned tcopied mixed recip normed "


class Attention:

    def __init__(self, K, st, s, tag, total, keys, scale, cols=UCOL, split=1):
        self.K, self.s, self.total, self.keys, self.scale, self.cols = K, s, total, keys, scale, cols
        self.groups = cols // keys
        self.split = split
        nc = K.nc
        self.P = st.enter_context(nc.sbuf_tensor(tag + "P", [P, 2, cols], F32))
        self.PT = st.enter_context(nc.sbuf_tensor(tag + "PT", [P, 2, cols], F32))
        self.mx = st.enter_context(nc.sbuf_tensor(tag + "mx", [P, 2, self.groups], F32))
        self.banks = (cols + 511) // 512

    def scores_free(self, pe, a):
        wait(pe, self.s["shifted" if self.bias is None else "biased"], a.n - 1)

    def shift(self, dve, a):
        if not a.inside(self.total):
            return
        s, g = self.s, self.groups
        if self.split == 1:
            sc = self.K.psS[a.up][:, 0:self.cols].rearrange("p (g k) -> p g k", g=g)
        else:
            sc = self.K.psS[a.up][:, :].rearrange("p (a g k) -> p a g k", a=2, k=self.keys)[:, :, 0:g // 2, :]
        pr = self.P[:, a.up, :].rearrange("p (g k) -> p g k", g=g)
        mx = self.mx[:, a.up, :]
        out, top, wide = pr, bc(mx.unsqueeze(2), [P, g, self.keys]), mx
        if self.split == 2:
            out = pr.rearrange("p (a g) k -> p a g k", a=2)
            wide = mx.rearrange("p (a g) -> p a g", a=2)
            top = bc(wide.unsqueeze(3), [P, 2, g // 2, self.keys])
        dve.wait_ge(s["scored"], a.n + 1)
        if self.bias is not None:
            wait(dve, s["turned"], (a.n - 1) * self.banks)
            self.bias(dve, a, out, sc).then_inc(s["biased"], 1)
            dve.wait_ge(s["biased"], a.n + 1)
            sc = out
        wait(dve, s["shifted"], a.n - 1)
        dve.tensor_reduce(wide, sc, AX.X, ALU.max).then_inc(s["maxed"], 1)
        wait(dve, s["turned"], (a.n - 1) * self.banks)
        dve.wait_ge(s["maxed"], a.n + 1)
        dve.tensor_tensor(out, sc, top, ALU.subtract).then_inc(s["shifted"], 1)

    def exp(self, act, a):
        if not a.inside(self.total):
            return
        act.wait_ge(self.s["shifted"], a.n + 1)
        act.activation(self.P[:, a.up, :], self.P[:, a.up, :], ACT.Exp, scale=self.scale).then_inc(self.s["exped"], 1)

    def turn(self, pe, a):
        if not a.inside(self.total):
            return
        pe.wait_ge(self.s["exped"], a.n + 1)
        for b in range(self.banks):
            wait(pe, self.s["tcopied"], (a.n - 1) * self.banks + b + 1)
            for c in range(4):
                i = 4 * b + c
                last = pe.transpose(self.K.psT[:, i * P:(i + 1) * P], self.P[:, a.up, i * P:(i + 1) * P], self.K.ident)
            last.then_inc(self.s["turned"], 1)

    def tcopy(self, act, a):
        if not a.inside(self.total):
            return
        for b in range(self.banks):
            act.wait_ge(self.s["turned"], a.n * self.banks + b + 1)
            wait(act, self.s[self.reader[0]], (a.n - 1) * self.reader[1])
            act.copy(self.PT[:, a.up, b * 512:(b + 1) * 512], self.K.psT[:, b * 512:(b + 1) * 512]).then_inc(
                self.s["tcopied"], 1)

    bias = None
    reader = "mixed", 1


def row_tile_wait(pe, s, a, g):
    if g:
        pe.wait_ge(s["tiled"], 3 * a.n + g)


def quad_order():
    return [(g % 2, (g // 2) * 2 + cc, g, cc) for g in range(4) for cc in range(2)]


def pair_slot(c):
    g, cc = c // 2, c % 2
    return (g % 2) * 4 + (g // 2) * 2 + cc


def stage_cross_wide(K):
    layer_norm(K, "n1_")
    nc, w = K.nc, K.w
    with ExitStack() as st:
        s = K.sems(st, "c1_", UNIT_SEMS + "chain cin pre preout gt gtout read rtout scaled y yout xin")
        sb = lambda n, sh, dt=F32: st.enter_context(nc.sbuf_tensor("c1_" + n, sh, dt))
        AQ = sb("AQ", [P, HEADS, D])
        VO = sb("VO", [P, HEADS, D])
        xs = sb("xs", [P, 2, P])
        GT = sb("GT", [P, 2, TB, HEADS, S])
        cs = sb("cs", [KEYS, 2, D])
        RT = sb("RT", [D, 2, HEADS, P])
        rl = sb("rl", [P, 2, PAIRS])
        yb = sb("yb", [P, 2, D])
        U, TOTAL = TB, TILES * TB
        at = Attention(K, st, s, "c1_", TOTAL, KEYS, 1.0 / DK ** 0.5)
        M = K.psM
        at.reader = "read", 2
        PRE = 8

        def weight_products():
            for left, right, dst in (("WQT", "WKT", AQ), ("WVT", "WO", VO)):
                for r in range(2):
                    for hh in range(2):
                        yield left, right, dst, r, hh

        with nc.Block() as block:
            @block.gpsimd
            def _(pool):
                def tile_in(a):
                    if not a.inside(TOTAL):
                        return
                    wait(pool, s["gt"], 4 * (a.t - 1))
                    pool.tensor_copy(xs[:, a.par, :], K.XnT[:, bass.ds(a.t * P, P)]).then_inc(s["xin"], 1)

                def context(a):
                    if not a.inside(TOTAL):
                        return
                    wait(pool, s["read"], 2 * (a.n - 1))
                    pool.tensor_copy(cs[:, a.up, :], K.ctx[:, a.n, :]).then_inc(s["cin"], 1)

                def scale(a):
                    if not a.inside(TOTAL):
                        return
                    pool.wait_ge(s["recip"], a.n + 1)
                    pr = at.P[:, a.up, :].rearrange("p (g k) -> p g k", g=PAIRS)
                    pool.tensor_tensor(pr, pr, bc(rl[:, a.up, :].unsqueeze(2), [P, PAIRS, KEYS]), ALU.mult).then_inc(
                        s["scaled"], 1)

                def step(a):
                    if a.u == 0:
                        tile_in(a.plus(2 * U))
                    context(a.plus(1))
                    scale(a.plus(1))

                first = At(0, 0, U)
                tile_in(first)
                tile_in(first.plus(U))
                context(first)
                scale(first)
                run_units(pool, U, TILES, step, 0, 0)

            @block.tensor
            def _(pe):
                for i, (left, right, _, r, hh) in enumerate(weight_products()):
                    wait(pe, s["preout"], i - 1)
                    for c in range(4):
                        rows = slice(hh * 64, hh * 64 + 64)
                        last = pe.matmul(K.psS[hh][:, c * P:(c + 1) * P], w(left, (4 * r + c) * P, P)[rows, :],
                                         w(right, (4 * r + c) * P, P)[rows, :], start=True, stop=True)
                    last.then_inc(s["pre"], 1)
                pe.wait_ge(s["preout"], PRE)

                def gt(a, r):
                    if not a.inside(TOTAL):
                        return
                    pe.wait_ge(s["xin"], a.t + 1)
                    wait(pe, s["gtout"], 4 * a.t + r)
                    for h in range(4 * r, 4 * r + 4):
                        last = pe.matmul(M[:, (h % 4) * P:(h % 4 + 1) * P], AQ[:, h, :], xs[:, a.par, :],
                                         start=True, stop=True)
                    last.then_inc(s["gt"], 1)

                def score(a):
                    if not a.inside(TOTAL):
                        return
                    at.scores_free(pe, a)
                    pe.wait_ge(s["gtout"], 4 * (a.t + 1))
                    for c in range(PAIRS):
                        last = pe.matmul(K.psS[a.up][:, c * KEYS:(c + 1) * KEYS],
                                         GT[:, a.par, a.u, 2 * c:2 * c + 2, :].rearrange("p h q -> p (h q)"),
                                         K.ctxT[:, a.n, :], start=True, stop=True)
                    last.then_inc(s["scored"], 1)

                def read(a, r):
                    if not a.inside(TOTAL):
                        return
                    pe.wait_ge(s["tcopied"], 2 * a.n + r + 1)
                    pe.wait_ge(s["cin"], a.n + 1)
                    wait(pe, s["rtout"], 2 * a.n + r)
                    if a.u == 1 and r == 0:
                        wait(pe, s["yout"], a.t)
                    pe.matmul(K.psO[:, :], cs[:, a.up, :], at.PT[:, a.up, r * 512:(r + 1) * 512], start=True,
                              stop=True).then_inc(s["read"], 1)

                def outputs(a):
                    if not a.inside(TOTAL):
                        return
                    after = 4 * a.t + 6
                    pe.wait_ge(s["rtout"], after if not isinstance(after, int) else min(after, 4 * TILES))
                    for h in range(HEADS):
                        last = pe.matmul(K.psO[:, 0:D], RT[:, a.par, h, :], VO[:, h, :], start=(h == 0), stop=(h == HEADS - 1))
                    last.then_inc(s["y"], 1)

                def step(a):
                    nt, p1 = a.plus(3), a.plus(-1)
                    score(a.plus(1))
                    read(p1, 0)
                    gt(nt, 2 * nt.u)
                    read(p1, 1)
                    gt(nt, 2 * nt.u + 1)
                    if a.u == 1:
                        outputs(a.plus(-2))
                    if a.inside(TOTAL):
                        pe.wait_ge(s["scaled"], a.n + 1)
                    at.turn(pe, a)

                first = At(0, 0, U)
                for r in range(4):
                    gt(first, r)
                for r in range(2):
                    gt(first.plus(U), r)
                score(first)
                run_units(pe, U, TILES, step, 0, 2)

            @block.scalar
            def _(act):
                for i, (_, _, dst, r, hh) in enumerate(weight_products()):
                    act.wait_ge(s["pre"], i + 1)
                    act.copy(dst[:, bass.ds(8 * r + hh, 4, 2), :],
                             K.psS[hh][:, 0:512].rearrange("p (c d) -> p c d", c=4)).then_inc(s["preout"], 1)

                def gt(a, r):
                    if not a.inside(TOTAL):
                        return
                    act.wait_ge(s["gt"], 4 * a.t + r + 1)
                    wait(act, s["scored"], 2 * (a.t - 1))
                    for b in range(TB):
                        last = act.copy(GT[:, a.par, b, 4 * r:4 * r + 4, :],
                                        M[:, :].rearrange("p (h b q) -> p h b q", h=4, b=TB)[:, :, b, :])
                    last.then_inc(s["gtout"], 1)

                def read(a, r):
                    if not a.inside(TOTAL):
                        return
                    act.wait_ge(s["read"], 2 * a.n + r + 1)
                    wait(act, s["y"], a.t - 1)
                    act.copy(RT[:, a.par, 8 * r:8 * r + 8, a.u * S:(a.u + 1) * S],
                             K.psO[:, :].rearrange("p (h q) -> p h q", h=8)).then_inc(s["rtout"], 1)

                def step(a):
                    p1, nt = a.plus(-1), a.plus(3)
                    at.tcopy(act, p1)
                    read(p1, 0)
                    gt(nt, 2 * nt.u)
                    read(p1, 1)
                    gt(nt, 2 * nt.u + 1)
                    at.exp(act, a.plus(1))

                first = At(0, 0, U)
                for r in range(4):
                    gt(first, r)
                for r in range(2):
                    gt(first.plus(U), r)
                at.exp(act, first)
                run_units(act, U, TILES, step, 0, 1)

            @block.vector
            def _(dve):
                def sums(a):
                    if not a.inside(TOTAL):
                        return
                    dve.wait_ge(s["exped"], a.n + 1)
                    wait(dve, s["scaled"], a.n - 1)
                    dve.tensor_reduce(rl[:, a.up, :], at.P[:, a.up, :].rearrange("p (g k) -> p g k", g=PAIRS),
                                      AX.X, ALU.add).then_inc(s["chain"], 1)
                    dve.wait_ge(s["chain"], a.n + 1)
                    dve.reciprocal(rl[:, a.up, :], rl[:, a.up, :]).then_inc(s["recip"], 1)

                def finish(a):
                    if not a.inside(TOTAL):
                        return
                    dve.wait_ge(s["y"], a.t + 1)
                    dve.tensor_tensor(yb[:, a.par, :], K.psO[:, 0:D], K.row("bO"), ALU.add).then_inc(s["yout"], 1)
                    dve.wait_ge(s["yout"], a.t + 1)
                    dve.tensor_tensor(K.X[:, a.t, :], K.X[:, a.t, :], yb[:, a.par, :], ALU.add)

                def step(a):
                    at.shift(dve, a.plus(1))
                    sums(a.plus(1))
                    if a.u == 1:
                        finish(a.plus(-2))

                first = At(0, 0, U)
                at.shift(dve, first)
                sums(first)
                run_units(dve, U, TILES, step, 0, 2)


def bank_views(K):
    return [K.psS[0][:, 0:512], K.psS[0][:, 512:1024], K.psS[1][:, 0:512], K.psS[1][:, 512:1024],
            K.psT[:, 0:512], K.psT[:, 512:1024], K.psO[:, :], K.psM[:, :]]


def stage_linear(K):
    nc, w, row = K.nc, K.w, K.row
    G, GROUPS = 2, TILES // 2
    N = G * P
    K.Xmid = K.es.enter_context(nc.sbuf_tensor("Xmid", [P, TILES, D], F32))
    with ExitStack() as st:
        s = K.sems(st, "l2_", "weights chain var scaled rs xn turned xnT q kv squared phi v kvm KV num rden rdenok o oT oTc y "
                              "ya yg xm")
        sb = lambda n, sh, dt=F32: st.enter_context(nc.sbuf_tensor("l2_" + n, sh, dt))
        Wqkv = sb("Wqkv", [D, 3 * D])
        st6, mv = sb("st6", [P, G, 6]), sb("mv", [P, G, 2])
        rs = sb("rs", [P, 2, G])
        xn = sb("xn", [P, 2, G, D])
        xnT, sqq, sqk = sb("xnT", [D, 2, N]), sb("sqq", [D, N]), sb("sqk", [P, G, D])
        phq, phk = sb("phq", [D, 2, N]), sb("phk", [P, 2, G, D])
        vb = sb("vb", [P, 2, G, TB * D + TB])
        KV = sb("KV", [P, 2, G, TB, D + HEADS])
        den, o, oT = sb("den", [P, G, HEADS]), sb("o", [P, 2, G, D]), sb("oT", [D, 2, N])
        ya = sb("ya", [P, 2, G, D])
        pT, pQ, pKV, pS0, pS1, pN, pO, pY = bank_views(K)
        inside = lambda a: a.inside(GROUPS)

        with nc.Block() as block:
            @block.vector
            def _(dve):
                ch = Chain(s["chain"])
                dve.tensor_scalar(Wqkv[:, :], w("qkvT"), w("scale1"), None, ALU.mult).then_inc(s["weights"], 1)
                ch.link(dve, dve.memset(vb[:, :, :, :], 0.0))
                for b in range(TB):
                    dve.memset(vb[64 * b:64 * b + 64, :, :, TB * D + b:TB * D + b + 1], 1.0).then_inc(s["weights"], 1)

                def xnorm(a):
                    if not inside(a):
                        return
                    src = K.X[:, bass.ds(a.n * G, G), :]
                    wait(dve, s["rs"], a.n)
                    for i in range(G):
                        dve.bn_stats(st6[:, i, :], K.X[:, a.n * G + i, :]).then_inc(s["chain"], 1)
                    dve.wait_ge(s["chain"], 1 + G * (a.n + 1))
                    wait(dve, s["xn"], a.n)
                    for i in range(G):
                        last = dve.bn_aggr(mv[:, i, :], st6[:, i, :])
                    last.then_inc(s["var"], 1)
                    dve.wait_ge(s["rs"], a.n + 1)
                    dve.wait_ge(s["var"], a.n + 1)
                    wait(dve, s["turned"], a.n - 1)
                    for i in range(G):
                        dve.tensor_scalar(K.Xmid[:, a.n * G + i, :], K.X[:, a.n * G + i, :], mv[:, i, 0:1], rs[:, 0, i:i + 1],
                                          ALU.subtract, ALU.mult)
                        last = dve.tensor_scalar(xn[:, a.par, i, :], K.X[:, a.n * G + i, :], mv[:, i, 0:1],
                                                 rs[:, 1, i:i + 1], ALU.subtract, ALU.mult)
                    last.then_inc(s["xn"], 1)

                def mask(a):
                    if not inside(a):
                        return
                    dve.wait_ge(s["KV"], a.n + 1)
                    wait(dve, s["num"], a.n - 1)
                    for i, ps in enumerate((pS0, pS1)):
                        dve.tensor_tensor(KV[:, a.par, i, :, 0:D].rearrange("p b (h e) -> p b h e", h=HEADS),
                                          ps[:, 0:TB * D].rearrange("p (b h e) -> p b h e", b=TB, h=HEADS),
                                          bc(w("headmask").unsqueeze(1).unsqueeze(3), [P, TB, HEADS, HD]), ALU.mult)
                        for b in range(TB):
                            last = dve.tensor_scalar(KV[:, a.par, i, b, D:], w("headmask"),
                                                     ps[:, TB * D + b:TB * D + b + 1], None, ALU.mult)
                    last.then_inc(s["kvm"], 1)

                def values(a):
                    if not inside(a):
                        return
                    dve.wait_ge(s["kv"], a.n + 1)
                    wait(dve, s["KV"], a.n - 1)
                    for b in range(TB):
                        last = dve.tensor_copy(vb[64 * b:64 * b + 64, a.par, :, b * D:(b + 1) * D],
                                               pKV[64 * b:64 * b + 64, :].rearrange("p (i c) -> p i c", i=G)[:, :, D:])
                    last.then_inc(s["v"], 1)

                def divide(a):
                    if not inside(a):
                        return
                    dve.wait_ge(s["num"], a.n + 1)
                    wait(dve, s["o"], a.n)
                    ps = pN[:, 0:G * (D + HEADS)].rearrange("p (i c) -> p i c", i=G)
                    dve.tensor_scalar(den[:, :, :], ps[:, :, D:], 1e-6, None, ALU.add).then_inc(s["rden"], 1)
                    dve.wait_ge(s["rden"], a.n + 1)
                    dve.reciprocal(den[:, :, :], den[:, :, :]).then_inc(s["rdenok"], 1)
                    dve.wait_ge(s["rdenok"], a.n + 1)
                    wait(dve, s["oT"], a.n - 1)
                    for i in range(G):
                        last = dve.tensor_tensor(o[:, a.par, i, :].rearrange("p (h e) -> p h e", h=HEADS),
                                                 ps[:, i, 0:D].rearrange("p (h e) -> p h e", h=HEADS),
                                                 bc(den[:, i, :].unsqueeze(2), [P, HEADS, HD]), ALU.mult)
                    last.then_inc(s["o"], 1)

                def bias(a):
                    if not inside(a):
                        return
                    dve.wait_ge(s["y"], a.n + 1)
                    wait(dve, s["xm"], a.n - 1)
                    dve.tensor_tensor(ya[:, a.par, :, :], pY[:, 0:N].rearrange("p (i d) -> p i d", i=G),
                                      bc(row("proj_b").unsqueeze(1), [P, G, D]), ALU.add).then_inc(s["ya"], 1)

                def step(a):
                    xnorm(a)
                    mask(a.plus(-1))
                    values(a)
                    divide(a.plus(-1))
                    bias(a.plus(-2))

                run_units(dve, 1, GROUPS, step, 0, 2)

            @block.gpsimd
            def _(pool):
                def scales(a):
                    if not inside(a):
                        return
                    pool.wait_ge(s["var"], a.n + 1)
                    wait(pool, s["xn"], a.n)
                    pool.tensor_scalar(rs[:, 0, :], mv[:, :, 1], LN_EPS, None, ALU.add)
                    pool.tensor_scalar(rs[:, 1, :], mv[:, :, 1], D / RMS_NUM ** 2, None, ALU.mult).then_inc(s["scaled"], 1)
                    pool.wait_ge(s["scaled"], a.n + 1)
                    pool.tensor_tensor(rs[:, :, :], rs[:, :, :], K.nhalf[:, 0:2 * G].rearrange("p (a b) -> p a b", a=2),
                                       ALU.pow).then_inc(s["rs"], 1)

                def mid(a):
                    if not inside(a):
                        return
                    pool.wait_ge(s["ya"], a.n + 1)
                    y = ya[:, a.par, :, :]
                    pool.tensor_tensor(y, y, bc(row("gamma").unsqueeze(1), [P, G, D]), ALU.mult).then_inc(s["yg"], 1)
                    pool.wait_ge(s["yg"], a.n + 1)
                    xl = K.Xmid[:, bass.ds(a.n * G, G), :]
                    pool.tensor_tensor(xl, xl, y, ALU.add).then_inc(s["xm"], 1)

                def step(a):
                    scales(a)
                    mid(a.plus(-2))

                run_units(pool, 1, GROUPS, step, 0, 2)

            @block.scalar
            def _(act):
                def xT(a):
                    if not inside(a):
                        return
                    act.wait_ge(s["turned"], a.n + 1)
                    wait(act, s["kv"], a.n - 1)
                    act.copy(xnT[:, a.par, :], pT[:, 0:N]).then_inc(s["xnT"], 1)

                def outT(a):
                    if not inside(a):
                        return
                    act.wait_ge(s["oT"], a.n + 1)
                    wait(act, s["y"], a.n - 1)
                    act.copy(oT[:, a.par, :], pO[:, 0:N]).then_inc(s["oTc"], 1)

                def phi(a):
                    if not inside(a):
                        return
                    act.wait_ge(s["q"], a.n + 1)
                    wait(act, s["phi"], a.n)
                    act.activation(sqq[:, :], pQ[:, 0:N], ACT.Square)
                    act.wait_ge(s["v"], a.n + 1)
                    act.activation(sqk[:, :, :], pKV[:, :].rearrange("p (i c) -> p i c", i=G)[:, :, 0:D],
                                   ACT.Square).then_inc(s["squared"], 1)
                    act.wait_ge(s["squared"], a.n + 1)
                    wait(act, s["num"], a.n - 1)
                    act.activation(phq[:, a.par, :], sqq[:, :], ACT.Exp, scale=-0.5)
                    act.activation(phk[:, a.par, :, :], sqk[:, :, :], ACT.Exp, scale=-0.5).then_inc(s["phi"], 1)

                def step(a):
                    xT(a)
                    outT(a.plus(-2))
                    phi(a)

                run_units(act, 1, GROUPS, step, 0, 2)

            @block.tensor
            def _(pe):
                def turn(a):
                    if not inside(a):
                        return
                    pe.wait_ge(s["xn"], a.n + 1)
                    wait(pe, s["xnT"], a.n)
                    for i in range(G):
                        last = pe.transpose(pT[:, i * P:(i + 1) * P], xn[:, a.par, i, :], K.ident)
                    last.then_inc(s["turned"], 1)

                def sums(a):
                    if not inside(a):
                        return
                    pe.wait_ge(s["phi"], a.n + 1)
                    pe.wait_ge(s["v"], a.n + 1)
                    wait(pe, s["kvm"], a.n)
                    for i, ps in enumerate((pS0, pS1)):
                        last = pe.matmul(ps[:, 0:TB * D + TB], phk[:, a.par, i, :], vb[:, a.par, i, :], start=True, stop=True)
                    last.then_inc(s["KV"], 1)

                def oturn(a):
                    if not inside(a):
                        return
                    pe.wait_ge(s["o"], a.n + 1)
                    wait(pe, s["oTc"], a.n)
                    for i in range(G):
                        last = pe.transpose(pO[:, i * P:(i + 1) * P], o[:, a.par, i, :], K.ident)
                    last.then_inc(s["oT"], 1)

                def qkv(a):
                    if not inside(a):
                        return
                    pe.wait_ge(s["xnT"], a.n + 1)
                    wait(pe, s["phi"], a.n)
                    wait(pe, s["v"], a.n)
                    pe.matmul(pQ[:, 0:N], Wqkv[:, 0:D], xnT[:, a.par, :], start=True, stop=True).then_inc(s["q"], 1)
                    for i in range(G):
                        last = pe.matmul(pKV[:, i * 2 * D:(i + 1) * 2 * D], xnT[:, a.par, i * P:(i + 1) * P],
                                         Wqkv[:, D:], start=True, stop=True)
                    last.then_inc(s["kv"], 1)

                def numer(a):
                    if not inside(a):
                        return
                    pe.wait_ge(s["kvm"], a.n + 1)
                    wait(pe, s["o"], a.n)
                    c = D + HEADS
                    for i in range(G):
                        for b in range(TB):
                            last = pe.matmul(pN[64 * b:64 * b + 64, i * c:(i + 1) * c],
                                             phq[:, a.par, i * P + 64 * b:i * P + 64 * b + 64],
                                             KV[:, a.par, i, b, :], start=True, stop=True)
                    last.then_inc(s["num"], 1)

                def proj(a):
                    if not inside(a):
                        return
                    pe.wait_ge(s["oTc"], a.n + 1)
                    wait(pe, s["ya"], a.n)
                    for i in range(G):
                        last = pe.matmul(pY[:, i * D:(i + 1) * D], oT[:, a.par, i * P:(i + 1) * P], w("projT"),
                                         start=True, stop=True)
                    last.then_inc(s["y"], 1)

                def step(a):
                    turn(a)
                    sums(a.plus(-1))
                    oturn(a.plus(-2))
                    qkv(a)
                    numer(a.plus(-1))
                    proj(a.plus(-2))

                pe.wait_ge(s["weights"], 3)
                run_units(pe, 1, GROUPS, step, 0, 2)


def stage_mlp(K):
    nc, w, row = K.nc, K.w, K.row
    G, GROUPS = 2, TILES // 2
    N = G * P
    with ExitStack() as st:
        s = K.sems(st, "m2_", "weights ss scaled rs xn turned xnT h gelu y ya yg ym")
        sb = lambda n, sh, dt=F32: st.enter_context(nc.sbuf_tensor("m2_" + n, sh, dt))
        W1 = sb("W1", [D, 2 * D])
        sq, ss, rs = sb("sq", [P, G, D]), sb("ss", [P, G]), sb("rs", [P, G])
        xn, xnT, hT = sb("xn", [P, 2, G, D]), sb("xnT", [D, 2, N]), sb("hT", [P, 2, 2, N])
        ya = sb("ya", [P, 2, G, D])
        banks = bank_views(K)
        pT, pH, pY = banks[0:2], banks[2:4], banks[4:6]
        inside = lambda a: a.inside(GROUPS)

        with nc.Block() as block:
            @block.vector
            def _(dve):
                dve.tensor_scalar(W1[:, :], w("conv1T"), w("scale2"), None, ALU.mult).then_inc(s["weights"], 1)

                def xnorm(a):
                    if not inside(a):
                        return
                    wait(dve, s["scaled"], a.n)
                    wait(dve, s["ss"], G * a.n)
                    for i in range(G):
                        x = K.Xmid[:, a.n * G + i, :]
                        dve.tensor_tensor_reduce(sq[:, i, :], x, x, 1.0, 0.0, ALU.mult, ALU.add,
                                                 ss[:, i:i + 1]).then_inc(s["ss"], 1)
                    dve.wait_ge(s["rs"], a.n + 1)
                    wait(dve, s["turned"], a.n - 1)
                    for i in range(G):
                        last = dve.tensor_scalar(xn[:, a.par, i, :], K.Xmid[:, a.n * G + i, :], rs[:, i:i + 1], None, ALU.mult)
                    last.then_inc(s["xn"], 1)

                def bias(a):
                    if not inside(a):
                        return
                    dve.wait_ge(s["y"], a.n + 1)
                    wait(dve, s["ym"], a.n - 1)
                    dve.tensor_tensor(ya[:, a.par, :, :], pY[a.par][:, 0:N].rearrange("p (i d) -> p i d", i=G),
                                      bc(row("conv2_b").unsqueeze(1), [P, G, D]), ALU.add).then_inc(s["ya"], 1)

                def step(a):
                    xnorm(a)
                    bias(a.plus(-1))

                run_units(dve, 1, GROUPS, step, 0, 1)

            @block.gpsimd
            def _(pool):
                def scales(a):
                    if not inside(a):
                        return
                    pool.wait_ge(s["ss"], G * (a.n + 1))
                    wait(pool, s["xn"], a.n)
                    pool.tensor_scalar(rs[:, :], ss[:, :], 1.0 / RMS_NUM ** 2, None, ALU.mult).then_inc(s["scaled"], 1)
                    pool.wait_ge(s["scaled"], a.n + 1)
                    pool.tensor_tensor(rs[:, :], rs[:, :], K.nhalf[:, 0:G], ALU.pow).then_inc(s["rs"], 1)

                def residual(a):
                    if not inside(a):
                        return
                    pool.wait_ge(s["ya"], a.n + 1)
                    y = ya[:, a.par, :, :]
                    at = bass.ds(a.n * G, G)
                    pool.tensor_tensor(y, y, bc(row("gamma").unsqueeze(1), [P, G, D]), ALU.mult).then_inc(s["yg"], 1)
                    pool.tensor_tensor(K.X[:, at, :], K.X[:, at, :], K.Xmid[:, at, :], ALU.add).then_inc(s["yg"], 1)
                    pool.wait_ge(s["yg"], 2 * a.n + 2)
                    pool.tensor_tensor(K.X[:, at, :], K.X[:, at, :], y, ALU.add).then_inc(s["ym"], 1)

                def step(a):
                    scales(a)
                    residual(a.plus(-1))

                run_units(pool, 1, GROUPS, step, 0, 1)

            @block.scalar
            def _(act):
                def xT(a):
                    if not inside(a):
                        return
                    act.wait_ge(s["turned"], a.n + 1)
                    wait(act, s["h"], 2 * (a.n - 1))
                    act.copy(xnT[:, a.par, :], pT[a.par][:, 0:N]).then_inc(s["xnT"], 1)

                def gelu(a):
                    if not inside(a):
                        return
                    wait(act, s["y"], a.n - 1)
                    for c in range(2):
                        act.wait_ge(s["h"], 2 * a.n + c + 1)
                        act.activation(hT[:, a.par, c, :], pH[c][:, 0:N], ACT.Gelu, bias=w("conv1_b", c, 1)).then_inc(s["gelu"], 1)

                def step(a):
                    xT(a)
                    gelu(a)

                run_units(act, 1, GROUPS, step, 0, 0)

            @block.tensor
            def _(pe):
                def turn(a):
                    if not inside(a):
                        return
                    pe.wait_ge(s["xn"], a.n + 1)
                    wait(pe, s["xnT"], a.n - 1)
                    for i in range(G):
                        last = pe.transpose(pT[a.par][:, i * P:(i + 1) * P], xn[:, a.par, i, :], K.ident)
                    last.then_inc(s["turned"], 1)

                def up(a):
                    if not inside(a):
                        return
                    pe.wait_ge(s["xnT"], a.n + 1)
                    for c in range(2):
                        wait(pe, s["gelu"], 2 * (a.n - 1) + c + 1)
                        pe.matmul(pH[c][:, 0:N], W1[:, c * P:(c + 1) * P], xnT[:, a.par, :], start=True,
                                  stop=True).then_inc(s["h"], 1)

                def down(a):
                    if not inside(a):
                        return
                    pe.wait_ge(s["gelu"], 2 * (a.n + 1))
                    wait(pe, s["ya"], a.n - 1)
                    for i in range(G):
                        for c in range(2):
                            last = pe.matmul(pY[a.par][:, i * D:(i + 1) * D], hT[:, a.par, c, i * P:(i + 1) * P],
                                             w("conv2T", c * P, P), start=(c == 0), stop=(c == 1))
                    last.then_inc(s["y"], 1)

                def step(a):
                    turn(a)
                    down(a.plus(-1))
                    up(a)

                pe.wait_ge(s["weights"], 1)
                run_units(pe, 1, GROUPS, step, 0, 1)


def rank_columns(dve, ch, rank, less, l, E):
    ch.link(dve, dve.memset(less[:, :, :, :], 0.0))
    shape = [P, TILES, E]
    for e in range(E):
        le = l[:, :, e:e + 1]
        if e + 1 < E:
            last = dve.tensor_tensor(less[:, :, e + 1:, e], l[:, :, e + 1:], bc(le, [P, TILES, E - e - 1]), ALU.is_le)
        if e:
            last = dve.tensor_tensor(less[:, :, 0:e, e], l[:, :, 0:e], bc(le, [P, TILES, e]), ALU.is_lt)
    ch.link(dve, last)
    ch.link(dve, dve.tensor_reduce(rank, less[:, :, :, :], AX.X, ALU.add))


def stage_expert_attention(K):
    nc, w, row = K.nc, K.w, K.row
    K.late = K.sems(K.es, "late_", "context")
    K.mask = K.es.enter_context(nc.sbuf_tensor("mask", [P, TILES, KEYS], I32))
    K.ctxS = K.es.enter_context(nc.sbuf_tensor("ctxS", [P, TILES, 2, KEYS], F32))
    with ExitStack() as keep:
        rt = lambda n, sh, dt=F32: keep.enter_context(nc.sbuf_tensor("e3_" + n, sh, dt))
        logits = rt("logits", [P, TILES, E0])
        layer_norm(K, "n3_", router=(w("rw"), E0, logits))
        wtok = rt("wtok", [P, TILES, E0])
        neg, batch = rt("neg", [TB, TILES * E0, S], BF16), rt("batch", [TB, P], BF16)

        with ExitStack() as st:
            s = K.sems(st, "r3_", "chain shifted exped negated turned copied stored row")
            sb = lambda n, sh, dt=F32: st.enter_context(nc.sbuf_tensor("r3_" + n, sh, dt))
            mx, ex, rank = sb("mx", [P, TILES]), sb("ex", [P, TILES, E0]), sb("rank", [P, TILES, E0])
            less, negm = sb("less", [P, TILES, E0, E0]), sb("negm", [P, TILES * E0])
            negT = sb("negT", [TILES * E0, P], BF16)
            scratch = K.dram("hbm_negT", (TB, TILES * E0, S), BF16)
            with nc.Block() as block:
                @block.vector
                def _(dve):
                    ch = Chain(s["chain"])
                    ch.link(dve, dve.tensor_tensor(logits[:, :, :], logits[:, :, :],
                                                   bc(row("rb").unsqueeze(1), [P, TILES, E0]), ALU.add))
                    ch.link(dve, dve.tensor_reduce(mx[:, :], logits[:, :, :], AX.X, ALU.max))
                    dve.tensor_tensor(ex[:, :, :], logits[:, :, :], bc(mx[:, :].unsqueeze(2), [P, TILES, E0]),
                                      ALU.subtract).then_inc(s["shifted"], 1)
                    rank_columns(dve, ch, rank[:, :, :], less, logits, E0)
                    ch.link(dve, dve.tensor_scalar(rank[:, :, :], rank[:, :, :], float(TOPK), None, ALU.is_lt))
                    dve.tensor_scalar(negm[:, :], rank[:, :, :].rearrange("p t e -> p (t e)"), 1.0, -NEG0, ALU.subtract,
                                      ALU.mult).then_inc(s["negated"], 1)
                    dve.wait_ge(s["exped"], 1)
                    ch.link(dve, dve.tensor_reduce(mx[:, :], ex[:, :, :], AX.X, ALU.add))
                    ch.link(dve, dve.reciprocal(mx[:, :], mx[:, :]))
                    ch.link(dve, dve.tensor_tensor(ex[:, :, :], ex[:, :, :], rank[:, :, :], ALU.mult))
                    ch.link(dve, dve.tensor_tensor(wtok[:, :, :], ex[:, :, :], bc(mx[:, :].unsqueeze(2), [P, TILES, E0]),
                                                   ALU.mult))

                @block.tensor
                def _(pe):
                    pe.wait_ge(s["negated"], 1)
                    pe.transpose(K.psM[0:TILES * E0, 0:P], negm[:, :], K.ident).then_inc(s["turned"], 1)

                @block.scalar
                def _(act):
                    act.wait_ge(s["shifted"], 1)
                    act.activation(ex[:, :, :], ex[:, :, :], ACT.Exp).then_inc(s["exped"], 1)
                    act.wait_ge(s["turned"], 1)
                    act.copy(negT[:, :], K.psM[0:TILES * E0, 0:P]).then_inc(s["copied"], 1)
                    act.copy(batch[:, :], w("batch")[0:TB, :])

                @block.sync
                def _(sp):
                    sp.wait_ge(s["copied"], 1)
                    sp.dma_start(scratch.rearrange("b r k -> r b k"), negT[:, :].rearrange("r (b k) -> r b k", b=TB)).then_inc(
                        s["stored"], 16)
                    sp.wait_ge(s["stored"], 16)
                    sp.dma_start(neg[:, :, :], scratch).then_inc(s["row"], 16)
                    sp.wait_ge(s["row"], 16)
                    sp.dma_start(K.mask[:, :, :], K.A["mask"].rearrange("t p k -> p t k")).then_inc(K.late["context"], 16)
                    sp.dma_start(K.ctxS[:, :, :, :], K.A["ctxS"]).then_inc(K.late["context"], 16)

        with ExitStack() as st:
            s = K.sems(st, "e3_", UNIT_SEMS + "init xin q qout k kout v vout kbd weighted oT oTc win wb ysum xsum")
            sb = lambda n, sh, dt=F32: st.enter_context(nc.sbuf_tensor("e3_" + n, sh, dt))
            U, TOTAL = E0, TILES * E0
            xs = sb("xs", [D, 2, P])
            LQ = sb("LQ", [P, 2, E0, 2, P])
            Ks = sb("Ks", [P, 2, E0, 2, S])
            RK = sb("RK", [P, 2, 2, 8, S])
            Vbd = sb("Vbd", [P, 2, E0, PAIRS, TB, 2, HD + 1])
            rl, o = sb("rl", [P, 2, PAIRS, 2]), sb("o", [P, 2, E0, D])
            oT, ya = sb("oT", [D, E0, P]), sb("ya", [P, D])
            ws = sb("ws", [P, E0])
            wb, yb = sb("wb", [P, E0, D]), sb("yb", [P, 2, D])
            at = Attention(K, st, s, "e3_", TOTAL, S, 0.5)
            M = K.psM

            with nc.Block() as block:
                @block.gpsimd
                def _(pool):
                    pool.memset(Vbd[:, :, :, :, :, :, :], 0.0).then_inc(s["init"], 1)
                    pool.memset(LQ[:, :, :, :, :], 0.0).then_inc(s["init"], 1)
                    pool.wait_ge(s["init"], 2)
                    for hh in range(2):
                        pool.memset(Vbd[64 * hh:64 * hh + 64, :, :, :, :, hh, HD].rearrange("p x e c b -> p (x e c b)"),
                                    1.0).then_inc(s["init"], 1)
                    pool.wait_ge(s["init"], 4)

                    def tile_in(a):
                        if not a.inside(TOTAL):
                            return
                        wait(pool, s["v"], a.t - 1)
                        pool.tensor_copy(xs[:, a.par, :], K.XnT[:, bass.ds(a.t * P, P)]).then_inc(s["xin"], 1)

                    def keys(a):
                        if not a.inside(TOTAL):
                            return
                        pool.wait_ge(s["kout"], a.t + 1)
                        wait(pool, s["scored"], a.n - 1)
                        pool.tensor_tensor(RK[:, a.up, :, :, :], bc(Ks[:, a.par, a.u, :, :].unsqueeze(2), [P, 2, 8, S]),
                                           bc(w("mask8").unsqueeze(1).unsqueeze(3), [P, 2, 8, S]), ALU.mult).then_inc(
                                               s["kbd"], 1)

                    def weights(a):
                        if not a.inside(TOTAL):
                            return
                        wait(pool, s["wb"], 3 * a.t)
                        pool.tensor_copy(ws[:, :], wtok[:, a.t, :]).then_inc(s["win"], 1)

                    def weigh(a):
                        if not a.inside(TOTAL):
                            return
                        pool.wait_ge(s["normed"], U * (a.t + 1))
                        pool.wait_ge(s["win"], a.t + 1)
                        ob = o[:, a.par, :, :]
                        pool.tensor_tensor(ob, ob, bc(ws[:, :].unsqueeze(2), [P, E0, D]), ALU.mult).then_inc(
                            s["weighted"], 1)

                    def biases(a):
                        if not a.inside(TOTAL):
                            return
                        pool.tensor_tensor(wb[:, :, :], row("bo").rearrange("p (e d) -> p e d", e=E0),
                                           bc(ws[:, :].unsqueeze(2), [P, E0, D]), ALU.mult).then_inc(s["wb"], 1)
                        pool.wait_ge(s["wb"], 3 * a.t + 1)
                        pool.tensor_tensor(wb[:, 0:2, :], wb[:, 0:2, :], wb[:, 2:4, :], ALU.add).then_inc(s["wb"], 1)
                        pool.wait_ge(s["wb"], 3 * a.t + 2)
                        wait(pool, s["ysum"], a.t - 1)
                        pool.tensor_tensor(yb[:, a.par, :], wb[:, 0, :], wb[:, 1, :], ALU.add).then_inc(s["wb"], 1)

                    def step(a):
                        if a.u == 0:
                            tile_in(a.plus(2 * U))
                            weights(a.plus(-U))
                        keys(a.plus(1))
                        if a.u == 1:
                            weigh(a.plus(-U))
                        if a.u == 2:
                            biases(a.plus(-U))

                    first = At(0, 0, U)
                    tile_in(first)
                    tile_in(first.plus(U))
                    keys(first)
                    run_units(pool, U, TILES, step, 0, U)

                @block.tensor
                def _(pe):
                    def queries(a):
                        if not a.inside(TOTAL):
                            return
                        pe.wait_ge(s["xin"], a.t + 1)
                        wait(pe, s["oTc"], a.t - 2)
                        for e in range(E0):
                            last = pe.matmul(M[:, e * P:(e + 1) * P], w("wq", e * D, D), xs[:, a.par, :], start=True, stop=True)
                        last.then_inc(s["q"], 1)

                    def keys(a):
                        if not a.inside(TOTAL):
                            return
                        pe.wait_ge(s["qout"], a.t + 1)
                        for e in range(E0):
                            last = pe.matmul(M[:, e * P:(e + 1) * P], w("wk", e * D, D), xs[:, a.par, :], start=True, stop=True)
                        last.then_inc(s["k"], 1)

                    def values(a):
                        if not a.inside(TOTAL):
                            return
                        pe.wait_ge(s["kout"], a.t + 1)
                        pe.matmul(M[:, :], xs[:, a.par, :], w("wv"), start=True, stop=True).then_inc(s["v"], 1)

                    def score(a):
                        if not a.inside(TOTAL):
                            return
                        at.scores_free(pe, a)
                        pe.wait_ge(s["qout"], a.t + 1)
                        pe.wait_ge(s["kbd"], a.n + 1)
                        for half in range(2):
                            bank = K.psS[a.up][:, half * 512:(half + 1) * 512]
                            pe.matmul(bank.rearrange("p (h k) -> p h k", h=8), batch[:, :],
                                      bc(neg[:, a.t * E0 + a.u, :].unsqueeze(1), [TB, 8, S]), start=True, stop=False,
                                      skip_group_check=True)
                            last = pe.matmul(bank, LQ[:, a.par, a.u, half, :],
                                             RK[:, a.up, half, :, :].rearrange("p h k -> p (h k)"), start=False, stop=True,
                                             skip_group_check=True)
                        last.then_inc(s["scored"], 1)

                    def mix(a):
                        if a.inside(TOTAL):
                            pe.wait_ge(s["tcopied"], 2 * (a.n + 1))
                            pe.wait_ge(s["vout"], a.t + 1)
                            wait(pe, s["normed"], a.n)
                            for c in range(PAIRS):
                                last = pe.matmul(K.psO[:, c * 36:(c + 1) * 36], at.PT[:, a.up, c * P:(c + 1) * P],
                                                 Vbd[:, a.par, a.u, c, :, :, :], start=True, stop=True)
                        done = a.plus(-U)
                        if a.u == U - 1 and done.inside(TOTAL):
                            pe.wait_ge(s["oTc"], done.t + 1)
                            if not a.inside(TOTAL):
                                pe.wait_ge(s["normed"], TOTAL)
                            for e in range(E0):
                                last = pe.matmul(K.psO[:, 384:384 + D], oT[:, e, :], w("wo", e * D, D), start=(e == 0),
                                                 stop=(e == E0 - 1))
                            last.then_inc(s["mixed"], 1)
                        elif a.inside(TOTAL):
                            last.then_inc(s["mixed"], 1)

                    def oturn(a):
                        if not a.inside(TOTAL):
                            return
                        pe.wait_ge(s["weighted"], a.t + 1)
                        if not isinstance(a.t, int) or a.t + 2 < TILES:
                            pe.wait_ge(s["vout"], a.t + 3)
                        for e in range(E0):
                            last = pe.transpose(M[:, e * P:(e + 1) * P], o[:, a.par, e, :], K.ident)
                        last.then_inc(s["oT"], 1)

                    def step(a):
                        score(a.plus(1))
                        mix(a.plus(-1))
                        at.turn(pe, a)
                        if a.u == 0:
                            queries(a.plus(U))
                        if a.u == 1:
                            keys(a.plus(U - 1))
                        if a.u == 2:
                            values(a.plus(U - 2))
                        if a.u == 3:
                            oturn(a.plus(-U - 3))

                    pe.wait_ge(s["init"], 4)
                    first = At(0, 0, U)
                    queries(first)
                    keys(first)
                    values(first)
                    score(first)
                    run_units(pe, U, TILES, step, 0, U + 1)

                @block.scalar
                def _(act):
                    def outT(a):
                        if not a.inside(TOTAL):
                            return
                        act.wait_ge(s["oT"], a.t + 1)
                        wait(act, s["mixed"], U * (a.t + 1))
                        act.copy(oT[:, :, :], M[:, :].rearrange("p (e q) -> p e q", e=E0)).then_inc(s["oTc"], 1)

                    def step(a):
                        at.tcopy(act, a.plus(-1))
                        if a.u == 0:
                            outT(a.plus(-2 * U))
                        at.exp(act, a)

                    run_units(act, U, TILES, step, 0, U + 1)

                @block.vector
                def _(dve):
                    def spread(dst, bias):
                        for half in range(2):
                            rows = slice(64 * half, 64 * half + 64)
                            for b in range(TB):
                                last = dve.tensor_tensor(dst(b, half),
                                                         M[rows, :].rearrange("p (e b q) -> p e b q", e=E0, b=TB)[:, :, b, :],
                                                         bc(w(bias)[rows, :].unsqueeze(2), [64, E0, S]), ALU.add)
                        return last

                    def queries(a):
                        if not a.inside(TOTAL):
                            return
                        dve.wait_ge(s["q"], a.t + 1)
                        wait(dve, s["scored"], U * (a.t - 1))
                        spread(lambda b, half: LQ[64 * b:64 * b + 64, a.par, :, half, b * S:(b + 1) * S], "bq").then_inc(
                            s["qout"], 1)

                    def keys(a):
                        if not a.inside(TOTAL):
                            return
                        dve.wait_ge(s["k"], a.t + 1)
                        wait(dve, s["kbd"], U * (a.t - 1))
                        spread(lambda b, half: Ks[64 * b:64 * b + 64, a.par, :, half, :], "bk").then_inc(s["kout"], 1)

                    def values(a):
                        if not a.inside(TOTAL):
                            return
                        dve.wait_ge(s["v"], a.t + 1)
                        wait(dve, s["mixed"], U * (a.t - 1))
                        for b in range(TB):
                            rows = slice(64 * b, 64 * b + 64)
                            for hh in range(2):
                                split = lambda x: x.rearrange("p (e c h d) -> p e c h d", e=E0, c=PAIRS, h=2)[:, :, :, hh, :]
                                last = dve.tensor_tensor(Vbd[64 * hh:64 * hh + 64, a.par, :, :, b, hh, 0:HD],
                                                         split(M[rows, :]), split(row("bv")[rows, :]), ALU.add)
                        last.then_inc(s["vout"], 1)

                    def finish(a):
                        dve.wait_ge(s["wb"], 3 * (a.t + 1))
                        wait(dve, s["xsum"], a.t)
                        dve.tensor_tensor(ya[:, :], K.psO[:, 384:384 + D], yb[:, a.par, :], ALU.add).then_inc(s["ysum"], 1)
                        dve.wait_ge(s["ysum"], a.t + 1)
                        dve.tensor_tensor(K.X[:, a.t, :], K.X[:, a.t, :], ya[:, :], ALU.add).then_inc(s["xsum"], 1)

                    def normalise(a):
                        done = a.plus(-U)
                        if a.inside(TOTAL):
                            dve.wait_ge(s["mixed"], a.n + 1)
                        elif a.u == U - 1 and done.inside(TOTAL):
                            dve.wait_ge(s["mixed"], TOTAL + 1)
                        if a.u == U - 1 and done.inside(TOTAL):
                            finish(done)
                        if not a.inside(TOTAL):
                            return
                        wait(dve, s["normed"], a.n - 1)
                        ps = K.psO[:, 0:288].rearrange("p (c b h e) -> p c b h e", c=PAIRS, b=TB, h=2)
                        for b in range(TB):
                            rows = slice(64 * b, 64 * b + 64)
                            last = dve.reciprocal(rl[rows, a.up, :, :], ps[rows, :, b, :, HD])
                        last.then_inc(s["recip"], 1)
                        dve.wait_ge(s["recip"], a.n + 1)
                        wait(dve, s["oT"], a.t - 1)
                        for b in range(TB):
                            rows = slice(64 * b, 64 * b + 64)
                            last = dve.tensor_tensor(o[rows, a.par, a.u, :].rearrange("p (c h d) -> p c h d", c=PAIRS, h=2),
                                                     ps[rows, :, b, :, 0:HD],
                                                     bc(rl[rows, a.up, :, :].unsqueeze(3), [64, PAIRS, 2, HD]), ALU.mult)
                        last.then_inc(s["normed"], 1)

                    def step(a):
                        at.shift(dve, a)
                        normalise(a.plus(-2))
                        if a.u == 1:
                            queries(a.plus(U - 1))
                        if a.u == 2:
                            keys(a.plus(U - 2))
                        if a.u == 3:
                            values(a.plus(U - 3))

                    dve.wait_ge(s["init"], 4)
                    first = At(0, 0, U)
                    queries(first)
                    keys(first)
                    values(first)
                    run_units(dve, U, TILES, step, 0, U + 2)


def stage_cross_masked(K):
    layer_norm(K, "n4_")
    nc, w, row = K.nc, K.w, K.row
    with ExitStack() as st:
        s = K.sems(st, "x4_", UNIT_SEMS + "biased masked zero ones qin kin vin oT oTc ysum xsum")
        sb = lambda n, sh, dt=F32: st.enter_context(nc.sbuf_tensor("x4_" + n, sh, dt))
        U, TOTAL, HALF = 2, TILES * 2, HEADS // 2
        neg = sb("neg", [P, TILES, KEYS], BF16)
        LQ, RK = sb("LQ", [P, 2, 2, P]), sb("RK", [P, 2, HALF, KEYS])
        V1 = sb("V1", [KEYS, 2, TB, HEADS, HD + 1])
        rl, o = sb("rl", [P, 2, HALF]), sb("o", [P, 2, D])
        oT, ya = sb("oT", [D, P]), sb("ya", [P, 2, D])
        at = Attention(K, st, s, "x4_", TOTAL, KEYS, 1.0 / float(D) ** 0.5)
        at.bias = lambda dve, a, out, sc: dve.tensor_tensor(out, sc, bc(neg[:, a.t, :].unsqueeze(1), [P, HALF, KEYS]), ALU.add)
        M = K.psM

        with nc.Block() as block:
            @block.gpsimd
            def _(pool):
                pool.memset(V1[:, :, :, :, HD:HD + 1], 1.0).then_inc(s["ones"], 1)
                pool.memset(LQ[:, :, :, :], 0.0).then_inc(s["zero"], 1)
                pool.wait_ge(K.late["context"], 32)

                def keys(a):
                    if not a.inside(TOTAL):
                        return
                    wait(pool, s["scored"], a.n - 1)
                    pool.tensor_tensor(RK[:, a.up, :, :], bc(K.ctxS[:, a.t, a.u, :].unsqueeze(1), [P, HALF, KEYS]),
                                       bc(w("mask8").unsqueeze(2), [P, HALF, KEYS]), ALU.mult).then_inc(s["kin"], 1)

                def values(a):
                    if not a.inside(TOTAL):
                        return
                    wait(pool, s["mixed"], U * (a.t - 1))
                    pool.tensor_copy(V1[:, a.par, :, :, 0:HD],
                                     K.ctx[:, bass.ds(a.t * TB, TB), :].rearrange("p b (h d) -> p b h d", h=HEADS)).then_inc(
                                         s["vin"], 1)

                def step(a):
                    keys(a.plus(1))
                    if a.u == 1:
                        values(a.plus(1))

                first = At(0, 0, U)
                keys(first)
                values(first)
                run_units(pool, U, TILES, step, 0, 0)

            @block.tensor
            def _(pe):
                def score(a):
                    if not a.inside(TOTAL):
                        return
                    at.scores_free(pe, a)
                    pe.wait_ge(s["qin"], a.t + 1)
                    pe.wait_ge(s["kin"], a.n + 1)
                    for c in range(2):
                        last = pe.matmul(K.psS[a.up][:, c * 512:(c + 1) * 512], LQ[:, a.par, a.u, :],
                                         RK[:, a.up, 4 * c:4 * c + 4, :].rearrange("p h k -> p (h k)"), start=True, stop=True)
                    last.then_inc(s["scored"], 1)

                def mix(a):
                    done = a.plus(-U)
                    if a.inside(TOTAL):
                        pe.wait_ge(s["tcopied"], 2 * (a.n + 1))
                        pe.wait_ge(s["vin"], a.t + 1)
                        wait(pe, s["normed"], a.n)
                        for h in range(HALF):
                            last = pe.matmul(K.psO[:, h * 18:(h + 1) * 18], at.PT[:, a.up, h * P:(h + 1) * P],
                                             V1[:, a.par, :, HALF * a.u + h, :], start=True, stop=True)
                    if a.u == U - 1 and done.inside(TOTAL):
                        pe.wait_ge(s["oTc"], done.t + 1)
                        if not a.inside(TOTAL):
                            pe.wait_ge(s["normed"], TOTAL)
                        last = pe.matmul(K.psO[:, 384:384 + D], oT[:, :], w("W_outT"), start=True, stop=True)
                        last.then_inc(s["mixed"], 1)
                    elif a.inside(TOTAL):
                        last.then_inc(s["mixed"], 1)

                def oturn(a):
                    if not a.inside(TOTAL):
                        return
                    pe.wait_ge(s["normed"], U * (a.t + 1))
                    wait(pe, s["oTc"], a.t)
                    pe.transpose(M[:, 0:P], o[:, a.par, :], K.ident).then_inc(s["oT"], 1)

                def step(a):
                    score(a.plus(1))
                    mix(a.plus(-1))
                    at.turn(pe, a)
                    if a.u == 1:
                        oturn(a.plus(-U))

                pe.wait_ge(s["ones"], 1)
                score(At(0, 0, U))
                run_units(pe, U, TILES, step, 0, U + 1)

            @block.scalar
            def _(act):
                def queries(a):
                    if not a.inside(TOTAL):
                        return
                    wait(act, s["scored"], U * (a.t - 1))
                    for half in range(2):
                        for b in range(TB):
                            last = act.copy(LQ[64 * b:64 * b + 64, a.par, half, b * S:(b + 1) * S],
                                            K.XnT[64 * half:64 * half + 64, bass.ds(a.t * P + b * S, S)])
                    last.then_inc(s["qin"], 1)

                def outT(a):
                    if not a.inside(TOTAL):
                        return
                    act.wait_ge(s["oT"], a.t + 1)
                    wait(act, s["mixed"], U * (a.t + 1))
                    act.copy(oT[:, :], M[:, 0:P]).then_inc(s["oTc"], 1)

                def step(a):
                    at.tcopy(act, a.plus(-1))
                    at.exp(act, a)
                    if a.u == 0:
                        queries(a.plus(U))
                    if a.u == 1:
                        outT(a.plus(-U))

                act.wait_ge(s["zero"], 1)
                queries(At(0, 0, U))
                run_units(act, U, TILES, step, 0, U)

            @block.vector
            def _(dve):
                dve.wait_ge(K.late["context"], 32)
                dve.tensor_scalar(neg[:, :, :], K.mask[:, :, :], 0.0, NEG1, ALU.is_equal, ALU.mult).then_inc(s["masked"], 1)
                dve.wait_ge(s["masked"], 1)

                def finish(a):
                    wait(dve, s["xsum"], a.t - 1)
                    dve.tensor_tensor(ya[:, a.par, :], K.psO[:, 384:384 + D], row("b_out"), ALU.add).then_inc(s["ysum"], 1)
                    dve.wait_ge(s["ysum"], a.t + 1)
                    dve.tensor_tensor(K.X[:, a.t, :], K.X[:, a.t, :], ya[:, a.par, :], ALU.add).then_inc(s["xsum"], 1)

                def normalise(a):
                    done = a.plus(-U)
                    if a.inside(TOTAL):
                        dve.wait_ge(s["mixed"], a.n + 1)
                    elif a.u == U - 1 and done.inside(TOTAL):
                        dve.wait_ge(s["mixed"], TOTAL + 1)
                    if a.u == U - 1 and done.inside(TOTAL):
                        finish(done)
                    if not a.inside(TOTAL):
                        return
                    wait(dve, s["normed"], a.n - 1)
                    ps = K.psO[:, 0:144].rearrange("p (h b e) -> p h b e", h=HALF, b=TB)
                    for b in range(TB):
                        rows = slice(64 * b, 64 * b + 64)
                        last = dve.reciprocal(rl[rows, a.up, :], ps[rows, :, b, HD])
                    last.then_inc(s["recip"], 1)
                    dve.wait_ge(s["recip"], a.n + 1)
                    wait(dve, s["oT"], a.t - 1)
                    for b in range(TB):
                        rows = slice(64 * b, 64 * b + 64)
                        last = dve.tensor_tensor(o[rows, a.par, 64 * a.u:64 * a.u + 64].rearrange("p (h d) -> p h d", h=HALF),
                                                 ps[rows, :, b, 0:HD], bc(rl[rows, a.up, :].unsqueeze(2), [64, HALF, HD]),
                                                 ALU.mult)
                    last.then_inc(s["normed"], 1)

                def step(a):
                    at.shift(dve, a)
                    normalise(a.plus(-2))

                run_units(dve, U, TILES, step, 0, U + 2)


def project(K, tag, QT, KT, V, wq, wk, wv, bq=None, bk=None, bv=None):
    nc, w = K.nc, K.w
    G, GROUPS = 4, TILES // 4
    N = G * P
    with ExitStack() as st:
        s = K.sems(st, tag, "xin q k v qout kout vout")
        xs = st.enter_context(nc.sbuf_tensor(tag + "xs", [D, 2, N], F32))
        banks = bank_views(K)

        def groups(eng, group):
            group(0, 0)
            group(1, 1)
            with eng.Fori(1, GROUPS // 2) as p:
                group(p * 2, 0)
                group(p * 2 + 1, 1)

        with nc.Block() as block:
            @block.gpsimd
            def _(pool):
                def group(g, par):
                    wait(pool, s["v"], g - 1)
                    pool.tensor_copy(xs[:, par, :], K.XnT[:, bass.ds(g * N, N)]).then_inc(s["xin"], 1)

                groups(pool, group)

            @block.tensor
            def _(pe):
                def group(g, par):
                    pe.wait_ge(s["xin"], g + 1)
                    wait(pe, s["qout"], g - 1)
                    pe.matmul(banks[par], w(wq), xs[:, par, :], start=True, stop=True).then_inc(s["q"], 1)
                    wait(pe, s["kout"], g - 1)
                    pe.matmul(banks[2 + par], w(wk), xs[:, par, :], start=True, stop=True).then_inc(s["k"], 1)
                    wait(pe, s["vout"], g - 1)
                    for i in range(G):
                        last = pe.matmul(banks[4 + par][:, i * D:(i + 1) * D], xs[:, par, i * P:(i + 1) * P], w(wv),
                                         start=True, stop=True)
                    last.then_inc(s["v"], 1)

                groups(pe, group)

            @block.scalar
            def _(act):
                def group(g, par):
                    for ready, out, dst, bank, bias in (("q", "qout", QT, par, bq), ("k", "kout", KT, 2 + par, bk)):
                        act.wait_ge(s[ready], g + 1)
                        view = dst[:, bass.ds(g * N, N)]
                        if bias is None:
                            act.copy(view, banks[bank]).then_inc(s[out], 1)
                        else:
                            act.activation(view, banks[bank], ACT.Identity, bias=w(bias)).then_inc(s[out], 1)

                groups(act, group)

            @block.vector
            def _(dve):
                def group(g, par):
                    dve.wait_ge(s["v"], g + 1)
                    ps = banks[4 + par].rearrange("p (i d) -> p i d", i=G)
                    dst = V[:, bass.ds(g * G, G), :]
                    if bv is None:
                        dve.tensor_copy(dst, ps).then_inc(s["vout"], 1)
                    else:
                        dve.tensor_tensor(dst, ps, bc(K.row(bv).unsqueeze(1), [P, G, D]), ALU.add).then_inc(s["vout"], 1)

                groups(dve, group)


def spread_queries(K, dst, src, nb, n):
    return K.nc.gpsimd.tensor_tensor(dst, bc(src.rearrange("p (b q) -> p b q", b=nb).unsqueeze(2), [D, nb, 4, n]),
                                     bc(K.w("quadmask").unsqueeze(1).unsqueeze(3), [D, nb, 4, n]), ALU.mult)


def stage_relative(K):
    layer_norm(K, "n5_")
    nc, w, row = K.nc, K.w, K.row
    with ExitStack() as keep:
        rt = lambda n, sh, dt=F32: keep.enter_context(nc.sbuf_tensor("a5_" + n, sh, dt))
        QT, KT, V = rt("QT", [D, TILES * P]), rt("KTall", [D, TILES * P]), rt("V", [P, TILES, D])
        project(K, "p5_", QT, KT, V, "WqT", "WkT", "WvT", "bq1", "bk1", "bv1")
        dist = K.dram("hbm_dist", (TILES, P, 2 * UCOL))

        with ExitStack() as st:
            s = K.sems(st, "z5_", "rel relbd qin z zout stored0 stored1")
            sb = lambda n, sh, dt=F32: st.enter_context(nc.sbuf_tensor("z5_" + n, sh, dt))
            rel, relbd = sb("rel", [D, P]), sb("relbd", [D, HEADS, P])
            qs, Z = sb("qs", [D, 2, P]), sb("Z", [P, 2, 2, 8, P])
            with nc.Block() as block:
                @block.gpsimd
                def _(pool):
                    pool.wait_ge(s["rel"], 1)
                    pool.tensor_tensor(relbd[:, :, :], bc(rel[:, :].unsqueeze(1), [D, HEADS, P]),
                                       bc(w("headmask").unsqueeze(2), [D, HEADS, P]), ALU.mult).then_inc(s["relbd"], 1)

                    def step(a):
                        wait(pool, s["z"], 2 * (a.t - 1))
                        pool.tensor_copy(qs[:, a.par, :], QT[:, bass.ds(a.t * P, P)]).then_inc(s["qin"], 1)

                    run_units(pool, 1, TILES, step, 0, 0)

                @block.tensor
                def _(pe):
                    pe.wait_ge(s["relbd"], 1)
                    rb = relbd[:, :, :].rearrange("p h j -> p (h j)")

                    def step(a):
                        pe.wait_ge(s["qin"], a.t + 1)
                        for half in range(2):
                            wait(pe, s["zout"], 2 * (a.t - 1) + half + 1)
                            for c in range(2):
                                last = pe.matmul(K.psS[half][:, c * 512:(c + 1) * 512], qs[:, a.par, :],
                                                 rb[:, half * UCOL + c * 512:half * UCOL + (c + 1) * 512], start=True, stop=True)
                            last.then_inc(s["z"], 1)

                    run_units(pe, 1, TILES, step, 0, 0)

                @block.scalar
                def _(act):
                    def step(a):
                        for half in range(2):
                            act.wait_ge(s["z"], 2 * a.t + half + 1)
                            wait(act, s[f"stored{a.par}"], 16 * a.round)
                            act.copy(Z[:, a.par, half, :, :],
                                     K.psS[half][:, :].rearrange("p (h j) -> p h j", h=8)).then_inc(s["zout"], 1)

                    run_units(act, 1, TILES, step, 0, 0)

                @block.vector
                def _(dve):
                    dve.tensor_scalar(rel[:, :], w("relT"), float(HD) ** 0.5, None, ALU.mult).then_inc(s["rel"], 1)

                @block.sync
                def _(sp):
                    def step(a):
                        dst = dist[a.t, :, :]
                        if not isinstance(a.t, int):
                            ready, at = sp.snap(2 * (a.t + 1)), sp.snap(a.t * (P * 2 * UCOL))
                            dst = bass.AP(dist.tensor, at, [[2 * UCOL, P], [1, 2 * UCOL]])
                            sp.wait_ge(s["zout"], ready)
                        else:
                            sp.wait_ge(s["zout"], 2 * (a.t + 1))
                        sp.dma_start(dst, Z[:, a.par, :, :, :].rearrange("p i h j -> p (i h j)")).then_inc(
                            s[f"stored{a.par}"], 16)

                    run_units(sp, 1, TILES, step, 0, 0)
                    for par in range(2):
                        sp.wait_ge(s[f"stored{par}"], 16 * TILES // 2)

        with ExitStack() as st:
            s = K.sems(st, "a5_", UNIT_SEMS + "biased zero init din0 din1 qin kout kin vin oT oTc ysum xsum")
            sb = lambda n, sh, dt=F32: st.enter_context(nc.sbuf_tensor("u5_" + n, sh, dt))
            U, TOTAL = 1, TILES
            S2 = sb("S2", [P, 2, UCOL])
            LQ = sb("LQ", [P, 2, 2, P])
            Ks, RK = sb("Ks", [P, 2, 2, S]), sb("RK", [P, 2, 2, 8, S])
            Vbd = sb("Vbd", [P, 2, PAIRS, TB, 2, HD + 1])
            rl, o = sb("rl", [P, 2, PAIRS, 2]), sb("o", [P, 2, D])
            oT, ya = sb("oT", [D, P]), sb("ya", [P, D])
            at = Attention(K, st, s, "a5_", TOTAL, S, 1.0 / float(HD) ** 0.5)
            M = K.psM

            def add_distances(dve, a, out, sc):
                dve.wait_ge(s[f"din{a.par}"], 16 * TB * (a.round + 1))
                return dve.tensor_tensor(out, sc, S2[:, a.par, :].rearrange("p (g k) -> p g k", g=HEADS), ALU.add)

            at.bias = add_distances

            with nc.Block() as block:
                @block.sync
                def _(sp):
                    def step(a):
                        base = a.t * (P * 2 * UCOL) + (S - 1)
                        if not isinstance(a.t, int):
                            rows = [sp.snap(base), sp.snap(base + S * 2 * UCOL)]
                            sp.wait_ge(s["biased"], sp.snap(a.n - 1))
                        else:
                            rows = [base, base + S * 2 * UCOL]
                            wait(sp, s["biased"], a.n - 1)
                        for b in range(TB):
                            src = bass.AP(dist.tensor, rows[b], [[2 * UCOL - 1, S], [P, HEADS], [1, S]])
                            sp.dma_start(S2[64 * b:64 * b + 64, a.par, :].rearrange("p (h k) -> p h k", h=HEADS),
                                         src).then_inc(s[f"din{a.par}"], 16)

                    run_units(sp, 1, TILES, step, 0, 0)

                @block.gpsimd
                def _(pool):
                    pool.memset(LQ[:, :, :, :], 0.0).then_inc(s["zero"], 1)
                    pool.memset(Vbd[:, :, :, :, :, :], 0.0).then_inc(s["zero"], 1)
                    pool.wait_ge(s["zero"], 2)

                    def step(a):
                        pool.wait_ge(s["kout"], a.n + 1)
                        wait(pool, s["scored"], a.n - 1)
                        last = pool.tensor_tensor(RK[:, a.par, :, :, :], bc(Ks[:, a.par, :, :].unsqueeze(2), [P, 2, 8, S]),
                                                  bc(w("mask8").unsqueeze(1).unsqueeze(3), [P, 2, 8, S]), ALU.mult)
                        last.then_inc(s["kin"], 1)

                    run_units(pool, U, TILES, step, 0, 0)

                @block.tensor
                def _(pe):
                    def score(a):
                        if not a.inside(TOTAL):
                            return
                        at.scores_free(pe, a)
                        pe.wait_ge(s["qin"], a.n + 1)
                        pe.wait_ge(s["kin"], a.n + 1)
                        for half in range(2):
                            last = pe.matmul(K.psS[a.up][:, half * 512:(half + 1) * 512], LQ[:, a.par, half, :],
                                             RK[:, a.par, half, :, :].rearrange("p h k -> p (h k)"), start=True, stop=True)
                        last.then_inc(s["scored"], 1)

                    def mix(a):
                        done = a.plus(-2)
                        if a.inside(TOTAL):
                            pe.wait_ge(s["tcopied"], 2 * (a.n + 1))
                            pe.wait_ge(s["vin"], a.n + 1)
                            wait(pe, s["normed"], a.n)
                            for c in range(PAIRS):
                                last = pe.matmul(K.psO[:, c * 36:(c + 1) * 36], at.PT[:, a.up, c * P:(c + 1) * P],
                                                 Vbd[:, a.par, c, :, :, :], start=True, stop=True)
                        if done.inside(TOTAL):
                            pe.wait_ge(s["oTc"], done.n + 1)
                            if not a.inside(TOTAL):
                                pe.wait_ge(s["normed"], TOTAL)
                                pe.wait_ge(s["ysum"], done.n)
                            last = pe.matmul(K.psO[:, 384:384 + D], oT[:, :], w("WoT"), start=True, stop=True)
                        if a.inside(TOTAL) or done.inside(TOTAL):
                            last.then_inc(s["mixed"], 1)

                    def oturn(a):
                        if not a.inside(TOTAL):
                            return
                        pe.wait_ge(s["normed"], a.n + 1)
                        wait(pe, s["oTc"], a.n)
                        pe.transpose(M[:, 0:P], o[:, a.par, :], K.ident).then_inc(s["oT"], 1)

                    def step(a):
                        score(a.plus(1))
                        mix(a.plus(-1))
                        at.turn(pe, a)
                        oturn(a.plus(-2))

                    score(At(0, 0, U))
                    run_units(pe, U, TILES, step, 0, 3)

                @block.scalar
                def _(act):
                    act.wait_ge(s["zero"], 2)
                    for hh in range(2):
                        ones = Vbd[64 * hh:64 * hh + 64, :, :, :, hh, HD].rearrange("p x c b -> p (x c b)")
                        act.activation(ones, ones, ACT.Identity, bias=1.0).then_inc(s["init"], 1)

                    def queries(a):
                        if not a.inside(TOTAL):
                            return
                        wait(act, s["scored"], a.n - 1)
                        for half in range(2):
                            for b in range(TB):
                                last = act.copy(LQ[64 * b:64 * b + 64, a.par, half, b * S:(b + 1) * S],
                                                QT[64 * half:64 * half + 64, bass.ds(a.t * P + b * S, S)])
                        last.then_inc(s["qin"], 1)
                        wait(act, s["kin"], a.n - 1)
                        for half in range(2):
                            for b in range(TB):
                                last = act.copy(Ks[64 * b:64 * b + 64, a.par, half, :],
                                                KT[64 * half:64 * half + 64, bass.ds(a.t * P + b * S, S)])
                        last.then_inc(s["kout"], 1)

                    def values(a):
                        if not a.inside(TOTAL):
                            return
                        act.wait_ge(s["init"], 2)
                        wait(act, s["mixed"], a.n - 1)
                        for b in range(TB):
                            for hh in range(2):
                                src = V[64 * b:64 * b + 64, a.t, :].rearrange("p (c h d) -> p c h d", c=PAIRS, h=2)
                                last = act.copy(Vbd[64 * hh:64 * hh + 64, a.par, :, b, hh, 0:HD], src[:, :, hh, :])
                        last.then_inc(s["vin"], 1)

                    def outT(a):
                        if not a.inside(TOTAL):
                            return
                        act.wait_ge(s["oT"], a.n + 1)
                        wait(act, s["mixed"], a.n + 2)
                        act.copy(oT[:, :], M[:, 0:P]).then_inc(s["oTc"], 1)

                    def step(a):
                        at.tcopy(act, a.plus(-1))
                        at.exp(act, a)
                        queries(a.plus(2))
                        values(a.plus(1))
                        outT(a.plus(-2))

                    first = At(0, 0, U)
                    queries(first)
                    queries(first.plus(1))
                    values(first)
                    run_units(act, U, TILES, step, 0, 2)

                @block.vector
                def _(dve):
                    def finish(a):
                        wait(dve, s["xsum"], a.n)
                        dve.tensor_tensor(ya[:, :], K.psO[:, 384:384 + D], row("bo1"), ALU.add).then_inc(s["ysum"], 1)
                        dve.wait_ge(s["ysum"], a.n + 1)
                        dve.tensor_tensor(K.X[:, a.t, :], K.X[:, a.t, :], ya[:, :], ALU.add).then_inc(s["xsum"], 1)

                    def normalise(a):
                        done = a.plus(-2)
                        if a.inside(TOTAL) or done.inside(TOTAL):
                            dve.wait_ge(s["mixed"], a.n + 1)
                        if done.inside(TOTAL):
                            finish(done)
                        if not a.inside(TOTAL):
                            return
                        wait(dve, s["normed"], a.n - 1)
                        ps = K.psO[:, 0:288].rearrange("p (c b h e) -> p c b h e", c=PAIRS, b=TB, h=2)
                        for b in range(TB):
                            rows = slice(64 * b, 64 * b + 64)
                            last = dve.reciprocal(rl[rows, a.up, :, :], ps[rows, :, b, :, HD])
                        last.then_inc(s["recip"], 1)
                        dve.wait_ge(s["recip"], a.n + 1)
                        wait(dve, s["oT"], a.n - 1)
                        for b in range(TB):
                            rows = slice(64 * b, 64 * b + 64)
                            last = dve.tensor_tensor(o[rows, a.par, :].rearrange("p (c h d) -> p c h d", c=PAIRS, h=2),
                                                     ps[rows, :, b, :, 0:HD],
                                                     bc(rl[rows, a.up, :, :].unsqueeze(3), [64, PAIRS, 2, HD]), ALU.mult)
                        last.then_inc(s["normed"], 1)

                    def step(a):
                        at.shift(dve, a)
                        normalise(a.plus(-2))

                    run_units(dve, U, TILES, step, 0, 4, peel=3)


def regroup(K, tag, pairs, back):
    nc = K.nc
    with ExitStack() as st:
        s = K.sems(st, tag, "out in")
        mem = [K.dram(f"hbm_{tag}{i}", (TILES * P, D)) for i in range(len(pairs))]
        with nc.Block() as block:
            @block.sync
            def _(sp):
                def natural(m):
                    return m.rearrange("(t p) d -> p t d", p=P)

                def grouped(m, b5):
                    return m.rearrange("(s u b) d -> b s u d", s=S5, b=4)[b5, :, :, :]

                def grouped_sb(x, b5):
                    return x[32 * b5:32 * b5 + 32, :, :]

                n = 0
                for m, (src, _) in zip(mem, pairs):
                    if back:
                        for b5 in range(4):
                            sp.dma_start(grouped(m, b5), grouped_sb(src, b5)).then_inc(s["out"], 16)
                            n += 16
                    else:
                        sp.dma_start(natural(m), src[:, :, :]).then_inc(s["out"], 16)
                        n += 16
                sp.wait_ge(s["out"], n)
                n = 0
                for m, (_, dst) in zip(mem, pairs):
                    if back:
                        sp.dma_start(dst[:, :, :], natural(m)).then_inc(s["in"], 16)
                        n += 16
                    else:
                        for b5 in range(4):
                            sp.dma_start(grouped_sb(dst, b5), grouped(m, b5)).then_inc(s["in"], 16)
                            n += 16
                sp.wait_ge(s["in"], n)


def plain_norm(K, tag, dst):
    nc = K.nc
    with ExitStack() as st:
        s = K.sems(st, tag, "stats var vareps rstd")
        sb = lambda n, sh, dt=F32: st.enter_context(nc.sbuf_tensor(tag + n, sh, dt))
        st6, mv, rstd = sb("st6", [P, TILES, 6]), sb("mv", [P, TILES, 2]), sb("rstd", [P, TILES])
        with nc.Block() as block:
            @block.vector
            def _(dve):
                with dve.Fori(0, TILES) as t:
                    dve.bn_stats(st6[:, t, :], K.X[:, t, :]).then_inc(s["stats"], 1)
                for t in range(TILES):
                    dve.wait_ge(s["stats"], t + 1)
                    last = dve.bn_aggr(mv[:, t, :], st6[:, t, :])
                last.then_inc(s["var"], 1)
                dve.wait_ge(s["rstd"], 1)
                dve.wait_ge(s["var"], 1)
                with dve.Fori(0, TILES) as t:
                    dve.tensor_scalar(dst[:, t, :], K.X[:, t, :], mv[:, t, 0:1], rstd[:, bass.ds(t, 1)], ALU.subtract, ALU.mult)

            @block.gpsimd
            def _(pool):
                pool.wait_ge(s["var"], 1)
                pool.tensor_scalar(rstd[:, :], mv[:, :, 1], LN_EPS, None, ALU.add).then_inc(s["vareps"], 1)
                pool.wait_ge(s["vareps"], 1)
                pool.tensor_tensor(rstd[:, :], rstd[:, :], K.nhalf[:, :], ALU.pow).then_inc(s["rstd"], 1)


def stage_causal(K):
    nc, w, row = K.nc, K.w, K.row
    K.H = K.es.enter_context(nc.sbuf_tensor("H", [P, TILES, D], F32))
    regroup(K, "g6_", [(K.X, K.X)], False)
    plain_norm(K, "h6_", K.H)
    layer_norm(K, "n6_", src=K.H, affine=("ln1w", "ln1b"))
    with ExitStack() as keep:
        rt = lambda n, sh, dt=F32: keep.enter_context(nc.sbuf_tensor("a6_" + n, sh, dt))
        QT, KT, V = rt("QT", [D, TILES * P]), rt("KTall", [D, TILES * P]), rt("V", [P, TILES, D])
        project(K, "p6_", QT, KT, V, "q5T", "k5T", "v5T")
        with ExitStack() as st:
            s = K.sems(st, "a6_", UNIT_SEMS + "const zero init qbd kin vin oT oTc y ysum")
            sb = lambda n, sh, dt=F32: st.enter_context(nc.sbuf_tensor("u6_" + n, sh, dt))
            U, TOTAL, NB = 1, TILES, 4
            Qbd, kt = sb("Qbd", [D, 2, NB, 4, S5]), sb("kt", [D, 2, P])
            Vbd = sb("Vbd", [P, 2, NB, HEADS, HD + 1])
            rep, tri = sb("rep", [S5, P], BF16), sb("tri", [S5, S5], BF16)
            rl, o = sb("rl", [P, 2, 4, NB]), sb("o", [P, 2, D])
            oT, ya = sb("oT", [D, P]), sb("ya", [P, D])
            at = Attention(K, st, s, "a6_", TOTAL, S5, 1.0 / float(HD) ** 0.5, cols=512, split=2)
            M = K.psM

            with nc.Block() as block:
                @block.gpsimd
                def _(pool):
                    pool.memset(Vbd[:, :, :, :, :], 0.0).then_inc(s["zero"], 1)

                    def step(a):
                        wait(pool, s["scored"], a.n - 1)
                        spread_queries(K, Qbd[:, a.par, :, :, :], QT[:, bass.ds(a.t * P, P)], NB, S5).then_inc(s["qbd"], 1)
                        pool.tensor_copy(kt[:, a.par, :], KT[:, bass.ds(a.t * P, P)]).then_inc(s["kin"], 1)

                    run_units(pool, U, TILES, step, 0, 0)

                @block.tensor
                def _(pe):
                    pe.wait_ge(s["const"], 2)

                    def score(a):
                        if not a.inside(TOTAL):
                            return
                        at.scores_free(pe, a)
                        pe.wait_ge(s["qbd"], a.n + 1)
                        pe.wait_ge(s["kin"], a.n + 1)
                        ps = K.psS[a.up]
                        for bank in range(2):
                            last = pe.matmul(ps[:, bank * 512:bank * 512 + 256].rearrange("p (c k) -> p c k", c=8), rep[:, :],
                                             bc(tri[:, :].unsqueeze(1), [S5, 8, S5]), start=True, stop=False,
                                             skip_group_check=True)
                        last.then_inc(s["tiled"], 1)
                        for g in range(4):
                            row_tile_wait(pe, s, a, g)
                            for b in range(NB):
                                col = (g % 2) * 512 + (g // 2) * 128 + b * S5
                                rows = slice(32 * g, 32 * g + 32)
                                last = pe.matmul(ps[:, col:col + S5], Qbd[rows, a.par, b, :, :].rearrange("p j q -> p (j q)"),
                                                 kt[rows, a.par, b * S5:(b + 1) * S5], start=False, stop=True,
                                                 skip_group_check=True)
                            if g < 2:
                                last.then_inc(s["tiled"], 1)
                        last.then_inc(s["scored"], 1)

                    def mix(a):
                        if not a.inside(TOTAL):
                            return
                        pe.wait_ge(s["tcopied"], a.n + 1)
                        pe.wait_ge(s["vin"], a.n + 1)
                        wait(pe, s["normed"], a.n)
                        for g in range(4):
                            i = (g % 2) * 2 + g // 2
                            for j in range(4):
                                last = pe.matmul(K.psO[32 * j:32 * j + 32, g * 36:(g + 1) * 36],
                                                 at.PT[:, a.up, i * P + 32 * j:i * P + 32 * j + 32],
                                                 Vbd[:, a.par, :, 4 * g + j, :], start=True, stop=True)
                        last.then_inc(s["mixed"], 1)

                    def finish(a):
                        if not a.inside(TOTAL):
                            return
                        pe.wait_ge(s["normed"], a.n + 1)
                        wait(pe, s["ysum"], 2 * a.n)
                        pe.transpose(M[:, 0:P], o[:, a.par, :], K.ident).then_inc(s["oT"], 1)
                        pe.wait_ge(s["oTc"], a.n + 1)
                        pe.matmul(M[:, 0:D], oT[:, :], w("proj5T"), start=True, stop=True).then_inc(s["y"], 1)

                    def step(a):
                        score(a.plus(1))
                        mix(a.plus(-1))
                        at.turn(pe, a)
                        finish(a.plus(-2))

                    score(At(0, 0, U))
                    run_units(pe, U, TILES, step, 0, 2)

                @block.scalar
                def _(act):
                    act.copy(rep[:, :], w("repq")[0:S5, :]).then_inc(s["const"], 1)
                    act.mul(tri[:, :], w("causal")[0:S5, :], NEG0).then_inc(s["const"], 1)
                    act.wait_ge(s["zero"], 1)
                    for b in range(NB):
                        act.activation(Vbd[32 * b:32 * b + 32, :, b, :, HD], Vbd[32 * b:32 * b + 32, :, b, :, HD],
                                       ACT.Identity, bias=1.0).then_inc(s["init"], 1)

                    def values(a):
                        if not a.inside(TOTAL):
                            return
                        act.wait_ge(s["init"], NB)
                        wait(act, s["mixed"], a.n - 1)
                        for b in range(NB):
                            rows = slice(32 * b, 32 * b + 32)
                            last = act.copy(Vbd[rows, a.par, b, :, 0:HD],
                                            V[rows, a.t, :].rearrange("p (h d) -> p h d", h=HEADS))
                        last.then_inc(s["vin"], 1)

                    def outT(a):
                        if not a.inside(TOTAL):
                            return
                        act.wait_ge(s["oT"], a.n + 1)
                        wait(act, s["y"], a.n)
                        act.copy(oT[:, :], M[:, 0:P]).then_inc(s["oTc"], 1)

                    def step(a):
                        values(a)
                        at.tcopy(act, a.plus(-1))
                        at.exp(act, a)
                        outT(a.plus(-2))

                    run_units(act, U, TILES, step, 0, 2)

                @block.vector
                def _(dve):
                    def normalise(a):
                        if not a.inside(TOTAL):
                            return
                        dve.wait_ge(s["mixed"], a.n + 1)
                        wait(dve, s["normed"], a.n - 1)
                        ps = K.psO[:, 0:144].rearrange("p (g b e) -> p g b e", g=4, b=NB)
                        dve.reciprocal(rl[:, a.up, :, :], ps[:, :, :, HD]).then_inc(s["recip"], 1)
                        dve.wait_ge(s["recip"], a.n + 1)
                        wait(dve, s["oT"], a.n - 1)
                        for b in range(NB):
                            for j in range(4):
                                rows = slice(32 * j, 32 * j + 32)
                                last = dve.tensor_tensor(
                                    o[32 * b:32 * b + 32, a.par, :].rearrange("p (g j d) -> p g j d", g=4, j=4)[:, :, j, :],
                                    ps[rows, :, b, 0:HD], bc(rl[rows, a.up, :, b].unsqueeze(2), [32, 4, HD]), ALU.mult)
                        last.then_inc(s["normed"], 1)

                    def finish(a):
                        if not a.inside(TOTAL):
                            return
                        dve.wait_ge(s["y"], a.n + 1)
                        wait(dve, s["ysum"], 2 * a.n)
                        dve.tensor_tensor(K.H[:, a.t, :], M[:, 0:D], K.H[:, a.t, :], ALU.add).then_inc(s["ysum"], 1)
                        dve.wait_ge(s["ysum"], 2 * a.n + 1)
                        dve.tensor_tensor(K.X[:, a.t, :], K.X[:, a.t, :], K.H[:, a.t, :], ALU.add).then_inc(s["ysum"], 1)

                    def step(a):
                        at.shift(dve, a)
                        normalise(a.plus(-2))
                        finish(a.plus(-3))

                    run_units(dve, U, TILES, step, 0, 3)
    regroup(K, "b6_", [(K.X, K.X), (K.H, K.H)], True)


def stage_moe(K):
    nc, w, row = K.nc, K.w, K.row
    SPARE = SLOTS
    xe = K.dram("hbm_slots", (SLOTS + TOPK * TILES * P, D))
    ye = K.dram("hbm_results", (SLOTS, D))
    with ExitStack() as keep:
        rt = lambda n, sh, dt=F32: keep.enter_context(nc.sbuf_tensor("f7_" + n, sh, dt))
        logits, X2 = rt("logits", [P, TILES, E1]), rt("X2", [P, TILES, D])
        layer_norm(K, "n7_", router=(w("rw5"), E1, logits), keep=X2, src=K.H, affine=("ln2w", "ln2b"))
        weight = rt("weight", [P, TOPK, TILES])
        into, back = rt("into", [P, TOPK, TILES], U32), rt("back", [P, TOPK, TILES], U32)

        with ExitStack() as st:
            s = K.sems(st, "r7_", "chain shifted exped counted summed zeroed zstored placed scattered")
            sb = lambda n, sh, dt=F32: st.enter_context(nc.sbuf_tensor("r7_" + n, sh, dt))
            mx, ex, rank = sb("mx", [P, TILES]), sb("ex", [P, TILES, E1]), sb("rank", [P, TILES, E1])
            less, pick = sb("less", [P, TILES, E1, E1]), sb("pick", [P, TOPK, TILES, E1])
            count, run = sb("count", [P, TILES, E1]), sb("run", [P, 2, TILES, E1])
            pos, tmp = sb("pos", [P, 2, TILES, E1]), sb("tmp", [P, TOPK, 3, TILES, E1])
            picked, fits = sb("picked", [P, TOPK, 3, TILES]), sb("fits", [P, TOPK, TILES])
            idx, zero = sb("idx", [P, TOPK, 2, TILES]), sb("zero", [P, D])
            TE = [P, TILES, E1]
            with nc.Block() as block:
                @block.vector
                def _(dve):
                    ch = Chain(s["chain"])
                    dve.memset(zero[:, :], 0.0).then_inc(s["zeroed"], 1)
                    ch.link(dve, dve.tensor_reduce(mx[:, :], logits[:, :, :], AX.X, ALU.max))
                    dve.tensor_tensor(ex[:, :, :], logits[:, :, :], bc(mx[:, :].unsqueeze(2), TE), ALU.subtract).then_inc(
                        s["shifted"], 1)
                    rank_columns(dve, ch, rank[:, :, :], less, logits, E1)
                    for k in range(TOPK):
                        last = dve.tensor_scalar(pick[:, k, :, :], rank[:, :, :], float(k), None, ALU.is_equal)
                    ch.link(dve, last)
                    dve.tensor_tensor(count[:, :, :], pick[:, 0, :, :], pick[:, 1, :, :], ALU.add).then_inc(s["counted"], 1)
                    dve.wait_ge(s["summed"], 1)
                    total = K.psM[:, 0:P].rearrange("p (t e) -> p t e", t=TILES)
                    ch.link(dve, dve.tensor_copy(run[:, 0, :, :], total))
                    half = 0
                    for d in (1, 2, 4, 8):
                        dve.tensor_tensor(run[:, 1 - half, d:, :], run[:, half, d:, :], run[:, half, 0:TILES - d, :], ALU.add)
                        ch.link(dve, dve.tensor_copy(run[:, 1 - half, 0:d, :], run[:, half, 0:d, :]))
                        half = 1 - half
                    ch.link(dve, dve.tensor_tensor(run[:, half, :, :], run[:, half, :, :], total, ALU.subtract))
                    before = K.psO[:, 0:P].rearrange("p (t e) -> p t e", t=TILES)
                    ch.link(dve, dve.tensor_tensor(pos[:, 0, :, :], run[:, half, :, :], before, ALU.add))
                    ch.link(dve, dve.tensor_scalar(run[:, half, 0, :], w("expert"), float(CAP), None, ALU.mult))
                    ch.link(dve, dve.tensor_tensor(pos[:, 1, :, :], pos[:, 0, :, :],
                                                   bc(run[:, half, 0, :].unsqueeze(1), TE), ALU.add))
                    dve.wait_ge(s["exped"], 1)
                    for k in range(TOPK):
                        for i, v in enumerate((pos[:, 0, :, :], pos[:, 1, :, :], ex[:, :, :])):
                            last = dve.tensor_tensor(tmp[:, k, i, :, :], pick[:, k, :, :], v, ALU.mult)
                    ch.link(dve, last)
                    ch.link(dve, dve.tensor_reduce(picked[:, :, :, :], tmp[:, :, :, :, :], AX.X, ALU.add))
                    ch.link(dve, dve.tensor_scalar(fits[:, :, :], picked[:, :, 0, :], float(CAP), None, ALU.is_lt))
                    ch.link(dve, dve.tensor_tensor(idx[:, :, 1, :], picked[:, :, 1, :], fits[:, :, :], ALU.mult))
                    for k in range(TOPK):
                        last = dve.tensor_scalar(idx[:, k, 0, :], w("token"), float(SPARE + k * TILES * P), None, ALU.add)
                    ch.link(dve, last)
                    ch.link(dve, dve.tensor_scalar(tmp[:, :, 0, :, 0], fits[:, :, :], -1.0, 1.0, ALU.mult, ALU.add))
                    ch.link(dve, dve.tensor_tensor(idx[:, :, 0, :], idx[:, :, 0, :], tmp[:, :, 0, :, 0], ALU.mult))
                    ch.link(dve, dve.tensor_tensor(idx[:, :, 0, :], idx[:, :, 0, :], idx[:, :, 1, :], ALU.add))
                    dve.tensor_copy(back[:, :, :], idx[:, :, 1, :])
                    dve.tensor_copy(into[:, :, :], idx[:, :, 0, :]).then_inc(s["placed"], 1)
                    ch.link(dve, dve.tensor_tensor(mx[:, :], picked[:, 0, 2, :], picked[:, 1, 2, :], ALU.add))
                    ch.link(dve, dve.reciprocal(mx[:, :], mx[:, :]))
                    ch.link(dve, dve.tensor_tensor(weight[:, :, :], picked[:, :, 2, :],
                                                   bc(mx[:, :].unsqueeze(1), [P, TOPK, TILES]), ALU.mult))
                    ch.link(dve, dve.tensor_tensor(weight[:, :, :], weight[:, :, :], fits[:, :, :], ALU.mult))

                @block.scalar
                def _(act):
                    act.wait_ge(s["shifted"], 1)
                    act.activation(ex[:, :, :], ex[:, :, :], ACT.Exp).then_inc(s["exped"], 1)

                @block.tensor
                def _(pe):
                    pe.wait_ge(s["counted"], 1)
                    cnt = count[:, :, :].rearrange("p t e -> p (t e)")
                    pe.matmul(K.psO[:, 0:P], w("tri"), cnt, start=True, stop=True)
                    pe.matmul(K.psM[:, 0:P], w("ones"), cnt, start=True, stop=True).then_inc(s["summed"], 1)

                @block.sync
                def _(sp):
                    sp.wait_ge(s["zeroed"], 1)
                    sp.dma_start(xe[0:SLOTS, :].rearrange("(p r) d -> p r d", p=P),
                                 bc(zero[:, :].unsqueeze(1), [P, SLOTS // P, D])).then_inc(s["zstored"], 16)

                @block.gpsimd
                def _(pool):
                    pool.wait_ge(s["placed"], 1)
                    pool.wait_ge(s["zstored"], 16)
                    for t in range(TILES):
                        for k in range(TOPK):
                            pool.indirect_dma_start(xe, bass.IndirectOffsetOnAxis(ap=into[:, k, t:t + 1], axis=0),
                                                    X2[:, t, :], None).then_inc(s["scattered"], 16)
                    pool.wait_ge(s["scattered"], 16 * TILES * TOPK)

        with ExitStack() as st:
            s = K.sems(st, "e7_", "xin0 xin1 w1in0 w1in1 w2in0 w2in1 turned xT h gelu y yout stored0 stored1")
            sb = lambda n, sh, dt=F32: st.enter_context(nc.sbuf_tensor("e7_" + n, sh, dt))
            R, FC = CAP // P, FFN // P
            xin, xT = sb("xin", [P, 2, R, D]), sb("xT", [D, 2, CAP])
            w1, w2 = sb("w1", [D, 2, FFN]), sb("w2", [P, 2, FC, D])
            hT, yo = sb("hT", [P, 2, FC, CAP]), sb("yo", [P, 2, R, D])
            psH = [K.psS[1], K.psT]

            def experts(eng, step):
                for e in range(2):
                    step(e, e, 0)
                with eng.Fori(1, E1 // 2) as p:
                    for j in range(2):
                        step(p * 2 + j, j, p)

            with nc.Block() as block:
                @block.sync
                def _(sp):
                    def value(x):
                        return x if isinstance(x, int) else sp.snap(x)

                    def load(e, par):
                        used = [value(e - 1), value(FC * (e - 1)), value(e - 1)]
                        src = [value(e * (CAP * D)), value(e * (D * FFN)), value(e * (FFN * D))]
                        wait(sp, s["turned"], used[0])
                        sp.dma_start(xin[:, par, :, :], bass.AP(xe.tensor, src[0], [[D, P], [P * D, R], [1, D]])).then_inc(
                            s[f"xin{par}"], 16)
                        wait(sp, s["h"], used[1])
                        sp.dma_start(w1[:, par, :], bass.AP(K.A["w1"].tensor, src[1], [[FFN, D], [1, FFN]])).then_inc(
                            s[f"w1in{par}"], 16)
                        wait(sp, s["y"], used[2])
                        sp.dma_start(w2[:, par, :, :], bass.AP(K.A["w2"].tensor, src[2], [[FC * D, P], [D, FC], [1, D]])).then_inc(
                            s[f"w2in{par}"], 16)

                    def store(e, par):
                        ready, dst = value(e + 1), value(e * (CAP * D))
                        sp.wait_ge(s["yout"], ready)
                        sp.dma_start(bass.AP(ye.tensor, dst, [[D, P], [P * D, R], [1, D]]), yo[:, par, :, :]).then_inc(
                            s[f"stored{par}"], 16)

                    load(0, 0)
                    load(1, 1)
                    store(0, 0)
                    with sp.Fori(1, E1 // 2) as p:
                        load(p * 2, 0)
                        store(p * 2 - 1, 1)
                        load(p * 2 + 1, 1)
                        store(p * 2, 0)
                    store(E1 - 1, 1)
                    for par in range(2):
                        sp.wait_ge(s[f"stored{par}"], 16 * E1 // 2)

                @block.tensor
                def _(pe):
                    def step(e, par, used):
                        pe.wait_ge(s[f"xin{par}"], 16 * (used + 1))
                        wait(pe, s["xT"], e)
                        for r in range(R):
                            last = pe.transpose(K.psS[0][:, r * P:(r + 1) * P], xin[:, par, r, :], K.ident)
                        last.then_inc(s["turned"], 1)
                        pe.wait_ge(s["xT"], e + 1)
                        pe.wait_ge(s[f"w1in{par}"], 16 * (used + 1))
                        for f in range(FC):
                            wait(pe, s["gelu"], FC * e + f - 1)
                            for lo, n in ((0, 512), (512, CAP - 512)):
                                last = pe.matmul(psH[f % 2][:, lo:lo + n], w1[:, par, f * P:(f + 1) * P],
                                                 xT[:, par, lo:lo + n], start=True, stop=True)
                            last.then_inc(s["h"], 1)
                        pe.wait_ge(s["gelu"], FC * (e + 1))
                        pe.wait_ge(s[f"w2in{par}"], 16 * (used + 1))
                        wait(pe, s["yout"], e)
                        for r in range(R):
                            dst = K.psO[:, r * D:(r + 1) * D] if r < 4 else K.psM[:, 0:D]
                            for f in range(FC):
                                last = pe.matmul(dst, hT[:, par, f, r * P:(r + 1) * P], w2[:, par, f, :],
                                                 start=(f == 0), stop=(f == FC - 1))
                        last.then_inc(s["y"], 1)

                    experts(pe, step)

                @block.scalar
                def _(act):
                    def step(e, par, used):
                        wait(act, s["y"], e - 1)
                        for f in range(FC):
                            act.wait_ge(s["h"], FC * e + f + 1)
                            act.activation(hT[:, par, f, :], psH[f % 2][:, 0:CAP], ACT.Gelu).then_inc(s["gelu"], 1)

                    experts(act, step)

                @block.vector
                def _(dve):
                    def step(e, par, used):
                        dve.wait_ge(s["turned"], e + 1)
                        wait(dve, s["h"], FC * (e - 1))
                        dve.tensor_copy(xT[:, par, :], K.psS[0][:, 0:CAP]).then_inc(s["xT"], 1)
                        dve.wait_ge(s["y"], e + 1)
                        wait(dve, s[f"stored{par}"], 16 * used)
                        dve.tensor_copy(yo[:, par, 0:4, :], K.psO[:, :].rearrange("p (r d) -> p r d", r=4))
                        dve.tensor_copy(yo[:, par, 4, :], K.psM[:, 0:D]).then_inc(s["yout"], 1)

                    experts(dve, step)

        with ExitStack() as st:
            s = K.sems(st, "f7_", "gathered added stored")
            got = st.enter_context(nc.sbuf_tensor("f7_got", [P, TOPK, TILES, D], F32))
            with nc.Block() as block:
                @block.gpsimd
                def _(pool):
                    for t in range(TILES):
                        for k in range(TOPK):
                            pool.indirect_dma_start(got[:, k, t, :], None, ye,
                                                    bass.IndirectOffsetOnAxis(ap=back[:, k, t:t + 1], axis=0)).then_inc(
                                                        s["gathered"], 16)

                @block.vector
                def _(dve):
                    dve.wait_ge(s["gathered"], 16 * TILES * TOPK)
                    for k in range(TOPK):
                        with dve.Fori(0, TILES) as t:
                            if k:
                                dve.wait_ge(s["added"], t + 1)
                            dve.scalar_tensor_tensor(K.X[:, t, :], got[:, k, t, :], weight[:, k, bass.ds(t, 1)], K.X[:, t, :],
                                                     ALU.mult, ALU.add).then_inc(s["added"], 1)

                @block.sync
                def _(sp):
                    sp.wait_ge(s["added"], TOPK * TILES)
                    sp.dma_start(K.out.rearrange("(t b) q d -> (b q) t d", b=TB), K.X[:, :, :]).then_inc(s["stored"], 16)
                    sp.wait_ge(s["stored"], 16)






def kernel(**inputs):
    import numpy as np
    import concourse.bacc as bacc
    from concourse.bass_utils import run_bass_kernel_spmd as run

    I = {k: np.asarray(v) for k, v in inputs.items()}
    f = np.float32

    def chunked(a, n):
        return a.reshape(n, P, -1).transpose(1, 0, 2).reshape(P, -1)

    def experts(a):
        return a.transpose(1, 0, 2).reshape(P, -1)

    p = np.arange(P)
    qkv5 = I["L1_ffn_qkv_weight"].reshape(8, 32, D)
    pack = {
        "WQT": chunked(I["L0_xattn_WQ"].T, 8), "WKT": chunked(I["L0_xattn_WK"].T, 8), "WVT": chunked(I["L0_xattn_WV"].T, 8),
        "WO": chunked(I["L0_xattn_WO"], 8),
        "ident": np.eye(P, dtype=f), "headmask": (p[:, None] // HD == np.arange(HEADS)).astype(f),
        "quadmask": (p[:, None] % 32 // HD == np.arange(4)).astype(f), "mask8": (p[:, None] % 64 // HD == np.arange(8)).astype(f),
        "batch": (p[:, None] == p[None, :] // S).astype(f), "tri": (p[:, None] < p[None, :]).astype(f),
        "ones": np.ones((P, P), f),
        "expert": np.broadcast_to(np.arange(8, dtype=f), (P, 8)),
        "repq": (p[:, None] == p[None, :] % 32).astype(f),
        "causal": np.where(np.arange(32)[None, :] > p[:, None], 1.0, 0.0).astype(f),
        "token": (p[:, None] + P * np.arange(16)[None, :]).astype(f),
        "qkvT": I["L0_attn_qkv_w"].T, "projT": I["L0_attn_proj_w"].T, "conv1T": I["L0_attn_conv1_w"].T,
        "conv2T": chunked(I["L0_attn_conv2_w"].T, 2), "scale1": I["L0_attn_scale1"][:, None],
        "scale2": I["L0_attn_scale2"][:, None], "conv1_b": I["L0_attn_conv1_b"].reshape(2, P).T,
        "rw": I["L0_ffn_router_w"], "wq": experts(I["L0_ffn_wq"]), "wk": experts(I["L0_ffn_wk"]),
        "wv": experts(I["L0_ffn_wv"]), "wo": experts(I["L0_ffn_wo"]), "bq": I["L0_ffn_bq"].T, "bk": I["L0_ffn_bk"].T,
        "W_outT": I["L1_xattn_W_out"].T, "WqT": I["L1_attn_Wq"].T, "WkT": I["L1_attn_Wk"].T,
        "WvT": I["L1_attn_Wv"].T, "WoT": I["L1_attn_Wo"].T, "bq1": I["L1_attn_bq"][:, None],
        "bk1": I["L1_attn_bk"][:, None], "relT": np.tile(I["L1_attn_rel_emb"][192:320].T, (16, 1)),
        "q5T": qkv5[:, 0:16].reshape(P, D).T, "k5T": np.repeat(qkv5[:, 16:24], 2, axis=0).reshape(P, D).T,
        "v5T": np.repeat(qkv5[:, 24:32], 2, axis=0).reshape(P, D).T, "proj5T": I["L1_ffn_proj_weight"].T,
        "rw5": I["L1_ffn_router_weight"],
    }
    for n, width in PACK:
        assert pack[n].shape == (P, width), (n, pack[n].shape)
    rows = {"bO": "L0_xattn_bO", "gamma": "L0_attn_gamma", "proj_b": "L0_attn_proj_b", "conv2_b": "L0_attn_conv2_b",
            "rb": "L0_ffn_router_b", "bv": "L0_ffn_bv", "bo": "L0_ffn_bo", "b_out": "L1_xattn_b_out",
            "bv1": "L1_attn_bv", "bo1": "L1_attn_bo", "ln1w": "L1_ffn_ln1_weight", "ln1b": "L1_ffn_ln1_bias",
            "ln2w": "L1_ffn_ln2_weight", "ln2b": "L1_ffn_ln2_bias"}
    arrays = {
        "x": I["x"].reshape(TILES, P, D), "ctx": I["ctx_1024"], "ctxT": I["ctx_1024"].transpose(0, 2, 1),
        "ctxS": I["ctx_1024"].reshape(TILES, TB, KEYS, 2, D // 2).transpose(1, 4, 0, 3, 2).reshape(P, TILES, 2, KEYS),
        "mask": I["mask_Bx1xSxS2_ik1"].reshape(TILES, P, KEYS),
        "w1": I["L1_ffn_moe_w1"], "w2": I["L1_ffn_moe_w2"].reshape(E1, FFN // P, P, D).transpose(0, 2, 1, 3),
        "wpack": np.concatenate([pack[n] for n, _ in PACK], 1),
        "rpack": np.concatenate([I[rows[n]].reshape(-1) for n, _ in ROWS]),
    }
    arrays = {k: np.ascontiguousarray(v) for k, v in arrays.items()}
    nc = bacc.Bacc("TRN2", target_bir_lowering=False, num_devices=1)
    aps = {k: nc.dram_tensor(f"in_{k}", v.shape, mybir.dt.from_np(v.dtype), kind="ExternalInput").ap()
           for k, v in arrays.items()}
    out = nc.dram_tensor("out_x", (B, S, D), F32, kind="ExternalOutput").ap()
    build(nc, aps, out)
    r = run(nc, [{f"in_{k}": v for k, v in arrays.items()}], core_ids=[0])
    return r.results[0]["out_x"]
```

```python
from contextlib import ExitStack

import concourse.bass as bass
from concourse import mybir
from concourse.alu_op_type import AluOpType as ALU

ACT = mybir.ActivationFunctionType
AX = mybir.AxisListType
F32 = mybir.dt.float32
BF16 = mybir.dt.bfloat16
I32 = mybir.dt.int32
U32 = mybir.dt.uint32

B, S, D = 32, 64, 128
KEYS = 128
HEADS = 16
HD = D // HEADS
DK = 64
P = 128
TILES = B * S // P
TB = P // S
PAIRS = HEADS // 2
UCOL = 1024
LN_EPS = 1e-5
RMS_NUM = float(D) ** 0.5 + 1e-6
E0 = 4
E1, TOPK, FFN = 8, 2, 512
CAP = 640
SLOTS = E1 * CAP
S5, B5 = B, S
NEG0, NEG1 = -1e9, -1e20

PACK = [("ident", 128), ("WQT", 1024), ("WKT", 1024), ("WVT", 1024), ("WO", 1024),
        ("headmask", 16), ("quadmask", 4), ("mask8", 8), ("batch", 128), ("blockmask", 4), ("tri", 128), ("ones", 128),
        ("expert", 8), ("repq", 128), ("causal", 32), ("token", 16),
        ("qkvT", 384), ("projT", 128), ("conv1T", 256), ("conv2T", 256),
        ("scale1", 1), ("scale2", 1), ("conv1_b", 2), ("rw", 4),
        ("wq", 512), ("wk", 512), ("wv", 512), ("wo", 512), ("bq", 4), ("bk", 4),
        ("W_outT", 128), ("WqT", 128), ("WkT", 128), ("WvT", 128), ("WoT", 128), ("bq1", 1), ("bk1", 1),
        ("relT", 128), ("q5T", 128), ("k5T", 128), ("v5T", 128), ("proj5T", 128), ("rw5", 8)]
EARLY = 128 + 4 * 1024
OFF, _at = {}, 0
for _n, _w in PACK:
    OFF[_n] = (_at, _w)
    _at += _w
WCOLS = _at
ROWS = [("bO", 128), ("gamma", 128), ("proj_b", 128), ("conv2_b", 128), ("rb", 4), ("bv", 512), ("bo", 512),
        ("b_out", 128), ("bv1", 128), ("bo1", 128), ("ln1w", 128), ("ln1b", 128), ("ln2w", 128), ("ln2b", 128)]
ROFF, _at = {}, 0
for _n, _w in ROWS:
    ROFF[_n] = (_at, _w)
    _at += _w
RCOLS = _at


class At:

    def __init__(self, p, j, units):
        self.p, self.j, self.units = p, j, units
        body = 2 * units
        self.n = p * body + j
        self.t = p * 2 + j // units
        self.u = j % units
        self.par = (j // units) % 2
        self.up = j % 2
        self.round = p + (j // units) // 2

    def plus(self, k):
        return At(self.p, self.j + k, self.units)

    def inside(self, total):
        return not isinstance(self.n, int) or 0 <= self.n < total


def run_units(eng, units, tiles, step, tail=3, peel=2):
    body = 2 * units
    turns = tiles // 2
    for p in range(peel):
        for j in range(body):
            step(At(p, j, units))
    with eng.Fori(peel, turns - 1) as p:
        for j in range(body):
            step(At(p, j, units))
    for j in range(body + tail):
        step(At(turns - 1, j, units))


def wait(eng, sem, value):
    if isinstance(value, int):
        if value <= 0:
            return
    else:
        assert value.min_val > 0, "a wait in a loop has to be on a count above zero"
    eng.wait_ge(sem, value)


class Chain:

    def __init__(self, sem):
        self.sem, self.n = sem, 0

    def link(self, eng, ins):
        ins.then_inc(self.sem, 1)
        self.n += 1
        eng.wait_ge(self.sem, self.n)


def bc(ap, shape):
    return ap.broadcast_to(shape)


def build(nc, A, out):
    es = ExitStack()
    with es:
        def sb(name, shape, dt=F32):
            return es.enter_context(nc.sbuf_tensor(name, shape, dt))

        held = []

        def sems(st, prefix, names):
            got = {x: nc.alloc_semaphore(prefix + x) for x in names.split()}
            held.extend(got.values())
            return got

        def clear_semaphores():
            nc.clear_and_free_semaphores(held)
            nc.all_engine_barrier()
            held.clear()

        W = sb("W", [P, WCOLS])
        R = sb("R", [P, RCOLS])
        X = sb("X", [P, TILES, D])
        XnT = sb("XnT", [D, TILES * P])
        ctx = sb("ctx", [KEYS, B, D])
        ctxT = sb("ctxT", [D, B, KEYS])
        nhalf = sb("nhalf", [P, TILES])

        def w(name, lo=0, n=None):
            o, width = OFF[name]
            return W[:, o + lo:o + (lo + n if n is not None else width)]

        def row(name, lo=0, n=None):
            o, width = ROFF[name]
            return R[:, o + lo:o + (lo + n if n is not None else width)]

        ident = w("ident")

        psS = [es.enter_context(nc.psum_tensor(f"scores{i}", [P, UCOL], F32)) for i in range(2)]
        psT = es.enter_context(nc.psum_tensor("probsT", [P, UCOL], F32))
        psO = es.enter_context(nc.psum_tensor("mixed", [P, 512], F32))
        psM = es.enter_context(nc.psum_tensor("misc", [P, 512], F32))

        def dram(name, shape, dt=F32):
            return nc.dram_tensor(name, shape, dt, kind="Internal").ap()

        shared = dict(nc=nc, A=A, out=out, es=es, sb=sb, sems=sems, W=W, R=R, X=X, XnT=XnT, ctx=ctx, ctxT=ctxT, nhalf=nhalf, w=w, row=row,
                     ident=ident, psS=psS, psT=psT, psO=psO, psM=psM, dram=dram)
        K = type("K", (), shared)
        load(K)
        stages = [stage_cross_wide, stage_linear, stage_mlp, stage_expert_attention, stage_cross_masked,
                  stage_relative, stage_causal, stage_moe]
        for f in stages:
            f(K)
            if f in (stage_mlp, stage_relative):
                clear_semaphores()


def load(K):
    nc = K.nc
    K.load = K.sems(K.es, "load_", "x weights first rest const")
    s = K.load
    with nc.Block() as block:
        @block.sync
        def _(sp):
            sp.dma_start(K.X[:, :, :], K.A["x"].rearrange("t p d -> p t d")).then_inc(s["x"], 16)
            sp.dma_start(K.W[:, 0:P], K.A["wpack"][:, 0:P]).then_inc(s["x"], 16)
            sp.dma_start(K.W[:, P:EARLY], K.A["wpack"][:, P:EARLY]).then_inc(s["weights"], 16)
            sp.dma_start(K.ctxT[:, :, :], K.A["ctxT"].rearrange("b d k -> d b k")).then_inc(s["first"], 16)
            sp.dma_start(K.ctx[:, :, :], K.A["ctx"].rearrange("b k d -> k b d")).then_inc(s["first"], 16)
            sp.dma_start(K.R[:, :], K.A["rpack"].partition_broadcast(P)).then_inc(s["first"], 16)
            sp.dma_start(K.W[:, EARLY:], K.A["wpack"][:, EARLY:]).then_inc(s["rest"], 16)
            sp.wait_ge(s["x"], 32)

        @block.gpsimd
        def _(pool):
            pool.memset(K.nhalf[:, :], -0.5).then_inc(s["const"], 1)
            pool.wait_ge(s["const"], 1)


def norm_stats(dve, stats, st6, mv, src, groups, var_ready):
    for t in range(TILES):
        last = dve.bn_stats(st6[:, t, :], src[:, t, :])
    last.then_inc(stats, 1)
    dve.wait_ge(stats, 1)
    for t in range(TILES):
        last = dve.bn_aggr(mv[:, t, :], st6[:, t, :])
        if (t + 1) % (TILES // groups) == 0:
            last.then_inc(var_ready, 1)


def layer_norm(K, tag, router=None, keep=None, src=None, affine=None):
    nc = K.nc
    G = 4
    groups = TILES // G
    src = K.X if src is None else src
    with ExitStack() as st:
        s = K.sems(st, tag, "stats scaled var vareps rstd normed turned copied logits logitsout xT")
        sb = lambda n, sh: st.enter_context(nc.sbuf_tensor(tag + n, sh, F32))
        st6, mv, rstd = sb("st6", [P, TILES, 6]), sb("mv", [P, TILES, 2]), sb("rstd", [P, TILES])
        xn = sb("xn", [P, TILES, D]) if keep is None else keep
        xT = sb("xT", [P, 2, G * P])
        with nc.Block() as block:
            @block.vector
            def _(dve):
                def logits(g):
                    dve.wait_ge(s["logits"], g + 1)
                    dve.tensor_copy(router[2][:, g * G:(g + 1) * G, :],
                                    K.psO[:, 0:G * router[1]].rearrange("p (g e) -> p g e", g=G)).then_inc(s["logitsout"], 1)

                norm_stats(dve, s["stats"], st6, mv, src, groups, s["var"])
                for g in range(groups):
                    dve.wait_ge(s["rstd"], g + 1)
                    for t in range(g * G, (g + 1) * G):
                        last = dve.tensor_scalar(xn[:, t, :], src[:, t, :], mv[:, t, 0:1], rstd[:, t:t + 1],
                                                 ALU.subtract, ALU.mult)
                    if affine is not None:
                        rows = xn[:, g * G:(g + 1) * G, :]
                        for i, (op, v) in enumerate(((ALU.mult, affine[0]), (ALU.add, affine[1]))):
                            last.then_inc(s["scaled"], 1)
                            dve.wait_ge(s["scaled"], 2 * g + i + 1)
                            last = dve.tensor_tensor(rows, rows, bc(K.row(v).unsqueeze(1), [P, G, D]), op)
                    last.then_inc(s["normed"], 1)
                    if router is not None and g:
                        logits(g - 1)
                if router is not None:
                    logits(groups - 1)

            @block.tensor
            def _(pe):
                for g in range(groups):
                    pe.wait_ge(s["normed"], g + 1)
                    wait(pe, s["copied"], g - 1)
                    for i in range(G):
                        last = pe.transpose(K.psS[g % 2][:, i * P:(i + 1) * P], xn[:, g * G + i, :], K.ident)
                    last.then_inc(s["turned"], 1)
                    if router is not None:
                        pe.wait_ge(s["xT"], g + 1)
                        wait(pe, s["logitsout"], g)
                        for i in range(G):
                            last = pe.matmul(K.psO[:, i * router[1]:(i + 1) * router[1]], xT[:, g % 2, i * P:(i + 1) * P],
                                             router[0], start=True, stop=True)
                        last.then_inc(s["logits"], 1)

            @block.scalar
            def _(act):
                for g in range(groups):
                    act.wait_ge(s["turned"], g + 1)
                    if router is not None:
                        wait(act, s["logits"], g - 1)
                        act.copy(xT[:, g % 2, :], K.psS[g % 2][:, 0:G * P]).then_inc(s["xT"], 1)
                    act.copy(K.XnT[:, g * G * P:(g + 1) * G * P], K.psS[g % 2][:, 0:G * P]).then_inc(s["copied"], 1)

            @block.gpsimd
            def _(pool):
                for g in range(groups):
                    tiles = slice(g * G, (g + 1) * G)
                    pool.wait_ge(s["var"], g + 1)
                    pool.tensor_scalar(rstd[:, tiles], mv[:, tiles, 1], LN_EPS, None, ALU.add).then_inc(s["vareps"], 1)
                    pool.wait_ge(s["vareps"], g + 1)
                    pool.tensor_tensor(rstd[:, tiles], rstd[:, tiles], K.nhalf[:, tiles], ALU.pow).then_inc(s["rstd"], 1)


UNIT_SEMS = "scored maxed shifted exped turned tcopied mixed recip normed "


class Attention:

    def __init__(self, K, st, s, tag, total, keys, scale, cols=UCOL):
        self.K, self.s, self.total, self.keys, self.scale, self.cols = K, s, total, keys, scale, cols
        self.groups = cols // keys
        nc = K.nc
        self.P = st.enter_context(nc.sbuf_tensor(tag + "P", [P, 2, cols], F32))
        self.PT = st.enter_context(nc.sbuf_tensor(tag + "PT", [P, 2, cols], F32))
        self.mx = st.enter_context(nc.sbuf_tensor(tag + "mx", [P, 2, self.groups], F32))
        self.banks = (cols + 511) // 512

    def scores_free(self, pe, a):
        wait(pe, self.s["shifted" if self.bias is None else "biased"], a.n - 1)

    def shift(self, dve, a):
        if not a.inside(self.total):
            return
        s, g = self.s, self.groups
        sc = self.K.psS[a.up][:, 0:self.cols].rearrange("p (g k) -> p g k", g=g)
        pr = self.P[:, a.up, :].rearrange("p (g k) -> p g k", g=g)
        mx = self.mx[:, a.up, :]
        top = bc(mx.unsqueeze(2), [P, g, self.keys])
        dve.wait_ge(s["scored"], a.n + 1)
        if self.bias is not None:
            wait(dve, s["turned"], (a.n - 1) * self.banks)
            self.bias(dve, a, pr, sc).then_inc(s["biased"], 1)
            dve.wait_ge(s["biased"], a.n + 1)
            sc = pr
        wait(dve, s["shifted"], a.n - 1)
        dve.tensor_reduce(mx, sc, AX.X, ALU.max).then_inc(s["maxed"], 1)
        if self.bias is None:
            wait(dve, s["turned"], (a.n - 1) * self.banks)
        dve.wait_ge(s["maxed"], a.n + 1)
        dve.tensor_tensor(pr, sc, top, ALU.subtract).then_inc(s["shifted"], 1)

    def exp(self, act, a):
        if not a.inside(self.total):
            return
        act.wait_ge(self.s["shifted"], a.n + 1)
        act.activation(self.P[:, a.up, :], self.P[:, a.up, :], ACT.Exp, scale=self.scale).then_inc(self.s["exped"], 1)

    def turn(self, pe, a):
        if not a.inside(self.total):
            return
        pe.wait_ge(self.s["exped"], a.n + 1)
        for b in range(self.banks):
            wait(pe, self.s["tcopied"], (a.n - 1) * self.banks + b + 1)
            for c in range(4):
                i = 4 * b + c
                last = pe.transpose(self.K.psT[:, i * P:(i + 1) * P], self.P[:, a.up, i * P:(i + 1) * P], self.K.ident)
            last.then_inc(self.s["turned"], 1)

    def tcopy(self, act, a):
        if not a.inside(self.total):
            return
        for b in range(self.banks):
            act.wait_ge(self.s["turned"], a.n * self.banks + b + 1)
            wait(act, self.s[self.reader[0]], (a.n - 1) * self.reader[1])
            act.copy(self.PT[:, a.up, b * 512:(b + 1) * 512], self.K.psT[:, b * 512:(b + 1) * 512]).then_inc(
                self.s["tcopied"], 1)

    bias = None
    reader = "mixed", 1


def stage_cross_wide(K):
    layer_norm(K, "n1_")
    nc, w = K.nc, K.w
    with ExitStack() as st:
        s = K.sems(st, "c1_", UNIT_SEMS + "chain cin pre preout gt gtout read rtout scaled y yout xin")
        sb = lambda n, sh, dt=F32: st.enter_context(nc.sbuf_tensor("c1_" + n, sh, dt))
        AQ = sb("AQ", [P, HEADS, D])
        VO = sb("VO", [P, HEADS, D])
        xs = sb("xs", [P, 2, P])
        GT = sb("GT", [P, 2, TB, HEADS, S])
        cs = sb("cs", [KEYS, 2, D])
        RT = sb("RT", [D, 2, HEADS, P])
        rl = sb("rl", [P, 2, PAIRS])
        yb = sb("yb", [P, 2, D])
        U, TOTAL = TB, TILES * TB
        at = Attention(K, st, s, "c1_", TOTAL, KEYS, 1.0 / DK ** 0.5)
        M = K.psM
        at.reader = "read", 2
        ahead = [K.psM, K.psO]
        PRE = 8

        def weight_products():
            for left, right, dst in (("WQT", "WKT", AQ), ("WVT", "WO", VO)):
                for r in range(2):
                    for hh in range(2):
                        yield left, right, dst, r, hh

        with nc.Block() as block:
            @block.sync
            def _(sp):
                sp.wait_ge(K.load["rest"], 16)

            @block.gpsimd
            def _(pool):
                def tile_in(a):
                    if not a.inside(TOTAL):
                        return
                    wait(pool, s["gt"], 4 * (a.t - 1))
                    pool.tensor_copy(xs[:, a.par, :], K.XnT[:, bass.ds(a.t * P, P)]).then_inc(s["xin"], 1)

                def context(a):
                    if not a.inside(TOTAL):
                        return
                    wait(pool, s["read"], 2 * (a.n - 1))
                    pool.tensor_copy(cs[:, a.up, :], K.ctx[:, a.n, :]).then_inc(s["cin"], 1)

                def scale(a):
                    if not a.inside(TOTAL):
                        return
                    pool.wait_ge(s["recip"], a.n + 1)
                    pr = at.P[:, a.up, :].rearrange("p (g k) -> p g k", g=PAIRS)
                    pool.tensor_tensor(pr, pr, bc(rl[:, a.up, :].unsqueeze(2), [P, PAIRS, KEYS]), ALU.mult).then_inc(
                        s["scaled"], 1)

                def step(a):
                    if a.u == 0:
                        tile_in(a.plus(2 * U))
                    context(a.plus(1))
                    scale(a.plus(1))

                pool.wait_ge(K.load["first"], 48)
                first = At(0, 0, U)
                tile_in(first)
                tile_in(first.plus(U))
                context(first)
                scale(first)
                run_units(pool, U, TILES, step, 0)

            @block.tensor
            def _(pe):
                pe.wait_ge(K.load["weights"], 16)
                for i, (left, right, _, r, hh) in enumerate(weight_products()):
                    wait(pe, s["preout"], i - 1)
                    for c in range(4):
                        rows = slice(hh * 64, hh * 64 + 64)
                        last = pe.matmul(K.psS[hh][:, c * P:(c + 1) * P], w(left, (4 * r + c) * P, P)[rows, :],
                                         w(right, (4 * r + c) * P, P)[rows, :], start=True, stop=True)
                    last.then_inc(s["pre"], 1)
                pe.wait_ge(s["preout"], PRE)
                pe.wait_ge(K.load["first"], 48)

                def gt(a, r, bank=M, banks=1):
                    if not a.inside(TOTAL):
                        return
                    pe.wait_ge(s["xin"], a.t + 1)
                    wait(pe, s["gtout"], 4 * a.t + r - (banks - 1))
                    for h in range(4 * r, 4 * r + 4):
                        last = pe.matmul(bank[:, (h % 4) * P:(h % 4 + 1) * P], AQ[:, h, :], xs[:, a.par, :],
                                         start=True, stop=True)
                    last.then_inc(s["gt"], 1)

                def score(a):
                    if not a.inside(TOTAL):
                        return
                    at.scores_free(pe, a)
                    pe.wait_ge(s["gtout"], 4 * (a.t + 1))
                    for c in range(PAIRS):
                        last = pe.matmul(K.psS[a.up][:, c * KEYS:(c + 1) * KEYS],
                                         GT[:, a.par, a.u, 2 * c:2 * c + 2, :].rearrange("p h q -> p (h q)"),
                                         K.ctxT[:, a.n, :], start=True, stop=True)
                    last.then_inc(s["scored"], 1)

                def read(a, r):
                    if not a.inside(TOTAL):
                        return
                    pe.wait_ge(s["tcopied"], 2 * a.n + r + 1)
                    pe.wait_ge(s["cin"], a.n + 1)
                    wait(pe, s["rtout"], 2 * a.n + r)
                    if a.u == 1 and r == 0:
                        wait(pe, s["yout"], a.t)
                    pe.matmul(K.psO[:, :], cs[:, a.up, :], at.PT[:, a.up, r * 512:(r + 1) * 512], start=True,
                              stop=True).then_inc(s["read"], 1)

                def outputs(a):
                    if not a.inside(TOTAL):
                        return
                    after = 4 * a.t + 6
                    pe.wait_ge(s["rtout"], after if not isinstance(after, int) else min(after, 4 * TILES))
                    for h in range(HEADS):
                        last = pe.matmul(K.psO[:, 0:D], RT[:, a.par, h, :], VO[:, h, :], start=(h == 0), stop=(h == HEADS - 1))
                    last.then_inc(s["y"], 1)

                def step(a):
                    nt, p1 = a.plus(3), a.plus(-1)
                    score(a.plus(1))
                    read(p1, 0)
                    gt(nt, 2 * nt.u)
                    read(p1, 1)
                    gt(nt, 2 * nt.u + 1)
                    if a.u == 1:
                        outputs(a.plus(-2))
                    if a.inside(TOTAL):
                        pe.wait_ge(s["scaled"], a.n + 1)
                    at.turn(pe, a)

                first = At(0, 0, U)
                for i in range(6):
                    gt(first if i < 4 else first.plus(U), i % 4, ahead[i % 2], 2)
                score(first)
                run_units(pe, U, TILES, step, 2)

            @block.scalar
            def _(act):
                for i, (_, _, dst, r, hh) in enumerate(weight_products()):
                    act.wait_ge(s["pre"], i + 1)
                    act.copy(dst[:, bass.ds(8 * r + hh, 4, 2), :],
                             K.psS[hh][:, 0:512].rearrange("p (c d) -> p c d", c=4)).then_inc(s["preout"], 1)

                def gt(a, r, bank=M):
                    if not a.inside(TOTAL):
                        return
                    act.wait_ge(s["gt"], 4 * a.t + r + 1)
                    wait(act, s["scored"], 2 * (a.t - 1))
                    for b in range(TB):
                        last = act.copy(GT[:, a.par, b, 4 * r:4 * r + 4, :],
                                        bank[:, :].rearrange("p (h b q) -> p h b q", h=4, b=TB)[:, :, b, :])
                    last.then_inc(s["gtout"], 1)

                def read(a, r):
                    if not a.inside(TOTAL):
                        return
                    act.wait_ge(s["read"], 2 * a.n + r + 1)
                    wait(act, s["y"], a.t - 1)
                    act.copy(RT[:, a.par, 8 * r:8 * r + 8, a.u * S:(a.u + 1) * S],
                             K.psO[:, :].rearrange("p (h q) -> p h q", h=8)).then_inc(s["rtout"], 1)

                def step(a):
                    p1, nt = a.plus(-1), a.plus(3)
                    at.tcopy(act, p1)
                    read(p1, 0)
                    gt(nt, 2 * nt.u)
                    read(p1, 1)
                    gt(nt, 2 * nt.u + 1)
                    at.exp(act, a.plus(1))

                first = At(0, 0, U)
                for i in range(6):
                    gt(first if i < 4 else first.plus(U), i % 4, ahead[i % 2])
                at.exp(act, first)
                run_units(act, U, TILES, step, 1)

            @block.vector
            def _(dve):
                def sums(a):
                    if not a.inside(TOTAL):
                        return
                    dve.wait_ge(s["exped"], a.n + 1)
                    wait(dve, s["scaled"], a.n - 1)
                    dve.tensor_reduce(rl[:, a.up, :], at.P[:, a.up, :].rearrange("p (g k) -> p g k", g=PAIRS),
                                      AX.X, ALU.add).then_inc(s["chain"], 1)
                    dve.wait_ge(s["chain"], a.n + 1)
                    dve.reciprocal(rl[:, a.up, :], rl[:, a.up, :]).then_inc(s["recip"], 1)

                def finish(a):
                    if not a.inside(TOTAL):
                        return
                    dve.wait_ge(s["y"], a.t + 1)
                    dve.tensor_tensor(yb[:, a.par, :], K.psO[:, 0:D], K.row("bO"), ALU.add).then_inc(s["yout"], 1)
                    dve.wait_ge(s["yout"], a.t + 1)
                    dve.tensor_tensor(K.X[:, a.t, :], K.X[:, a.t, :], yb[:, a.par, :], ALU.add)

                def step(a):
                    at.shift(dve, a.plus(1))
                    sums(a.plus(1))
                    if a.u == 1:
                        finish(a.plus(-2))

                dve.wait_ge(K.load["first"], 48)
                first = At(0, 0, U)
                at.shift(dve, first)
                sums(first)
                run_units(dve, U, TILES, step, 2)


def bank_views(K):
    return [K.psS[0][:, 0:512], K.psS[0][:, 512:1024], K.psS[1][:, 0:512], K.psS[1][:, 512:1024],
            K.psT[:, 0:512], K.psT[:, 512:1024], K.psO[:, :], K.psM[:, :]]


def stage_linear(K):
    nc, w, row = K.nc, K.w, K.row
    G, GROUPS = 2, TILES // 2
    N = G * P
    K.Xmid = K.es.enter_context(nc.sbuf_tensor("Xmid", [P, TILES, D], F32))
    with ExitStack() as st:
        s = K.sems(st, "l2_", "weights chain var scaled rs xn turned xnT q kv squared phi v kvm KV num rden rdenok o oT oTc y "
                              "ya yg xm")
        sb = lambda n, sh, dt=F32: st.enter_context(nc.sbuf_tensor("l2_" + n, sh, dt))
        Wqkv = sb("Wqkv", [D, 3 * D])
        st6, mv = sb("st6", [P, 2, G, 6]), sb("mv", [P, 2, G, 2])
        rs = sb("rs", [P, 2, 2, G])
        xn = sb("xn", [P, 2, G, D])
        xnT, sqq, sqk = sb("xnT", [D, 2, N]), sb("sqq", [D, N]), sb("sqk", [P, G, D])
        phq, phk = sb("phq", [D, 2, N]), sb("phk", [P, 2, G, D])
        vb = sb("vb", [P, 2, G, TB * D + TB])
        KV = sb("KV", [P, 2, G, TB, D + HEADS])
        den, o, oT = sb("den", [P, G, HEADS]), sb("o", [P, 2, G, D]), sb("oT", [D, 2, N])
        ya = sb("ya", [P, 2, G, D])
        pT, pQ, pKV, pS0, pS1, pN, pO, pY = bank_views(K)
        inside = lambda a: a.inside(GROUPS)

        with nc.Block() as block:
            @block.vector
            def _(dve):
                ch = Chain(s["chain"])
                dve.tensor_scalar(Wqkv[:, :], w("qkvT"), w("scale1"), None, ALU.mult).then_inc(s["weights"], 1)
                ch.link(dve, dve.memset(vb[:, :, :, :], 0.0))
                for b in range(TB):
                    dve.memset(vb[64 * b:64 * b + 64, :, :, TB * D + b:TB * D + b + 1], 1.0).then_inc(s["weights"], 1)

                def stats(a):
                    if not inside(a):
                        return
                    wait(dve, s["var"], a.n - 1)
                    for i in range(G):
                        dve.bn_stats(st6[:, a.par, i, :], K.X[:, a.n * G + i, :]).then_inc(s["chain"], 1)
                    dve.wait_ge(s["chain"], 1 + G * (a.n + 1))
                    wait(dve, s["xn"], a.n - 1)
                    wait(dve, s["rs"], a.n - 1)
                    for i in range(G):
                        last = dve.bn_aggr(mv[:, a.par, i, :], st6[:, a.par, i, :])
                    last.then_inc(s["var"], 1)

                def xnorm(a):
                    if not inside(a):
                        return
                    dve.wait_ge(s["rs"], a.n + 1)
                    dve.wait_ge(s["var"], a.n + 1)
                    wait(dve, s["turned"], a.n - 1)
                    for i in range(G):
                        mean, row_in = mv[:, a.par, i, 0:1], K.X[:, a.n * G + i, :]
                        dve.tensor_scalar(K.Xmid[:, a.n * G + i, :], row_in, mean, rs[:, a.par, 0, i:i + 1],
                                          ALU.subtract, ALU.mult)
                        last = dve.tensor_scalar(xn[:, a.par, i, :], row_in, mean, rs[:, a.par, 1, i:i + 1],
                                                 ALU.subtract, ALU.mult)
                    last.then_inc(s["xn"], 1)

                def mask(a):
                    if not inside(a):
                        return
                    dve.wait_ge(s["KV"], a.n + 1)
                    wait(dve, s["num"], a.n - 1)
                    for i, ps in enumerate((pS0, pS1)):
                        dve.tensor_tensor(KV[:, a.par, i, :, 0:D].rearrange("p b (h e) -> p b h e", h=HEADS),
                                          ps[:, 0:TB * D].rearrange("p (b h e) -> p b h e", b=TB, h=HEADS),
                                          bc(w("headmask").unsqueeze(1).unsqueeze(3), [P, TB, HEADS, HD]), ALU.mult)
                        for b in range(TB):
                            last = dve.tensor_scalar(KV[:, a.par, i, b, D:], w("headmask"),
                                                     ps[:, TB * D + b:TB * D + b + 1], None, ALU.mult)
                    last.then_inc(s["kvm"], 1)

                def values(a):
                    if not inside(a):
                        return
                    dve.wait_ge(s["kv"], a.n + 1)
                    wait(dve, s["KV"], a.n - 1)
                    for b in range(TB):
                        last = dve.tensor_copy(vb[64 * b:64 * b + 64, a.par, :, b * D:(b + 1) * D],
                                               pKV[64 * b:64 * b + 64, :].rearrange("p (i c) -> p i c", i=G)[:, :, D:])
                    last.then_inc(s["v"], 1)

                def divide(a):
                    if not inside(a):
                        return
                    dve.wait_ge(s["num"], a.n + 1)
                    wait(dve, s["o"], a.n)
                    ps = pN[:, 0:G * (D + HEADS)].rearrange("p (i c) -> p i c", i=G)
                    dve.tensor_scalar(den[:, :, :], ps[:, :, D:], 1e-6, None, ALU.add).then_inc(s["rden"], 1)
                    dve.wait_ge(s["rden"], a.n + 1)
                    dve.reciprocal(den[:, :, :], den[:, :, :]).then_inc(s["rdenok"], 1)
                    dve.wait_ge(s["rdenok"], a.n + 1)
                    wait(dve, s["oT"], a.n - 1)
                    for i in range(G):
                        last = dve.tensor_tensor(o[:, a.par, i, :].rearrange("p (h e) -> p h e", h=HEADS),
                                                 ps[:, i, 0:D].rearrange("p (h e) -> p h e", h=HEADS),
                                                 bc(den[:, i, :].unsqueeze(2), [P, HEADS, HD]), ALU.mult)
                    last.then_inc(s["o"], 1)

                def bias(a):
                    if not inside(a):
                        return
                    dve.wait_ge(s["y"], a.n + 1)
                    wait(dve, s["xm"], a.n - 1)
                    dve.tensor_tensor(ya[:, a.par, :, :], pY[:, 0:N].rearrange("p (i d) -> p i d", i=G),
                                      bc(row("proj_b").unsqueeze(1), [P, G, D]), ALU.add).then_inc(s["ya"], 1)

                def step(a):
                    mask(a.plus(-1))
                    xnorm(a.plus(1))
                    values(a)
                    stats(a.plus(2))
                    divide(a.plus(-1))
                    bias(a.plus(-2))

                first = At(0, 0, 1)
                stats(first)
                stats(first.plus(1))
                xnorm(first)
                run_units(dve, 1, GROUPS, step, 2)

            @block.gpsimd
            def _(pool):
                def scales(a):
                    if not inside(a):
                        return
                    pool.wait_ge(s["var"], a.n + 1)
                    wait(pool, s["xn"], a.n - 1)
                    var, rsa = mv[:, a.par, :, 1], rs[:, a.par, :, :]
                    pool.tensor_scalar(rsa[:, 0, :], var, LN_EPS, None, ALU.add)
                    pool.tensor_scalar(rsa[:, 1, :], var, D / RMS_NUM ** 2, None, ALU.mult).then_inc(s["scaled"], 1)
                    pool.wait_ge(s["scaled"], a.n + 1)
                    pool.tensor_tensor(rsa, rsa, K.nhalf[:, 0:2 * G].rearrange("p (a b) -> p a b", a=2),
                                       ALU.pow).then_inc(s["rs"], 1)

                def mid(a):
                    if not inside(a):
                        return
                    pool.wait_ge(s["ya"], a.n + 1)
                    y = ya[:, a.par, :, :]
                    pool.tensor_tensor(y, y, bc(row("gamma").unsqueeze(1), [P, G, D]), ALU.mult).then_inc(s["yg"], 1)
                    pool.wait_ge(s["yg"], a.n + 1)
                    xl = K.Xmid[:, bass.ds(a.n * G, G), :]
                    pool.tensor_tensor(xl, xl, y, ALU.add).then_inc(s["xm"], 1)

                def step(a):
                    scales(a.plus(2))
                    mid(a.plus(-2))

                first = At(0, 0, 1)
                scales(first)
                scales(first.plus(1))
                run_units(pool, 1, GROUPS, step, 2)

            @block.scalar
            def _(act):
                def xT(a):
                    if not inside(a):
                        return
                    act.wait_ge(s["turned"], a.n + 1)
                    wait(act, s["kv"], a.n - 1)
                    act.copy(xnT[:, a.par, :], pT[:, 0:N]).then_inc(s["xnT"], 1)

                def outT(a):
                    if not inside(a):
                        return
                    act.wait_ge(s["oT"], a.n + 1)
                    wait(act, s["y"], a.n - 1)
                    act.copy(oT[:, a.par, :], pO[:, 0:N]).then_inc(s["oTc"], 1)

                def phi(a):
                    if not inside(a):
                        return
                    act.wait_ge(s["q"], a.n + 1)
                    wait(act, s["phi"], a.n)
                    act.activation(sqq[:, :], pQ[:, 0:N], ACT.Square)
                    act.wait_ge(s["v"], a.n + 1)
                    act.activation(sqk[:, :, :], pKV[:, :].rearrange("p (i c) -> p i c", i=G)[:, :, 0:D],
                                   ACT.Square).then_inc(s["squared"], 1)
                    act.wait_ge(s["squared"], a.n + 1)
                    wait(act, s["num"], a.n - 1)
                    act.activation(phq[:, a.par, :], sqq[:, :], ACT.Exp, scale=-0.5)
                    act.activation(phk[:, a.par, :, :], sqk[:, :, :], ACT.Exp, scale=-0.5).then_inc(s["phi"], 1)

                def step(a):
                    outT(a.plus(-2))
                    phi(a)
                    xT(a.plus(1))

                xT(At(0, 0, 1))
                run_units(act, 1, GROUPS, step, 2)

            @block.tensor
            def _(pe):
                def turn(a):
                    if not inside(a):
                        return
                    pe.wait_ge(s["xn"], a.n + 1)
                    wait(pe, s["xnT"], a.n)
                    for i in range(G):
                        last = pe.transpose(pT[:, i * P:(i + 1) * P], xn[:, a.par, i, :], K.ident)
                    last.then_inc(s["turned"], 1)

                def sums(a):
                    if not inside(a):
                        return
                    pe.wait_ge(s["phi"], a.n + 1)
                    pe.wait_ge(s["v"], a.n + 1)
                    wait(pe, s["kvm"], a.n)
                    for i, ps in enumerate((pS0, pS1)):
                        last = pe.matmul(ps[:, 0:TB * D + TB], phk[:, a.par, i, :], vb[:, a.par, i, :], start=True, stop=True)
                    last.then_inc(s["KV"], 1)

                def oturn(a):
                    if not inside(a):
                        return
                    pe.wait_ge(s["o"], a.n + 1)
                    wait(pe, s["oTc"], a.n)
                    for i in range(G):
                        last = pe.transpose(pO[:, i * P:(i + 1) * P], o[:, a.par, i, :], K.ident)
                    last.then_inc(s["oT"], 1)

                def qkv(a):
                    if not inside(a):
                        return
                    pe.wait_ge(s["xnT"], a.n + 1)
                    wait(pe, s["phi"], a.n)
                    wait(pe, s["v"], a.n)
                    pe.matmul(pQ[:, 0:N], Wqkv[:, 0:D], xnT[:, a.par, :], start=True, stop=True).then_inc(s["q"], 1)
                    for i in range(G):
                        last = pe.matmul(pKV[:, i * 2 * D:(i + 1) * 2 * D], xnT[:, a.par, i * P:(i + 1) * P],
                                         Wqkv[:, D:], start=True, stop=True)
                    last.then_inc(s["kv"], 1)

                def numer(a):
                    if not inside(a):
                        return
                    pe.wait_ge(s["kvm"], a.n + 1)
                    wait(pe, s["o"], a.n)
                    c = D + HEADS
                    for i in range(G):
                        for b in range(TB):
                            last = pe.matmul(pN[64 * b:64 * b + 64, i * c:(i + 1) * c],
                                             phq[:, a.par, i * P + 64 * b:i * P + 64 * b + 64],
                                             KV[:, a.par, i, b, :], start=True, stop=True)
                    last.then_inc(s["num"], 1)

                def proj(a):
                    if not inside(a):
                        return
                    pe.wait_ge(s["oTc"], a.n + 1)
                    wait(pe, s["ya"], a.n)
                    for i in range(G):
                        last = pe.matmul(pY[:, i * D:(i + 1) * D], oT[:, a.par, i * P:(i + 1) * P], w("projT"),
                                         start=True, stop=True)
                    last.then_inc(s["y"], 1)

                def step(a):
                    sums(a.plus(-1))
                    oturn(a.plus(-2))
                    qkv(a)
                    turn(a.plus(1))
                    numer(a.plus(-1))
                    proj(a.plus(-2))

                pe.wait_ge(s["weights"], 3)
                turn(At(0, 0, 1))
                run_units(pe, 1, GROUPS, step, 2)


def stage_mlp(K):
    nc, w, row = K.nc, K.w, K.row
    G, GROUPS = 2, TILES // 2
    N = G * P
    with ExitStack() as st:
        s = K.sems(st, "m2_", "weights ss scaled rs xn turned xnT h gelu y ya yg ym")
        sb = lambda n, sh, dt=F32: st.enter_context(nc.sbuf_tensor("m2_" + n, sh, dt))
        W1 = sb("W1", [D, 2 * D])
        sq, ss, rs = sb("sq", [P, 2, G, D]), sb("ss", [P, 2, G]), sb("rs", [P, 2, G])
        xn, xnT, hT = sb("xn", [P, 2, G, D]), sb("xnT", [D, 2, N]), sb("hT", [P, 2, 2, N])
        ya = sb("ya", [P, 2, G, D])
        banks = bank_views(K)
        pT, pH, pY = banks[0:2], banks[2:4], banks[4:6]
        inside = lambda a: a.inside(GROUPS)

        with nc.Block() as block:
            @block.vector
            def _(dve):
                dve.tensor_scalar(W1[:, :], w("conv1T"), w("scale2"), None, ALU.mult).then_inc(s["weights"], 1)

                def squares(a):
                    if not inside(a):
                        return
                    wait(dve, s["scaled"], a.n - 1)
                    wait(dve, s["ss"], G * (a.n - 1))
                    for i in range(G):
                        x = K.Xmid[:, a.n * G + i, :]
                        dve.tensor_tensor_reduce(sq[:, a.par, i, :], x, x, 1.0, 0.0, ALU.mult, ALU.add,
                                                 ss[:, a.par, i:i + 1]).then_inc(s["ss"], 1)

                def xnorm(a):
                    if not inside(a):
                        return
                    dve.wait_ge(s["rs"], a.n + 1)
                    wait(dve, s["turned"], a.n - 1)
                    for i in range(G):
                        last = dve.tensor_scalar(xn[:, a.par, i, :], K.Xmid[:, a.n * G + i, :], rs[:, a.par, i:i + 1], None,
                                                 ALU.mult)
                    last.then_inc(s["xn"], 1)

                def bias(a):
                    if not inside(a):
                        return
                    dve.wait_ge(s["y"], a.n + 1)
                    wait(dve, s["ym"], a.n - 1)
                    dve.tensor_tensor(ya[:, a.par, :, :], pY[a.par][:, 0:N].rearrange("p (i d) -> p i d", i=G),
                                      bc(row("conv2_b").unsqueeze(1), [P, G, D]), ALU.add).then_inc(s["ya"], 1)

                def step(a):
                    xnorm(a.plus(1))
                    squares(a.plus(2))
                    bias(a.plus(-1))

                first = At(0, 0, 1)
                squares(first)
                squares(first.plus(1))
                xnorm(first)
                run_units(dve, 1, GROUPS, step, 1)

            @block.gpsimd
            def _(pool):
                def scales(a):
                    if not inside(a):
                        return
                    pool.wait_ge(s["ss"], G * (a.n + 1))
                    wait(pool, s["xn"], a.n - 1)
                    pool.tensor_scalar(rs[:, a.par, :], ss[:, a.par, :], 1.0 / RMS_NUM ** 2, None, ALU.mult).then_inc(s["scaled"], 1)
                    pool.wait_ge(s["scaled"], a.n + 1)
                    pool.tensor_tensor(rs[:, a.par, :], rs[:, a.par, :], K.nhalf[:, 0:G], ALU.pow).then_inc(s["rs"], 1)

                def residual(a):
                    if not inside(a):
                        return
                    pool.wait_ge(s["ya"], a.n + 1)
                    y = ya[:, a.par, :, :]
                    at = bass.ds(a.n * G, G)
                    pool.tensor_tensor(y, y, bc(row("gamma").unsqueeze(1), [P, G, D]), ALU.mult).then_inc(s["yg"], 1)
                    pool.tensor_tensor(K.X[:, at, :], K.X[:, at, :], K.Xmid[:, at, :], ALU.add).then_inc(s["yg"], 1)
                    pool.wait_ge(s["yg"], 2 * a.n + 2)
                    pool.tensor_tensor(K.X[:, at, :], K.X[:, at, :], y, ALU.add).then_inc(s["ym"], 1)

                def step(a):
                    scales(a.plus(2))
                    residual(a.plus(-1))

                first = At(0, 0, 1)
                scales(first)
                scales(first.plus(1))
                run_units(pool, 1, GROUPS, step, 1)

            @block.scalar
            def _(act):
                def xT(a):
                    if not inside(a):
                        return
                    act.wait_ge(s["turned"], a.n + 1)
                    wait(act, s["h"], 2 * (a.n - 1))
                    act.copy(xnT[:, a.par, :], pT[a.par][:, 0:N]).then_inc(s["xnT"], 1)

                def gelu(a):
                    if not inside(a):
                        return
                    wait(act, s["y"], a.n - 1)
                    for c in range(2):
                        act.wait_ge(s["h"], 2 * a.n + c + 1)
                        act.activation(hT[:, a.par, c, :], pH[c][:, 0:N], ACT.Gelu, bias=w("conv1_b", c, 1)).then_inc(s["gelu"], 1)

                def step(a):
                    gelu(a)
                    xT(a.plus(1))

                xT(At(0, 0, 1))
                run_units(act, 1, GROUPS, step, 0)

            @block.tensor
            def _(pe):
                def turn(a):
                    if not inside(a):
                        return
                    pe.wait_ge(s["xn"], a.n + 1)
                    wait(pe, s["xnT"], a.n - 1)
                    for i in range(G):
                        last = pe.transpose(pT[a.par][:, i * P:(i + 1) * P], xn[:, a.par, i, :], K.ident)
                    last.then_inc(s["turned"], 1)

                def up(a):
                    if not inside(a):
                        return
                    pe.wait_ge(s["xnT"], a.n + 1)
                    for c in range(2):
                        wait(pe, s["gelu"], 2 * (a.n - 1) + c + 1)
                        pe.matmul(pH[c][:, 0:N], W1[:, c * P:(c + 1) * P], xnT[:, a.par, :], start=True,
                                  stop=True).then_inc(s["h"], 1)

                def down(a):
                    if not inside(a):
                        return
                    pe.wait_ge(s["gelu"], 2 * (a.n + 1))
                    wait(pe, s["ya"], a.n - 1)
                    for i in range(G):
                        for c in range(2):
                            last = pe.matmul(pY[a.par][:, i * D:(i + 1) * D], hT[:, a.par, c, i * P:(i + 1) * P],
                                             w("conv2T", c * P, P), start=(c == 0), stop=(c == 1))
                    last.then_inc(s["y"], 1)

                def step(a):
                    down(a.plus(-1))
                    up(a)
                    turn(a.plus(1))

                pe.wait_ge(s["weights"], 1)
                turn(At(0, 0, 1))
                run_units(pe, 1, GROUPS, step, 1)


def rank_columns(dve, ch, rank, less, l, E):
    ch.link(dve, dve.memset(less[:, :, :, :], 0.0))
    shape = [P, TILES, E]
    for e in range(E):
        le = l[:, :, e:e + 1]
        if e + 1 < E:
            last = dve.tensor_tensor(less[:, :, e + 1:, e], l[:, :, e + 1:], bc(le, [P, TILES, E - e - 1]), ALU.is_le)
        if e:
            last = dve.tensor_tensor(less[:, :, 0:e, e], l[:, :, 0:e], bc(le, [P, TILES, e]), ALU.is_lt)
    ch.link(dve, last)
    ch.link(dve, dve.tensor_reduce(rank, less[:, :, :, :], AX.X, ALU.add))


def stage_expert_attention(K):
    nc, w, row = K.nc, K.w, K.row
    K.late = K.sems(K.es, "late_", "context")
    K.mask = K.es.enter_context(nc.sbuf_tensor("mask", [P, TILES, KEYS], I32))
    K.ctxS = K.es.enter_context(nc.sbuf_tensor("ctxS", [P, TILES, 2, KEYS], F32))
    with ExitStack() as keep:
        rt = lambda n, sh, dt=F32: keep.enter_context(nc.sbuf_tensor("e3_" + n, sh, dt))
        logits = rt("logits", [P, TILES, E0])
        layer_norm(K, "n3_", router=(w("rw"), E0, logits))
        wtok = rt("wtok", [P, TILES, E0])
        neg, batch = rt("neg", [TB, TILES * E0, S], BF16), rt("batch", [TB, P], BF16)

        with ExitStack() as st:
            s = K.sems(st, "r3_", "chain shifted exped negated turned copied stored row")
            sb = lambda n, sh, dt=F32: st.enter_context(nc.sbuf_tensor("r3_" + n, sh, dt))
            mx, ex, rank = sb("mx", [P, TILES]), sb("ex", [P, TILES, E0]), sb("rank", [P, TILES, E0])
            less, negm = sb("less", [P, TILES, E0, E0]), sb("negm", [P, TILES * E0])
            negT = sb("negT", [TILES * E0, P], BF16)
            scratch = K.dram("hbm_negT", (TB, TILES * E0, S), BF16)
            with nc.Block() as block:
                @block.vector
                def _(dve):
                    ch = Chain(s["chain"])
                    ch.link(dve, dve.tensor_tensor(logits[:, :, :], logits[:, :, :],
                                                   bc(row("rb").unsqueeze(1), [P, TILES, E0]), ALU.add))
                    ch.link(dve, dve.tensor_reduce(mx[:, :], logits[:, :, :], AX.X, ALU.max))
                    dve.tensor_tensor(ex[:, :, :], logits[:, :, :], bc(mx[:, :].unsqueeze(2), [P, TILES, E0]),
                                      ALU.subtract).then_inc(s["shifted"], 1)
                    rank_columns(dve, ch, rank[:, :, :], less, logits, E0)
                    ch.link(dve, dve.tensor_scalar(rank[:, :, :], rank[:, :, :], float(TOPK), None, ALU.is_lt))
                    dve.tensor_scalar(negm[:, :], rank[:, :, :].rearrange("p t e -> p (t e)"), 1.0, -NEG0, ALU.subtract,
                                      ALU.mult).then_inc(s["negated"], 1)
                    dve.wait_ge(s["exped"], 1)
                    ch.link(dve, dve.tensor_reduce(mx[:, :], ex[:, :, :], AX.X, ALU.add))
                    ch.link(dve, dve.reciprocal(mx[:, :], mx[:, :]))
                    ch.link(dve, dve.tensor_tensor(ex[:, :, :], ex[:, :, :], rank[:, :, :], ALU.mult))
                    ch.link(dve, dve.tensor_tensor(wtok[:, :, :], ex[:, :, :], bc(mx[:, :].unsqueeze(2), [P, TILES, E0]),
                                                   ALU.mult))

                @block.tensor
                def _(pe):
                    pe.wait_ge(s["negated"], 1)
                    pe.transpose(K.psM[0:TILES * E0, 0:P], negm[:, :], K.ident).then_inc(s["turned"], 1)

                @block.scalar
                def _(act):
                    act.wait_ge(s["shifted"], 1)
                    act.activation(ex[:, :, :], ex[:, :, :], ACT.Exp).then_inc(s["exped"], 1)
                    act.wait_ge(s["turned"], 1)
                    act.copy(negT[:, :], K.psM[0:TILES * E0, 0:P]).then_inc(s["copied"], 1)
                    act.copy(batch[:, :], w("batch")[0:TB, :])

                @block.sync
                def _(sp):
                    sp.wait_ge(s["copied"], 1)
                    sp.dma_start(scratch.rearrange("b r k -> r b k"), negT[:, :].rearrange("r (b k) -> r b k", b=TB)).then_inc(
                        s["stored"], 16)
                    sp.wait_ge(s["stored"], 16)
                    sp.dma_start(neg[:, :, :], scratch).then_inc(s["row"], 16)
                    sp.wait_ge(s["row"], 16)
                    sp.dma_start(K.mask[:, :, :], K.A["mask"].rearrange("t p k -> p t k")).then_inc(K.late["context"], 16)
                    sp.dma_start(K.ctxS[:, :, :, :], K.A["ctxS"]).then_inc(K.late["context"], 16)

        with ExitStack() as st:
            s = K.sems(st, "e3_", UNIT_SEMS + "init xin q qout k kout v vout kbd weighted oT oTc win wb ysum xsum")
            sb = lambda n, sh, dt=F32: st.enter_context(nc.sbuf_tensor("e3_" + n, sh, dt))
            U, TOTAL = E0, TILES * E0
            xs = sb("xs", [D, 2, P])
            LQ = sb("LQ", [P, 2, E0, 2, P])
            Ks = sb("Ks", [P, 2, E0, 2, S])
            RK = sb("RK", [P, 2, 2, 8, S])
            Vbd = sb("Vbd", [P, 2, E0, PAIRS, TB, 2, HD + 1])
            rl, o = sb("rl", [P, 2, PAIRS, 2]), sb("o", [P, 2, E0, D])
            oT, ya = sb("oT", [D, E0, P]), sb("ya", [P, D])
            ws = sb("ws", [P, E0])
            wb, yb = sb("wb", [P, E0, D]), sb("yb", [P, 2, D])
            at = Attention(K, st, s, "e3_", TOTAL, S, 0.5)
            M = K.psM

            with nc.Block() as block:
                @block.gpsimd
                def _(pool):
                    pool.memset(Vbd[:, :, :, :, :, :, :], 0.0).then_inc(s["init"], 1)
                    pool.memset(LQ[:, :, :, :, :], 0.0).then_inc(s["init"], 1)
                    pool.wait_ge(s["init"], 2)
                    for hh in range(2):
                        pool.memset(Vbd[64 * hh:64 * hh + 64, :, :, :, :, hh, HD].rearrange("p x e c b -> p (x e c b)"),
                                    1.0).then_inc(s["init"], 1)
                    pool.wait_ge(s["init"], 4)

                    def tile_in(a):
                        if not a.inside(TOTAL):
                            return
                        wait(pool, s["v"], a.t - 1)
                        pool.tensor_copy(xs[:, a.par, :], K.XnT[:, bass.ds(a.t * P, P)]).then_inc(s["xin"], 1)

                    def keys(a):
                        if not a.inside(TOTAL):
                            return
                        pool.wait_ge(s["kout"], a.t + 1)
                        wait(pool, s["scored"], a.n - 1)
                        pool.tensor_tensor(RK[:, a.up, :, :, :], bc(Ks[:, a.par, a.u, :, :].unsqueeze(2), [P, 2, 8, S]),
                                           bc(w("mask8").unsqueeze(1).unsqueeze(3), [P, 2, 8, S]), ALU.mult).then_inc(
                                               s["kbd"], 1)

                    def weights(a):
                        if not a.inside(TOTAL):
                            return
                        wait(pool, s["wb"], 3 * a.t)
                        pool.tensor_copy(ws[:, :], wtok[:, a.t, :]).then_inc(s["win"], 1)

                    def weigh(a):
                        if not a.inside(TOTAL):
                            return
                        pool.wait_ge(s["normed"], U * (a.t + 1))
                        pool.wait_ge(s["win"], a.t + 1)
                        ob = o[:, a.par, :, :]
                        pool.tensor_tensor(ob, ob, bc(ws[:, :].unsqueeze(2), [P, E0, D]), ALU.mult).then_inc(
                            s["weighted"], 1)

                    def biases(a):
                        if not a.inside(TOTAL):
                            return
                        pool.tensor_tensor(wb[:, :, :], row("bo").rearrange("p (e d) -> p e d", e=E0),
                                           bc(ws[:, :].unsqueeze(2), [P, E0, D]), ALU.mult).then_inc(s["wb"], 1)
                        pool.wait_ge(s["wb"], 3 * a.t + 1)
                        pool.tensor_tensor(wb[:, 0:2, :], wb[:, 0:2, :], wb[:, 2:4, :], ALU.add).then_inc(s["wb"], 1)
                        pool.wait_ge(s["wb"], 3 * a.t + 2)
                        wait(pool, s["ysum"], a.t - 1)
                        pool.tensor_tensor(yb[:, a.par, :], wb[:, 0, :], wb[:, 1, :], ALU.add).then_inc(s["wb"], 1)

                    def step(a):
                        if a.u == 0:
                            tile_in(a.plus(2 * U))
                            weights(a.plus(-U))
                        keys(a.plus(1))
                        if a.u == 1:
                            weigh(a.plus(-U))
                        if a.u == 2:
                            biases(a.plus(-U))

                    first = At(0, 0, U)
                    tile_in(first)
                    tile_in(first.plus(U))
                    keys(first)
                    run_units(pool, U, TILES, step, U)

                @block.tensor
                def _(pe):
                    def queries(a):
                        if not a.inside(TOTAL):
                            return
                        pe.wait_ge(s["xin"], a.t + 1)
                        wait(pe, s["oTc"], a.t - 2)
                        for e in range(E0):
                            last = pe.matmul(M[:, e * P:(e + 1) * P], w("wq", e * D, D), xs[:, a.par, :], start=True, stop=True)
                        last.then_inc(s["q"], 1)

                    def keys(a):
                        if not a.inside(TOTAL):
                            return
                        pe.wait_ge(s["qout"], a.t + 1)
                        for e in range(E0):
                            last = pe.matmul(M[:, e * P:(e + 1) * P], w("wk", e * D, D), xs[:, a.par, :], start=True, stop=True)
                        last.then_inc(s["k"], 1)

                    def values(a):
                        if not a.inside(TOTAL):
                            return
                        pe.wait_ge(s["kout"], a.t + 1)
                        pe.matmul(M[:, :], xs[:, a.par, :], w("wv"), start=True, stop=True).then_inc(s["v"], 1)

                    def score(a):
                        if not a.inside(TOTAL):
                            return
                        at.scores_free(pe, a)
                        pe.wait_ge(s["qout"], a.t + 1)
                        pe.wait_ge(s["kbd"], a.n + 1)
                        for half in range(2):
                            bank = K.psS[a.up][:, half * 512:(half + 1) * 512]
                            pe.matmul(bank.rearrange("p (h k) -> p h k", h=8), batch[:, :],
                                      bc(neg[:, a.t * E0 + a.u, :].unsqueeze(1), [TB, 8, S]), start=True, stop=False,
                                      skip_group_check=True)
                            last = pe.matmul(bank, LQ[:, a.par, a.u, half, :],
                                             RK[:, a.up, half, :, :].rearrange("p h k -> p (h k)"), start=False, stop=True,
                                             skip_group_check=True)
                        last.then_inc(s["scored"], 1)

                    def mix(a):
                        if a.inside(TOTAL):
                            pe.wait_ge(s["tcopied"], 2 * (a.n + 1))
                            pe.wait_ge(s["vout"], a.t + 1)
                            wait(pe, s["normed"], a.n)
                            for c in range(PAIRS):
                                last = pe.matmul(K.psO[:, c * 36:(c + 1) * 36], at.PT[:, a.up, c * P:(c + 1) * P],
                                                 Vbd[:, a.par, a.u, c, :, :, :], start=True, stop=True)
                        done = a.plus(-U)
                        if a.u == U - 1 and done.inside(TOTAL):
                            pe.wait_ge(s["oTc"], done.t + 1)
                            if not a.inside(TOTAL):
                                pe.wait_ge(s["normed"], TOTAL)
                            for e in range(E0):
                                last = pe.matmul(K.psO[:, 384:384 + D], oT[:, e, :], w("wo", e * D, D), start=(e == 0),
                                                 stop=(e == E0 - 1))
                            last.then_inc(s["mixed"], 1)
                        elif a.inside(TOTAL):
                            last.then_inc(s["mixed"], 1)

                    def oturn(a):
                        if not a.inside(TOTAL):
                            return
                        pe.wait_ge(s["weighted"], a.t + 1)
                        if not isinstance(a.t, int) or a.t + 2 < TILES:
                            pe.wait_ge(s["vout"], a.t + 3)
                        for e in range(E0):
                            last = pe.transpose(M[:, e * P:(e + 1) * P], o[:, a.par, e, :], K.ident)
                        last.then_inc(s["oT"], 1)

                    def step(a):
                        score(a.plus(1))
                        mix(a.plus(-1))
                        at.turn(pe, a)
                        if a.u == 0:
                            queries(a.plus(U))
                        if a.u == 1:
                            keys(a.plus(U - 1))
                        if a.u == 2:
                            values(a.plus(U - 2))
                        if a.u == 3:
                            oturn(a.plus(-U - 3))

                    pe.wait_ge(s["init"], 4)
                    first = At(0, 0, U)
                    queries(first)
                    keys(first)
                    values(first)
                    score(first)
                    run_units(pe, U, TILES, step, U + 1)

                @block.scalar
                def _(act):
                    def outT(a):
                        if not a.inside(TOTAL):
                            return
                        act.wait_ge(s["oT"], a.t + 1)
                        wait(act, s["mixed"], U * (a.t + 1))
                        act.copy(oT[:, :, :], M[:, :].rearrange("p (e q) -> p e q", e=E0)).then_inc(s["oTc"], 1)

                    def step(a):
                        at.tcopy(act, a.plus(-1))
                        if a.u == 0:
                            outT(a.plus(-2 * U))
                        at.exp(act, a)

                    run_units(act, U, TILES, step, U + 1)

                @block.vector
                def _(dve):
                    def spread(dst, bias):
                        for half in range(2):
                            rows = slice(64 * half, 64 * half + 64)
                            for b in range(TB):
                                last = dve.tensor_tensor(dst(b, half),
                                                         M[rows, :].rearrange("p (e b q) -> p e b q", e=E0, b=TB)[:, :, b, :],
                                                         bc(w(bias)[rows, :].unsqueeze(2), [64, E0, S]), ALU.add)
                        return last

                    def queries(a):
                        if not a.inside(TOTAL):
                            return
                        dve.wait_ge(s["q"], a.t + 1)
                        wait(dve, s["scored"], U * (a.t - 1))
                        spread(lambda b, half: LQ[64 * b:64 * b + 64, a.par, :, half, b * S:(b + 1) * S], "bq").then_inc(
                            s["qout"], 1)

                    def keys(a):
                        if not a.inside(TOTAL):
                            return
                        dve.wait_ge(s["k"], a.t + 1)
                        wait(dve, s["kbd"], U * (a.t - 1))
                        spread(lambda b, half: Ks[64 * b:64 * b + 64, a.par, :, half, :], "bk").then_inc(s["kout"], 1)

                    def values(a):
                        if not a.inside(TOTAL):
                            return
                        dve.wait_ge(s["v"], a.t + 1)
                        wait(dve, s["mixed"], U * (a.t - 1))
                        for b in range(TB):
                            rows = slice(64 * b, 64 * b + 64)
                            for hh in range(2):
                                split = lambda x: x.rearrange("p (e c h d) -> p e c h d", e=E0, c=PAIRS, h=2)[:, :, :, hh, :]
                                last = dve.tensor_tensor(Vbd[64 * hh:64 * hh + 64, a.par, :, :, b, hh, 0:HD],
                                                         split(M[rows, :]), split(row("bv")[rows, :]), ALU.add)
                        last.then_inc(s["vout"], 1)

                    def finish(a):
                        dve.wait_ge(s["wb"], 3 * (a.t + 1))
                        wait(dve, s["xsum"], a.t)
                        dve.tensor_tensor(ya[:, :], K.psO[:, 384:384 + D], yb[:, a.par, :], ALU.add).then_inc(s["ysum"], 1)
                        dve.wait_ge(s["ysum"], a.t + 1)
                        dve.tensor_tensor(K.X[:, a.t, :], K.X[:, a.t, :], ya[:, :], ALU.add).then_inc(s["xsum"], 1)

                    def normalise(a):
                        done = a.plus(-U)
                        if a.inside(TOTAL):
                            dve.wait_ge(s["mixed"], a.n + 1)
                        elif a.u == U - 1 and done.inside(TOTAL):
                            dve.wait_ge(s["mixed"], TOTAL + 1)
                        if a.u == U - 1 and done.inside(TOTAL):
                            finish(done)
                        if not a.inside(TOTAL):
                            return
                        wait(dve, s["normed"], a.n - 1)
                        ps = K.psO[:, 0:288].rearrange("p (c b h e) -> p c b h e", c=PAIRS, b=TB, h=2)
                        for b in range(TB):
                            rows = slice(64 * b, 64 * b + 64)
                            last = dve.reciprocal(rl[rows, a.up, :, :], ps[rows, :, b, :, HD])
                        last.then_inc(s["recip"], 1)
                        dve.wait_ge(s["recip"], a.n + 1)
                        wait(dve, s["oT"], a.t - 1)
                        for b in range(TB):
                            rows = slice(64 * b, 64 * b + 64)
                            last = dve.tensor_tensor(o[rows, a.par, a.u, :].rearrange("p (c h d) -> p c h d", c=PAIRS, h=2),
                                                     ps[rows, :, b, :, 0:HD],
                                                     bc(rl[rows, a.up, :, :].unsqueeze(3), [64, PAIRS, 2, HD]), ALU.mult)
                        last.then_inc(s["normed"], 1)

                    def step(a):
                        at.shift(dve, a)
                        normalise(a.plus(-2))
                        if a.u == 1:
                            queries(a.plus(U - 1))
                        if a.u == 2:
                            keys(a.plus(U - 2))
                        if a.u == 3:
                            values(a.plus(U - 3))

                    dve.wait_ge(s["init"], 4)
                    first = At(0, 0, U)
                    queries(first)
                    keys(first)
                    values(first)
                    run_units(dve, U, TILES, step, U + 2)


def stage_cross_masked(K):
    layer_norm(K, "n4_")
    nc, w, row = K.nc, K.w, K.row
    with ExitStack() as st:
        s = K.sems(st, "x4_", UNIT_SEMS + "masked zero ones qin kin vin oT oTc ysum xsum")
        sb = lambda n, sh, dt=F32: st.enter_context(nc.sbuf_tensor("x4_" + n, sh, dt))
        U, TOTAL, HALF = 2, TILES * 2, HEADS // 2
        neg, identb = sb("neg", [P, TILES, KEYS], BF16), sb("identb", [P, P], BF16)
        LQ, RK = sb("LQ", [P, 2, 2, P]), sb("RK", [P, 2, HALF, KEYS])
        V1 = sb("V1", [KEYS, 2, TB, HEADS, HD + 1])
        rl, o = sb("rl", [P, 2, HALF]), sb("o", [P, 2, D])
        oT, ya = sb("oT", [D, P]), sb("ya", [P, 2, D])
        at = Attention(K, st, s, "x4_", TOTAL, KEYS, 1.0 / float(D) ** 0.5)
        M = K.psM

        with nc.Block() as block:
            @block.gpsimd
            def _(pool):
                pool.memset(V1[:, :, :, :, HD:HD + 1], 1.0).then_inc(s["ones"], 1)
                pool.memset(LQ[:, :, :, :], 0.0).then_inc(s["zero"], 1)
                pool.wait_ge(K.late["context"], 32)

                def keys(a):
                    if not a.inside(TOTAL):
                        return
                    wait(pool, s["scored"], a.n - 1)
                    pool.tensor_tensor(RK[:, a.up, :, :], bc(K.ctxS[:, a.t, a.u, :].unsqueeze(1), [P, HALF, KEYS]),
                                       bc(w("mask8").unsqueeze(2), [P, HALF, KEYS]), ALU.mult).then_inc(s["kin"], 1)

                def values(a):
                    if not a.inside(TOTAL):
                        return
                    wait(pool, s["mixed"], U * (a.t - 1))
                    pool.tensor_copy(V1[:, a.par, :, :, 0:HD],
                                     K.ctx[:, bass.ds(a.t * TB, TB), :].rearrange("p b (h d) -> p b h d", h=HEADS)).then_inc(
                                         s["vin"], 1)

                def step(a):
                    keys(a.plus(1))
                    if a.u == 1:
                        values(a.plus(1))

                first = At(0, 0, U)
                keys(first)
                values(first)
                run_units(pool, U, TILES, step, 0)

            @block.tensor
            def _(pe):
                def score(a):
                    if not a.inside(TOTAL):
                        return
                    at.scores_free(pe, a)
                    pe.wait_ge(s["qin"], a.t + 1)
                    pe.wait_ge(s["kin"], a.n + 1)
                    for c in range(2):
                        bank = K.psS[a.up][:, c * 512:(c + 1) * 512]
                        pe.matmul(bank, LQ[:, a.par, a.u, :], RK[:, a.up, 4 * c:4 * c + 4, :].rearrange("p h k -> p (h k)"),
                                  start=True, stop=False)
                        last = pe.matmul(bank.rearrange("p (h k) -> p h k", h=4), identb[:, :],
                                         bc(neg[:, a.t, :].unsqueeze(1), [P, 4, KEYS]), start=False, stop=True)
                    last.then_inc(s["scored"], 1)

                def mix(a):
                    done = a.plus(-U)
                    if a.inside(TOTAL):
                        pe.wait_ge(s["tcopied"], 2 * (a.n + 1))
                        pe.wait_ge(s["vin"], a.t + 1)
                        wait(pe, s["normed"], a.n)
                        for h in range(HALF):
                            last = pe.matmul(K.psO[:, h * 18:(h + 1) * 18], at.PT[:, a.up, h * P:(h + 1) * P],
                                             V1[:, a.par, :, HALF * a.u + h, :], start=True, stop=True)
                    if a.u == U - 1 and done.inside(TOTAL):
                        pe.wait_ge(s["oTc"], done.t + 1)
                        if not a.inside(TOTAL):
                            pe.wait_ge(s["normed"], TOTAL)
                        last = pe.matmul(K.psO[:, 384:384 + D], oT[:, :], w("W_outT"), start=True, stop=True)
                        last.then_inc(s["mixed"], 1)
                    elif a.inside(TOTAL):
                        last.then_inc(s["mixed"], 1)

                def oturn(a):
                    if not a.inside(TOTAL):
                        return
                    pe.wait_ge(s["normed"], U * (a.t + 1))
                    wait(pe, s["oTc"], a.t)
                    pe.transpose(M[:, 0:P], o[:, a.par, :], K.ident).then_inc(s["oT"], 1)

                def step(a):
                    score(a.plus(1))
                    mix(a.plus(-1))
                    at.turn(pe, a)
                    if a.u == 1:
                        oturn(a.plus(-U))

                pe.wait_ge(s["ones"], 1)
                pe.wait_ge(s["masked"], 2)
                score(At(0, 0, U))
                run_units(pe, U, TILES, step, U + 1)

            @block.scalar
            def _(act):
                def queries(a):
                    if not a.inside(TOTAL):
                        return
                    wait(act, s["scored"], U * (a.t - 1))
                    for half in range(2):
                        for b in range(TB):
                            last = act.copy(LQ[64 * b:64 * b + 64, a.par, half, b * S:(b + 1) * S],
                                            K.XnT[64 * half:64 * half + 64, bass.ds(a.t * P + b * S, S)])
                    last.then_inc(s["qin"], 1)

                def outT(a):
                    if not a.inside(TOTAL):
                        return
                    act.wait_ge(s["oT"], a.t + 1)
                    wait(act, s["mixed"], U * (a.t + 1))
                    act.copy(oT[:, :], M[:, 0:P]).then_inc(s["oTc"], 1)

                def step(a):
                    at.tcopy(act, a.plus(-1))
                    at.exp(act, a)
                    if a.u == 0:
                        queries(a.plus(U))
                    if a.u == 1:
                        outT(a.plus(-U))

                act.wait_ge(s["zero"], 1)
                queries(At(0, 0, U))
                run_units(act, U, TILES, step, U)

            @block.vector
            def _(dve):
                dve.wait_ge(K.late["context"], 32)
                dve.tensor_copy(identb[:, :], K.ident).then_inc(s["masked"], 1)
                dve.tensor_scalar(neg[:, :, :], K.mask[:, :, :], 0.0, NEG1, ALU.is_equal, ALU.mult).then_inc(s["masked"], 1)

                def finish(a):
                    wait(dve, s["xsum"], a.t - 1)
                    dve.tensor_tensor(ya[:, a.par, :], K.psO[:, 384:384 + D], row("b_out"), ALU.add).then_inc(s["ysum"], 1)
                    dve.wait_ge(s["ysum"], a.t + 1)
                    dve.tensor_tensor(K.X[:, a.t, :], K.X[:, a.t, :], ya[:, a.par, :], ALU.add).then_inc(s["xsum"], 1)

                def normalise(a):
                    done = a.plus(-U)
                    if a.inside(TOTAL):
                        dve.wait_ge(s["mixed"], a.n + 1)
                    elif a.u == U - 1 and done.inside(TOTAL):
                        dve.wait_ge(s["mixed"], TOTAL + 1)
                    if a.u == U - 1 and done.inside(TOTAL):
                        finish(done)
                    if not a.inside(TOTAL):
                        return
                    wait(dve, s["normed"], a.n - 1)
                    ps = K.psO[:, 0:144].rearrange("p (h b e) -> p h b e", h=HALF, b=TB)
                    for b in range(TB):
                        rows = slice(64 * b, 64 * b + 64)
                        last = dve.reciprocal(rl[rows, a.up, :], ps[rows, :, b, HD])
                    last.then_inc(s["recip"], 1)
                    dve.wait_ge(s["recip"], a.n + 1)
                    wait(dve, s["oT"], a.t - 1)
                    for b in range(TB):
                        rows = slice(64 * b, 64 * b + 64)
                        last = dve.tensor_tensor(o[rows, a.par, 64 * a.u:64 * a.u + 64].rearrange("p (h d) -> p h d", h=HALF),
                                                 ps[rows, :, b, 0:HD], bc(rl[rows, a.up, :].unsqueeze(2), [64, HALF, HD]),
                                                 ALU.mult)
                    last.then_inc(s["normed"], 1)

                def step(a):
                    at.shift(dve, a)
                    normalise(a.plus(-2))

                run_units(dve, U, TILES, step, U + 2)


def project(K, tag, QT, KT, V, wq, wk, wv, bq=None, bk=None, bv=None):
    nc, w = K.nc, K.w
    G, GROUPS = 4, TILES // 4
    N = G * P
    with ExitStack() as st:
        s = K.sems(st, tag, "xin q k v qout kout vout")
        xs = st.enter_context(nc.sbuf_tensor(tag + "xs", [D, 2, N], F32))
        banks = bank_views(K)

        def groups(eng, group):
            group(0, 0)
            group(1, 1)
            with eng.Fori(1, GROUPS // 2) as p:
                group(p * 2, 0)
                group(p * 2 + 1, 1)

        with nc.Block() as block:
            @block.gpsimd
            def _(pool):
                def group(g, par):
                    wait(pool, s["v"], g - 1)
                    pool.tensor_copy(xs[:, par, :], K.XnT[:, bass.ds(g * N, N)]).then_inc(s["xin"], 1)

                groups(pool, group)

            @block.tensor
            def _(pe):
                def group(g, par):
                    pe.wait_ge(s["xin"], g + 1)
                    wait(pe, s["qout"], g - 1)
                    pe.matmul(banks[par], w(wq), xs[:, par, :], start=True, stop=True).then_inc(s["q"], 1)
                    wait(pe, s["kout"], g - 1)
                    pe.matmul(banks[2 + par], w(wk), xs[:, par, :], start=True, stop=True).then_inc(s["k"], 1)
                    wait(pe, s["vout"], g - 1)
                    for i in range(G):
                        last = pe.matmul(banks[4 + par][:, i * D:(i + 1) * D], xs[:, par, i * P:(i + 1) * P], w(wv),
                                         start=True, stop=True)
                    last.then_inc(s["v"], 1)

                groups(pe, group)

            @block.scalar
            def _(act):
                def group(g, par):
                    for ready, out, dst, bank, bias in (("q", "qout", QT, par, bq), ("k", "kout", KT, 2 + par, bk)):
                        act.wait_ge(s[ready], g + 1)
                        view = dst[:, bass.ds(g * N, N)]
                        if bias is None:
                            act.copy(view, banks[bank]).then_inc(s[out], 1)
                        else:
                            act.activation(view, banks[bank], ACT.Identity, bias=w(bias)).then_inc(s[out], 1)

                groups(act, group)

            @block.vector
            def _(dve):
                def group(g, par):
                    dve.wait_ge(s["v"], g + 1)
                    ps = banks[4 + par].rearrange("p (i d) -> p i d", i=G)
                    dst = V[:, bass.ds(g * G, G), :]
                    if bv is None:
                        dve.tensor_copy(dst, ps).then_inc(s["vout"], 1)
                    else:
                        dve.tensor_tensor(dst, ps, bc(K.row(bv).unsqueeze(1), [P, G, D]), ALU.add).then_inc(s["vout"], 1)

                groups(dve, group)


def stage_relative(K):
    layer_norm(K, "n5_")
    nc, w, row = K.nc, K.w, K.row
    with ExitStack() as keep:
        rt = lambda n, sh, dt=F32: keep.enter_context(nc.sbuf_tensor("a5_" + n, sh, dt))
        QT, KT, V = rt("QT", [D, TILES * P]), rt("KTall", [D, TILES * P]), rt("V", [P, TILES, D])
        project(K, "p5_", QT, KT, V, "WqT", "WkT", "WvT", "bq1", "bk1", "bv1")
        dist = K.dram("hbm_dist", (TILES, P, 2 * UCOL))

        with ExitStack() as st:
            s = K.sems(st, "z5_", "rel relbd qin z zout stored0 stored1")
            sb = lambda n, sh, dt=F32: st.enter_context(nc.sbuf_tensor("z5_" + n, sh, dt))
            rel, relbd = sb("rel", [D, P]), sb("relbd", [D, HEADS, P])
            qs, Z = sb("qs", [D, 2, P]), sb("Z", [P, 2, 2, 8, P])
            with nc.Block() as block:
                @block.gpsimd
                def _(pool):
                    pool.wait_ge(s["rel"], 1)
                    pool.tensor_tensor(relbd[:, :, :], bc(rel[:, :].unsqueeze(1), [D, HEADS, P]),
                                       bc(w("headmask").unsqueeze(2), [D, HEADS, P]), ALU.mult).then_inc(s["relbd"], 1)

                    def step(a):
                        wait(pool, s["z"], 2 * (a.t - 1))
                        pool.tensor_copy(qs[:, a.par, :], QT[:, bass.ds(a.t * P, P)]).then_inc(s["qin"], 1)

                    run_units(pool, 1, TILES, step, 0)

                @block.tensor
                def _(pe):
                    pe.wait_ge(s["relbd"], 1)
                    rb = relbd[:, :, :].rearrange("p h j -> p (h j)")

                    def step(a):
                        pe.wait_ge(s["qin"], a.t + 1)
                        for half in range(2):
                            wait(pe, s["zout"], 2 * (a.t - 1) + half + 1)
                            for c in range(2):
                                last = pe.matmul(K.psS[half][:, c * 512:(c + 1) * 512], qs[:, a.par, :],
                                                 rb[:, half * UCOL + c * 512:half * UCOL + (c + 1) * 512], start=True, stop=True)
                            last.then_inc(s["z"], 1)

                    run_units(pe, 1, TILES, step, 0)

                @block.scalar
                def _(act):
                    def step(a):
                        for half in range(2):
                            act.wait_ge(s["z"], 2 * a.t + half + 1)
                            wait(act, s[f"stored{a.par}"], 16 * a.round)
                            act.copy(Z[:, a.par, half, :, :],
                                     K.psS[half][:, :].rearrange("p (h j) -> p h j", h=8)).then_inc(s["zout"], 1)

                    run_units(act, 1, TILES, step, 0)

                @block.vector
                def _(dve):
                    dve.tensor_scalar(rel[:, :], w("relT"), float(HD) ** 0.5, None, ALU.mult).then_inc(s["rel"], 1)

                @block.sync
                def _(sp):
                    def step(a):
                        dst = dist[a.t, :, :]
                        if not isinstance(a.t, int):
                            ready, at = sp.snap(2 * (a.t + 1)), sp.snap(a.t * (P * 2 * UCOL))
                            dst = bass.AP(dist.tensor, at, [[2 * UCOL, P], [1, 2 * UCOL]])
                            sp.wait_ge(s["zout"], ready)
                        else:
                            sp.wait_ge(s["zout"], 2 * (a.t + 1))
                        sp.dma_start(dst, Z[:, a.par, :, :, :].rearrange("p i h j -> p (i h j)")).then_inc(
                            s[f"stored{a.par}"], 16)

                    run_units(sp, 1, TILES, step, 0)
                    for par in range(2):
                        sp.wait_ge(s[f"stored{par}"], 16 * TILES // 2)

        with ExitStack() as st:
            s = K.sems(st, "a5_", UNIT_SEMS + "biased zero init din0 din1 qin kout kin vin oT oTc ysum xsum")
            sb = lambda n, sh, dt=F32: st.enter_context(nc.sbuf_tensor("u5_" + n, sh, dt))
            U, TOTAL = 1, TILES
            S2 = sb("S2", [P, 2, UCOL])
            LQ = sb("LQ", [P, 2, 2, P])
            Ks, RK = sb("Ks", [P, 2, 2, S]), sb("RK", [P, 2, 2, 8, S])
            Vbd = sb("Vbd", [P, 2, PAIRS, TB, 2, HD + 1])
            rl, o = sb("rl", [P, 2, PAIRS, 2]), sb("o", [P, 2, D])
            oT, ya = sb("oT", [D, P]), sb("ya", [P, D])
            at = Attention(K, st, s, "a5_", TOTAL, S, 1.0 / float(HD) ** 0.5)
            M = K.psM

            def add_distances(dve, a, out, sc):
                dve.wait_ge(s[f"din{a.par}"], 16 * TB * (a.round + 1))
                return dve.tensor_tensor(out, sc, S2[:, a.par, :].rearrange("p (g k) -> p g k", g=HEADS), ALU.add)

            at.bias = add_distances

            with nc.Block() as block:
                @block.sync
                def _(sp):
                    def step(a):
                        base = a.t * (P * 2 * UCOL) + (S - 1)
                        if not isinstance(a.t, int):
                            rows = [sp.snap(base), sp.snap(base + S * 2 * UCOL)]
                            sp.wait_ge(s["biased"], sp.snap(a.n - 1))
                        else:
                            rows = [base, base + S * 2 * UCOL]
                            wait(sp, s["biased"], a.n - 1)
                        for b in range(TB):
                            src = bass.AP(dist.tensor, rows[b], [[2 * UCOL - 1, S], [P, HEADS], [1, S]])
                            sp.dma_start(S2[64 * b:64 * b + 64, a.par, :].rearrange("p (h k) -> p h k", h=HEADS),
                                         src).then_inc(s[f"din{a.par}"], 16)

                    run_units(sp, 1, TILES, step, 0)

                @block.gpsimd
                def _(pool):
                    pool.memset(LQ[:, :, :, :], 0.0).then_inc(s["zero"], 1)
                    pool.memset(Vbd[:, :, :, :, :, :], 0.0).then_inc(s["zero"], 1)
                    pool.wait_ge(s["zero"], 2)

                    def step(a):
                        pool.wait_ge(s["kout"], a.n + 1)
                        wait(pool, s["scored"], a.n - 1)
                        last = pool.tensor_tensor(RK[:, a.par, :, :, :], bc(Ks[:, a.par, :, :].unsqueeze(2), [P, 2, 8, S]),
                                                  bc(w("mask8").unsqueeze(1).unsqueeze(3), [P, 2, 8, S]), ALU.mult)
                        last.then_inc(s["kin"], 1)

                    run_units(pool, U, TILES, step, 0)

                @block.tensor
                def _(pe):
                    def score(a):
                        if not a.inside(TOTAL):
                            return
                        at.scores_free(pe, a)
                        pe.wait_ge(s["qin"], a.n + 1)
                        pe.wait_ge(s["kin"], a.n + 1)
                        for half in range(2):
                            last = pe.matmul(K.psS[a.up][:, half * 512:(half + 1) * 512], LQ[:, a.par, half, :],
                                             RK[:, a.par, half, :, :].rearrange("p h k -> p (h k)"), start=True, stop=True)
                        last.then_inc(s["scored"], 1)

                    def mix(a):
                        done = a.plus(-2)
                        if a.inside(TOTAL):
                            pe.wait_ge(s["tcopied"], 2 * (a.n + 1))
                            pe.wait_ge(s["vin"], a.n + 1)
                            wait(pe, s["normed"], a.n)
                            for c in range(PAIRS):
                                last = pe.matmul(K.psO[:, c * 36:(c + 1) * 36], at.PT[:, a.up, c * P:(c + 1) * P],
                                                 Vbd[:, a.par, c, :, :, :], start=True, stop=True)
                        if done.inside(TOTAL):
                            pe.wait_ge(s["oTc"], done.n + 1)
                            if not a.inside(TOTAL):
                                pe.wait_ge(s["normed"], TOTAL)
                                pe.wait_ge(s["ysum"], done.n)
                            last = pe.matmul(K.psO[:, 384:384 + D], oT[:, :], w("WoT"), start=True, stop=True)
                        if a.inside(TOTAL) or done.inside(TOTAL):
                            last.then_inc(s["mixed"], 1)

                    def oturn(a):
                        if not a.inside(TOTAL):
                            return
                        pe.wait_ge(s["normed"], a.n + 1)
                        wait(pe, s["oTc"], a.n)
                        pe.transpose(M[:, 0:P], o[:, a.par, :], K.ident).then_inc(s["oT"], 1)

                    def step(a):
                        score(a.plus(1))
                        mix(a.plus(-1))
                        at.turn(pe, a)
                        oturn(a.plus(-2))

                    score(At(0, 0, U))
                    run_units(pe, U, TILES, step, 3)

                @block.scalar
                def _(act):
                    act.wait_ge(s["zero"], 2)
                    for hh in range(2):
                        ones = Vbd[64 * hh:64 * hh + 64, :, :, :, hh, HD].rearrange("p x c b -> p (x c b)")
                        act.activation(ones, ones, ACT.Identity, bias=1.0).then_inc(s["init"], 1)

                    def queries(a):
                        if not a.inside(TOTAL):
                            return
                        wait(act, s["scored"], a.n - 1)
                        for half in range(2):
                            for b in range(TB):
                                last = act.copy(LQ[64 * b:64 * b + 64, a.par, half, b * S:(b + 1) * S],
                                                QT[64 * half:64 * half + 64, bass.ds(a.t * P + b * S, S)])
                        last.then_inc(s["qin"], 1)
                        wait(act, s["kin"], a.n - 1)
                        for half in range(2):
                            for b in range(TB):
                                last = act.copy(Ks[64 * b:64 * b + 64, a.par, half, :],
                                                KT[64 * half:64 * half + 64, bass.ds(a.t * P + b * S, S)])
                        last.then_inc(s["kout"], 1)

                    def values(a):
                        if not a.inside(TOTAL):
                            return
                        act.wait_ge(s["init"], 2)
                        wait(act, s["mixed"], a.n - 1)
                        for b in range(TB):
                            for hh in range(2):
                                src = V[64 * b:64 * b + 64, a.t, :].rearrange("p (c h d) -> p c h d", c=PAIRS, h=2)
                                last = act.copy(Vbd[64 * hh:64 * hh + 64, a.par, :, b, hh, 0:HD], src[:, :, hh, :])
                        last.then_inc(s["vin"], 1)

                    def outT(a):
                        if not a.inside(TOTAL):
                            return
                        act.wait_ge(s["oT"], a.n + 1)
                        wait(act, s["mixed"], a.n + 2)
                        act.copy(oT[:, :], M[:, 0:P]).then_inc(s["oTc"], 1)

                    def step(a):
                        at.tcopy(act, a.plus(-1))
                        at.exp(act, a)
                        queries(a.plus(2))
                        values(a.plus(1))
                        outT(a.plus(-2))

                    first = At(0, 0, U)
                    queries(first)
                    queries(first.plus(1))
                    values(first)
                    run_units(act, U, TILES, step, 2)

                @block.vector
                def _(dve):
                    def finish(a):
                        wait(dve, s["xsum"], a.n)
                        dve.tensor_tensor(ya[:, :], K.psO[:, 384:384 + D], row("bo1"), ALU.add).then_inc(s["ysum"], 1)
                        dve.wait_ge(s["ysum"], a.n + 1)
                        dve.tensor_tensor(K.X[:, a.t, :], K.X[:, a.t, :], ya[:, :], ALU.add).then_inc(s["xsum"], 1)

                    def normalise(a):
                        done = a.plus(-2)
                        if a.inside(TOTAL) or done.inside(TOTAL):
                            dve.wait_ge(s["mixed"], a.n + 1)
                        if done.inside(TOTAL):
                            finish(done)
                        if not a.inside(TOTAL):
                            return
                        wait(dve, s["normed"], a.n - 1)
                        ps = K.psO[:, 0:288].rearrange("p (c b h e) -> p c b h e", c=PAIRS, b=TB, h=2)
                        for b in range(TB):
                            rows = slice(64 * b, 64 * b + 64)
                            last = dve.reciprocal(rl[rows, a.up, :, :], ps[rows, :, b, :, HD])
                        last.then_inc(s["recip"], 1)
                        dve.wait_ge(s["recip"], a.n + 1)
                        wait(dve, s["oT"], a.n - 1)
                        for b in range(TB):
                            rows = slice(64 * b, 64 * b + 64)
                            last = dve.tensor_tensor(o[rows, a.par, :].rearrange("p (c h d) -> p c h d", c=PAIRS, h=2),
                                                     ps[rows, :, b, :, 0:HD],
                                                     bc(rl[rows, a.up, :, :].unsqueeze(3), [64, PAIRS, 2, HD]), ALU.mult)
                        last.then_inc(s["normed"], 1)

                    def step(a):
                        at.shift(dve, a)
                        normalise(a.plus(-2))

                    run_units(dve, U, TILES, step, 4, peel=3)


def regroup(K, tag, pairs, back):
    nc = K.nc
    with ExitStack() as st:
        s = K.sems(st, tag, "out in")
        mem = [K.dram(f"hbm_{tag}{i}", (TILES * P, D)) for i in range(len(pairs))]
        with nc.Block() as block:
            @block.sync
            def _(sp):
                def natural(m):
                    return m.rearrange("(t p) d -> p t d", p=P)

                def grouped(m, b5):
                    return m.rearrange("(s u b) d -> b s u d", s=S5, b=4)[b5, :, :, :]

                def grouped_sb(x, b5):
                    return x[32 * b5:32 * b5 + 32, :, :]

                n = 0
                for m, (src, _) in zip(mem, pairs):
                    if back:
                        for b5 in range(4):
                            sp.dma_start(grouped(m, b5), grouped_sb(src, b5)).then_inc(s["out"], 16)
                            n += 16
                    else:
                        sp.dma_start(natural(m), src[:, :, :]).then_inc(s["out"], 16)
                        n += 16
                sp.wait_ge(s["out"], n)
                n = 0
                for m, (_, dst) in zip(mem, pairs):
                    if back:
                        sp.dma_start(dst[:, :, :], natural(m)).then_inc(s["in"], 16)
                        n += 16
                    else:
                        for b5 in range(4):
                            sp.dma_start(grouped_sb(dst, b5), grouped(m, b5)).then_inc(s["in"], 16)
                            n += 16
                sp.wait_ge(s["in"], n)


def plain_norm(K, tag, dst):
    nc = K.nc
    with ExitStack() as st:
        s = K.sems(st, tag, "stats var vareps rstd")
        sb = lambda n, sh, dt=F32: st.enter_context(nc.sbuf_tensor(tag + n, sh, dt))
        st6, mv, rstd = sb("st6", [P, TILES, 6]), sb("mv", [P, TILES, 2]), sb("rstd", [P, TILES])
        with nc.Block() as block:
            @block.vector
            def _(dve):
                norm_stats(dve, s["stats"], st6, mv, K.X, 1, s["var"])
                dve.wait_ge(s["rstd"], 1)
                for t in range(TILES):
                    dve.tensor_scalar(dst[:, t, :], K.X[:, t, :], mv[:, t, 0:1], rstd[:, t:t + 1], ALU.subtract, ALU.mult)

            @block.gpsimd
            def _(pool):
                pool.wait_ge(s["var"], 1)
                pool.tensor_scalar(rstd[:, :], mv[:, :, 1], LN_EPS, None, ALU.add).then_inc(s["vareps"], 1)
                pool.wait_ge(s["vareps"], 1)
                pool.tensor_tensor(rstd[:, :], rstd[:, :], K.nhalf[:, :], ALU.pow).then_inc(s["rstd"], 1)


def stage_causal(K):
    nc, w, row = K.nc, K.w, K.row
    K.H = K.es.enter_context(nc.sbuf_tensor("H", [P, TILES, D], F32))
    regroup(K, "g6_", [(K.X, K.X)], False)
    plain_norm(K, "h6_", K.H)
    layer_norm(K, "n6_", src=K.H, affine=("ln1w", "ln1b"))
    with ExitStack() as keep:
        rt = lambda n, sh, dt=F32: keep.enter_context(nc.sbuf_tensor("a6_" + n, sh, dt))
        QT, KT, V = rt("QT", [D, TILES * P]), rt("KTall", [D, TILES * P]), rt("V", [P, TILES, D])
        project(K, "p6_", QT, KT, V, "q5T", "k5T", "v5T")
        with ExitStack() as st:
            s = K.sems(st, "a6_", UNIT_SEMS + "const zero spread qin kin vin oT oTc ysum xsum")
            sb = lambda n, sh, dt=F32: st.enter_context(nc.sbuf_tensor("u6_" + n, sh, dt))
            U, TOTAL, NB, G = 1, TILES, 4, 4
            QS, KS = sb("QS", [P, G, TILES, S5]), sb("KS", [P, G, TILES, S5])
            VS = sb("VS", [P, TILES, G, NB, HD])
            LQ, RK = sb("LQ", [P, 2, G, NB, S5]), sb("RK", [P, 2, G, 4, S5])
            Vbd = sb("Vbd", [P, 2, G * NB, 4, HD + 1])
            rep, tri = sb("rep", [S5, P], BF16), sb("tri", [S5, S5], BF16)
            rl, o = sb("rl", [P, 2, G, NB, 4]), sb("o", [P, 2, D])
            oT, ya = sb("oT", [D, P]), sb("ya", [P, D])
            at = Attention(K, st, s, "a6_", TOTAL, S5, 1.0 / float(HD) ** 0.5, cols=512)
            M = K.psM
            mixed = [K.psO[:, 0:288], K.psT[:, 512:512 + 288]]
            block_of = w("blockmask")

            def spread_rows(eng, copy, kinds):
                for kind in kinds:
                    for i in range(4):
                        for b in range(NB):
                            if kind == "v":
                                dst = VS[32 * i:32 * i + 32, :, :, b, :]
                                src = V[32 * b:32 * b + 32, :, :].rearrange("p t (g j d) -> p t g j d", g=G, j=4)[:, :, :, i, :]
                            else:
                                dst = {"q": QS, "k": KS}[kind][32 * b:32 * b + 32, i, :, :]
                                src = {"q": QT, "k": KT}[kind][32 * i:32 * i + 32, :].rearrange(
                                    "p (t b q) -> p t b q", t=TILES, b=NB)[:, :, b, :]
                            last = copy(dst, src)
                last.then_inc(s["spread"], 1)

            with nc.Block() as block:
                @block.gpsimd
                def _(pool):
                    for par in range(2):
                        pool.tensor_copy(Vbd[:, par, :, :, HD], bc(block_of.unsqueeze(1), [P, G * NB, 4])).then_inc(
                            s["zero"], 1)
                    pool.wait_ge(s["spread"], 2)

                    def step(a):
                        wait(pool, s["scored"], a.n - 1)
                        pool.tensor_tensor(LQ[:, a.par, :, :, :], bc(QS[:, :, a.t, :].unsqueeze(2), [P, G, NB, S5]),
                                           bc(block_of.unsqueeze(1).unsqueeze(3), [P, G, NB, S5]), ALU.mult).then_inc(
                                               s["qin"], 1)
                        pool.tensor_tensor(RK[:, a.par, :, :, :], bc(KS[:, :, a.t, :].unsqueeze(2), [P, G, 4, S5]),
                                           bc(w("quadmask").unsqueeze(1).unsqueeze(3), [P, G, 4, S5]), ALU.mult).then_inc(
                                               s["kin"], 1)
                        wait(pool, s["mixed"], a.n - 1)
                        pool.tensor_tensor(Vbd[:, a.par, :, :, 0:HD],
                                           bc(VS[:, a.t, :, :, :].rearrange("p g b d -> p (g b) d").unsqueeze(2),
                                              [P, G * NB, 4, HD]),
                                           bc(block_of.unsqueeze(1).unsqueeze(3), [P, G * NB, 4, HD]), ALU.mult).then_inc(
                                               s["vin"], 1)

                    run_units(pool, U, TILES, step, 0)

                @block.tensor
                def _(pe):
                    pe.wait_ge(s["const"], 2)
                    pe.wait_ge(s["zero"], 2)

                    def score(a):
                        if not a.inside(TOTAL):
                            return
                        at.scores_free(pe, a)
                        pe.wait_ge(s["qin"], a.n + 1)
                        pe.wait_ge(s["kin"], a.n + 1)
                        bank = K.psS[a.up][:, 0:512]
                        pe.matmul(bank.rearrange("p (h k) -> p h k", h=HEADS), rep[:, :],
                                  bc(tri[:, :].unsqueeze(1), [S5, HEADS, S5]), start=True, stop=False, skip_group_check=True)
                        for g in range(G):
                            last = pe.matmul(bank[:, g * P:(g + 1) * P], LQ[:, a.par, g, :, :].rearrange("p b q -> p (b q)"),
                                             RK[:, a.par, g, :, :].rearrange("p j k -> p (j k)"), start=False, stop=True,
                                             skip_group_check=True)
                        last.then_inc(s["scored"], 1)

                    def mix(a):
                        done = a.plus(-2)
                        if a.inside(TOTAL):
                            pe.wait_ge(s["tcopied"], a.n + 1)
                            pe.wait_ge(s["vin"], a.n + 1)
                            wait(pe, s["normed"], a.n)
                            for g in range(G):
                                last = pe.matmul(mixed[g // 2][:, (g % 2) * 144:(g % 2 + 1) * 144],
                                                 at.PT[:, a.up, g * P:(g + 1) * P],
                                                 Vbd[:, a.par, NB * g:NB * (g + 1), :, :].rearrange("p b j e -> p (b j e)"),
                                                 start=True, stop=True)
                        if done.inside(TOTAL):
                            pe.wait_ge(s["oTc"], done.n + 1)
                            if not a.inside(TOTAL):
                                pe.wait_ge(s["normed"], TOTAL)
                                pe.wait_ge(s["ysum"], done.n)
                            last = pe.matmul(K.psO[:, 384:384 + D], oT[:, :], w("proj5T"), start=True, stop=True)
                        if a.inside(TOTAL) or done.inside(TOTAL):
                            last.then_inc(s["mixed"], 1)

                    def oturn(a):
                        if not a.inside(TOTAL):
                            return
                        pe.wait_ge(s["normed"], a.n + 1)
                        wait(pe, s["oTc"], a.n)
                        pe.transpose(M[:, 0:P], o[:, a.par, :], K.ident).then_inc(s["oT"], 1)

                    def step(a):
                        score(a.plus(1))
                        mix(a.plus(-1))
                        at.turn(pe, a)
                        oturn(a.plus(-2))

                    score(At(0, 0, U))
                    run_units(pe, U, TILES, step, 3)

                @block.scalar
                def _(act):
                    act.copy(rep[:, :], w("repq")[0:S5, :]).then_inc(s["const"], 1)
                    act.mul(tri[:, :], w("causal")[0:S5, :], NEG0).then_inc(s["const"], 1)
                    spread_rows(act, act.copy, "q")

                    def outT(a):
                        if not a.inside(TOTAL):
                            return
                        act.wait_ge(s["oT"], a.n + 1)
                        wait(act, s["mixed"], a.n + 2)
                        act.copy(oT[:, :], M[:, 0:P]).then_inc(s["oTc"], 1)

                    def step(a):
                        at.tcopy(act, a.plus(-1))
                        at.exp(act, a)
                        outT(a.plus(-2))

                    run_units(act, U, TILES, step, 2)

                @block.vector
                def _(dve):
                    spread_rows(dve, dve.tensor_copy, "kv")

                    def finish(a):
                        wait(dve, s["xsum"], a.n)
                        dve.tensor_tensor(K.H[:, a.t, :], K.psO[:, 384:384 + D], K.H[:, a.t, :], ALU.add).then_inc(s["ysum"], 1)
                        dve.wait_ge(s["ysum"], a.n + 1)
                        dve.tensor_tensor(K.X[:, a.t, :], K.X[:, a.t, :], K.H[:, a.t, :], ALU.add).then_inc(s["xsum"], 1)

                    def normalise(a):
                        done = a.plus(-2)
                        if a.inside(TOTAL) or done.inside(TOTAL):
                            dve.wait_ge(s["mixed"], a.n + 1)
                        if done.inside(TOTAL):
                            finish(done)
                        if not a.inside(TOTAL):
                            return
                        wait(dve, s["normed"], a.n - 1)

                        def parts():
                            for b in range(NB):
                                for x in range(2):
                                    rows = slice(32 * b, 32 * b + 32)
                                    yield b, rows, x, mixed[x][rows, :].rearrange("p (g b j e) -> p g b j e", g=2, b=NB,
                                                                               j=4)[:, :, b, :, :]

                        for x in range(2):
                            last = dve.reciprocal(rl[:, a.up, 2 * x:2 * x + 2, :, :].rearrange("p g b j -> p (g b j)"),
                                                  mixed[x].rearrange("p (c e) -> p c e", e=HD + 1)[:, :, HD])
                        last.then_inc(s["recip"], 1)
                        dve.wait_ge(s["recip"], a.n + 1)
                        wait(dve, s["oT"], a.n - 1)
                        for b, rows, x, ps in parts():
                            last = dve.tensor_tensor(
                                o[rows, a.par, 64 * x:64 * x + 64].rearrange("p (g j d) -> p g j d", g=2, j=4),
                                ps[:, :, :, 0:HD], bc(rl[rows, a.up, 2 * x:2 * x + 2, b, :].unsqueeze(3), [32, 2, 4, HD]), ALU.mult)
                        last.then_inc(s["normed"], 1)

                    def step(a):
                        at.shift(dve, a)
                        normalise(a.plus(-2))

                    run_units(dve, U, TILES, step, 4, peel=3)
    regroup(K, "b6_", [(K.X, K.X), (K.H, K.H)], True)


def stage_moe(K):
    nc, w, row = K.nc, K.w, K.row
    SPARE = SLOTS
    xe = K.dram("hbm_slots", (SLOTS + TOPK * TILES * P, D))
    ye = K.dram("hbm_results", (SLOTS, D))
    with ExitStack() as keep:
        rt = lambda n, sh, dt=F32: keep.enter_context(nc.sbuf_tensor("f7_" + n, sh, dt))
        logits, X2 = rt("logits", [P, TILES, E1]), rt("X2", [P, TILES, D])
        layer_norm(K, "n7_", router=(w("rw5"), E1, logits), keep=X2, src=K.H, affine=("ln2w", "ln2b"))
        weight = rt("weight", [P, TOPK, TILES])
        into, back = rt("into", [P, TOPK, TILES], U32), rt("back", [P, TOPK, TILES], U32)

        with ExitStack() as st:
            s = K.sems(st, "r7_", "chain shifted exped counted summed zeroed zstored placed scattered")
            sb = lambda n, sh, dt=F32: st.enter_context(nc.sbuf_tensor("r7_" + n, sh, dt))
            mx, ex, rank = sb("mx", [P, TILES]), sb("ex", [P, TILES, E1]), sb("rank", [P, TILES, E1])
            less, pick = sb("less", [P, TILES, E1, E1]), sb("pick", [P, TOPK, TILES, E1])
            count, run = sb("count", [P, TILES, E1]), sb("run", [P, 2, TILES, E1])
            pos, tmp = sb("pos", [P, 2, TILES, E1]), sb("tmp", [P, TOPK, 3, TILES, E1])
            picked, fits = sb("picked", [P, TOPK, 3, TILES]), sb("fits", [P, TOPK, TILES])
            idx, zero = sb("idx", [P, TOPK, 2, TILES]), sb("zero", [P, D])
            TE = [P, TILES, E1]
            with nc.Block() as block:
                @block.vector
                def _(dve):
                    ch = Chain(s["chain"])
                    dve.memset(zero[:, :], 0.0).then_inc(s["zeroed"], 1)
                    ch.link(dve, dve.tensor_reduce(mx[:, :], logits[:, :, :], AX.X, ALU.max))
                    dve.tensor_tensor(ex[:, :, :], logits[:, :, :], bc(mx[:, :].unsqueeze(2), TE), ALU.subtract).then_inc(
                        s["shifted"], 1)
                    rank_columns(dve, ch, rank[:, :, :], less, logits, E1)
                    for k in range(TOPK):
                        last = dve.tensor_scalar(pick[:, k, :, :], rank[:, :, :], float(k), None, ALU.is_equal)
                    ch.link(dve, last)
                    dve.tensor_tensor(count[:, :, :], pick[:, 0, :, :], pick[:, 1, :, :], ALU.add).then_inc(s["counted"], 1)
                    dve.wait_ge(s["summed"], 1)
                    total = K.psM[:, 0:P].rearrange("p (t e) -> p t e", t=TILES)
                    ch.link(dve, dve.tensor_copy(run[:, 0, :, :], total))
                    half = 0
                    for d in (1, 2, 4, 8):
                        dve.tensor_tensor(run[:, 1 - half, d:, :], run[:, half, d:, :], run[:, half, 0:TILES - d, :], ALU.add)
                        ch.link(dve, dve.tensor_copy(run[:, 1 - half, 0:d, :], run[:, half, 0:d, :]))
                        half = 1 - half
                    ch.link(dve, dve.tensor_tensor(run[:, half, :, :], run[:, half, :, :], total, ALU.subtract))
                    before = K.psO[:, 0:P].rearrange("p (t e) -> p t e", t=TILES)
                    ch.link(dve, dve.tensor_tensor(pos[:, 0, :, :], run[:, half, :, :], before, ALU.add))
                    ch.link(dve, dve.tensor_scalar(run[:, half, 0, :], w("expert"), float(CAP), None, ALU.mult))
                    ch.link(dve, dve.tensor_tensor(pos[:, 1, :, :], pos[:, 0, :, :],
                                                   bc(run[:, half, 0, :].unsqueeze(1), TE), ALU.add))
                    dve.wait_ge(s["exped"], 1)
                    for k in range(TOPK):
                        for i, v in enumerate((pos[:, 0, :, :], pos[:, 1, :, :], ex[:, :, :])):
                            last = dve.tensor_tensor(tmp[:, k, i, :, :], pick[:, k, :, :], v, ALU.mult)
                    ch.link(dve, last)
                    ch.link(dve, dve.tensor_reduce(picked[:, :, :, :], tmp[:, :, :, :, :], AX.X, ALU.add))
                    ch.link(dve, dve.tensor_scalar(fits[:, :, :], picked[:, :, 0, :], float(CAP), None, ALU.is_lt))
                    ch.link(dve, dve.tensor_tensor(idx[:, :, 1, :], picked[:, :, 1, :], fits[:, :, :], ALU.mult))
                    for k in range(TOPK):
                        last = dve.tensor_scalar(idx[:, k, 0, :], w("token"), float(SPARE + k * TILES * P), None, ALU.add)
                    ch.link(dve, last)
                    ch.link(dve, dve.tensor_scalar(tmp[:, :, 0, :, 0], fits[:, :, :], -1.0, 1.0, ALU.mult, ALU.add))
                    ch.link(dve, dve.tensor_tensor(idx[:, :, 0, :], idx[:, :, 0, :], tmp[:, :, 0, :, 0], ALU.mult))
                    ch.link(dve, dve.tensor_tensor(idx[:, :, 0, :], idx[:, :, 0, :], idx[:, :, 1, :], ALU.add))
                    dve.tensor_copy(back[:, :, :], idx[:, :, 1, :])
                    dve.tensor_copy(into[:, :, :], idx[:, :, 0, :]).then_inc(s["placed"], 1)
                    ch.link(dve, dve.tensor_tensor(mx[:, :], picked[:, 0, 2, :], picked[:, 1, 2, :], ALU.add))
                    ch.link(dve, dve.reciprocal(mx[:, :], mx[:, :]))
                    ch.link(dve, dve.tensor_tensor(weight[:, :, :], picked[:, :, 2, :],
                                                   bc(mx[:, :].unsqueeze(1), [P, TOPK, TILES]), ALU.mult))
                    ch.link(dve, dve.tensor_tensor(weight[:, :, :], weight[:, :, :], fits[:, :, :], ALU.mult))

                @block.scalar
                def _(act):
                    act.wait_ge(s["shifted"], 1)
                    act.activation(ex[:, :, :], ex[:, :, :], ACT.Exp).then_inc(s["exped"], 1)

                @block.tensor
                def _(pe):
                    pe.wait_ge(s["counted"], 1)
                    cnt = count[:, :, :].rearrange("p t e -> p (t e)")
                    pe.matmul(K.psO[:, 0:P], w("tri"), cnt, start=True, stop=True)
                    pe.matmul(K.psM[:, 0:P], w("ones"), cnt, start=True, stop=True).then_inc(s["summed"], 1)

                @block.sync
                def _(sp):
                    sp.wait_ge(s["zeroed"], 1)
                    sp.dma_start(xe[0:SLOTS, :].rearrange("(p r) d -> p r d", p=P),
                                 bc(zero[:, :].unsqueeze(1), [P, SLOTS // P, D])).then_inc(s["zstored"], 16)

                @block.gpsimd
                def _(pool):
                    pool.wait_ge(s["placed"], 1)
                    pool.wait_ge(s["zstored"], 16)
                    for t in range(TILES):
                        for k in range(TOPK):
                            pool.indirect_dma_start(xe, bass.IndirectOffsetOnAxis(ap=into[:, k, t:t + 1], axis=0),
                                                    X2[:, t, :], None).then_inc(s["scattered"], 16)
                    pool.wait_ge(s["scattered"], 16 * TILES * TOPK)

        with ExitStack() as st:
            s = K.sems(st, "e7_", "xin0 xin1 w1in0 w1in1 w2in0 w2in1 turned xT h gelu y yout stored0 stored1")
            sb = lambda n, sh, dt=F32: st.enter_context(nc.sbuf_tensor("e7_" + n, sh, dt))
            R, FC = CAP // P, FFN // P
            xin, xT = sb("xin", [P, 2, R, D]), sb("xT", [D, 2, CAP])
            w1, w2 = sb("w1", [D, 2, FFN]), sb("w2", [P, 2, FC, D])
            hT, yo = sb("hT", [P, 2, FC, CAP]), sb("yo", [P, 2, R, D])
            psH = [K.psS[1], K.psT]

            def experts(eng, step):
                for e in range(2):
                    step(e, e, 0, True)
                with eng.Fori(1, E1 // 2 - 1) as p:
                    for j in range(2):
                        step(p * 2 + j, j, p, True)
                for j in range(2):
                    step(E1 - 2 + j, j, E1 // 2 - 1, j == 0)

            with nc.Block() as block:
                @block.sync
                def _(sp):
                    def value(x):
                        return x if isinstance(x, int) else sp.snap(x)

                    def load(e, par):
                        used = [value(e - 1), value(FC * (e - 1)), value(e - 1)]
                        src = [value(e * (CAP * D)), value(e * (D * FFN)), value(e * (FFN * D))]
                        wait(sp, s["turned"], used[0])
                        sp.dma_start(xin[:, par, :, :], bass.AP(xe.tensor, src[0], [[D, P], [P * D, R], [1, D]])).then_inc(
                            s[f"xin{par}"], 16)
                        wait(sp, s["h"], used[1])
                        sp.dma_start(w1[:, par, :], bass.AP(K.A["w1"].tensor, src[1], [[FFN, D], [1, FFN]])).then_inc(
                            s[f"w1in{par}"], 16)
                        wait(sp, s["y"], used[2])
                        sp.dma_start(w2[:, par, :, :], bass.AP(K.A["w2"].tensor, src[2], [[FC * D, P], [D, FC], [1, D]])).then_inc(
                            s[f"w2in{par}"], 16)

                    def store(e, par):
                        ready, dst = value(e + 1), value(e * (CAP * D))
                        sp.wait_ge(s["yout"], ready)
                        sp.dma_start(bass.AP(ye.tensor, dst, [[D, P], [P * D, R], [1, D]]), yo[:, par, :, :]).then_inc(
                            s[f"stored{par}"], 16)

                    load(0, 0)
                    load(1, 1)
                    store(0, 0)
                    with sp.Fori(1, E1 // 2) as p:
                        load(p * 2, 0)
                        store(p * 2 - 1, 1)
                        load(p * 2 + 1, 1)
                        store(p * 2, 0)
                    store(E1 - 1, 1)
                    for par in range(2):
                        sp.wait_ge(s[f"stored{par}"], 16 * E1 // 2)

                @block.tensor
                def _(pe):
                    def turn(e, par, used):
                        pe.wait_ge(s[f"xin{par}"], 16 * (used + 1))
                        wait(pe, s["xT"], e)
                        for r in range(R):
                            last = pe.transpose(K.psS[0][:, r * P:(r + 1) * P], xin[:, par, r, :], K.ident)
                        last.then_inc(s["turned"], 1)

                    def step(e, par, used, more):
                        pe.wait_ge(s["xT"], e + 1)
                        pe.wait_ge(s[f"w1in{par}"], 16 * (used + 1))
                        for f in range(FC):
                            wait(pe, s["gelu"], FC * e + f - 1)
                            for lo, n in ((0, 512), (512, CAP - 512)):
                                last = pe.matmul(psH[f % 2][:, lo:lo + n], w1[:, par, f * P:(f + 1) * P],
                                                 xT[:, par, lo:lo + n], start=True, stop=True)
                            last.then_inc(s["h"], 1)
                        if more:
                            turn(e + 1, 1 - par, used + par)
                        pe.wait_ge(s["gelu"], FC * (e + 1))
                        pe.wait_ge(s[f"w2in{par}"], 16 * (used + 1))
                        wait(pe, s["yout"], e)
                        for r in range(R):
                            dst = K.psO[:, r * D:(r + 1) * D] if r < 4 else K.psM[:, 0:D]
                            for f in range(FC):
                                last = pe.matmul(dst, hT[:, par, f, r * P:(r + 1) * P], w2[:, par, f, :],
                                                 start=(f == 0), stop=(f == FC - 1))
                        last.then_inc(s["y"], 1)

                    turn(0, 0, 0)
                    experts(pe, step)

                @block.scalar
                def _(act):
                    def step(e, par, used, more):
                        wait(act, s["y"], e - 1)
                        for f in range(FC):
                            act.wait_ge(s["h"], FC * e + f + 1)
                            act.activation(hT[:, par, f, :], psH[f % 2][:, 0:CAP], ACT.Gelu).then_inc(s["gelu"], 1)

                    experts(act, step)

                @block.vector
                def _(dve):
                    def rows_in(e, par):
                        dve.wait_ge(s["turned"], e + 1)
                        wait(dve, s["h"], FC * (e - 1))
                        dve.tensor_copy(xT[:, par, :], K.psS[0][:, 0:CAP]).then_inc(s["xT"], 1)

                    def step(e, par, used, more):
                        if more:
                            rows_in(e + 1, 1 - par)
                        dve.wait_ge(s["y"], e + 1)
                        wait(dve, s[f"stored{par}"], 16 * used)
                        dve.tensor_copy(yo[:, par, 0:4, :], K.psO[:, :].rearrange("p (r d) -> p r d", r=4))
                        dve.tensor_copy(yo[:, par, 4, :], K.psM[:, 0:D]).then_inc(s["yout"], 1)

                    rows_in(0, 0)
                    experts(dve, step)

        with ExitStack() as st:
            s = K.sems(st, "f7_", "gathered0 gathered1 gathered2 gathered3 weighted added stored")
            got = st.enter_context(nc.sbuf_tensor("f7_got", [P, TILES, TOPK, D], F32))
            PARTS = 4
            per = TILES // PARTS
            with nc.Block() as block:
                @block.gpsimd
                def _(pool):
                    for t in range(TILES):
                        for k in range(TOPK):
                            pool.indirect_dma_start(got[:, t, k, :], None, ye,
                                                    bass.IndirectOffsetOnAxis(ap=back[:, k, t:t + 1], axis=0)).then_inc(
                                                        s[f"gathered{t // per}"], 16)

                @block.vector
                def _(dve):
                    for part in range(PARTS):
                        tiles = slice(part * per, (part + 1) * per)
                        dve.wait_ge(s[f"gathered{part}"], 16 * per * TOPK)
                        for k in range(TOPK):
                            last = dve.tensor_tensor(got[:, tiles, k, :], got[:, tiles, k, :],
                                                     bc(weight[:, k, tiles].unsqueeze(2), [P, per, D]), ALU.mult)
                        last.then_inc(s["weighted"], 1)
                        dve.wait_ge(s["weighted"], part + 1)
                        for k in range(TOPK):
                            dve.tensor_tensor(K.X[:, tiles, :], K.X[:, tiles, :], got[:, tiles, k, :], ALU.add).then_inc(
                                s["added"], 1)
                            dve.wait_ge(s["added"], TOPK * part + k + 1)

                @block.sync
                def _(sp):
                    dst = K.out.rearrange("(t b) q d -> (b q) t d", b=TB)
                    for part in range(PARTS):
                        tiles = slice(part * per, (part + 1) * per)
                        sp.wait_ge(s["added"], TOPK * (part + 1))
                        sp.dma_start(dst[:, tiles, :], K.X[:, tiles, :]).then_inc(s["stored"], 16)
                    sp.wait_ge(s["stored"], 16 * PARTS)




def kernel(**inputs):
    import numpy as np
    import concourse.bacc as bacc
    from concourse.bass_utils import run_bass_kernel_spmd as run

    I = {k: np.asarray(v) for k, v in inputs.items()}
    f = np.float32

    def chunked(a, n):
        return a.reshape(n, P, -1).transpose(1, 0, 2).reshape(P, -1)

    def experts(a):
        return a.transpose(1, 0, 2).reshape(P, -1)

    p = np.arange(P)
    qkv5 = I["L1_ffn_qkv_weight"].reshape(8, 32, D)
    pack = {
        "WQT": chunked(I["L0_xattn_WQ"].T, 8), "WKT": chunked(I["L0_xattn_WK"].T, 8), "WVT": chunked(I["L0_xattn_WV"].T, 8),
        "WO": chunked(I["L0_xattn_WO"], 8),
        "ident": np.eye(P, dtype=f), "headmask": (p[:, None] // HD == np.arange(HEADS)).astype(f),
        "quadmask": (p[:, None] % 32 // HD == np.arange(4)).astype(f), "mask8": (p[:, None] % 64 // HD == np.arange(8)).astype(f),
        "blockmask": (p[:, None] // 32 == np.arange(4)).astype(f),
        "batch": (p[:, None] == p[None, :] // S).astype(f), "tri": (p[:, None] < p[None, :]).astype(f),
        "ones": np.ones((P, P), f),
        "expert": np.broadcast_to(np.arange(8, dtype=f), (P, 8)),
        "repq": (p[:, None] == p[None, :] % 32).astype(f),
        "causal": np.where(np.arange(32)[None, :] > p[:, None], 1.0, 0.0).astype(f),
        "token": (p[:, None] + P * np.arange(16)[None, :]).astype(f),
        "qkvT": I["L0_attn_qkv_w"].T, "projT": I["L0_attn_proj_w"].T, "conv1T": I["L0_attn_conv1_w"].T,
        "conv2T": chunked(I["L0_attn_conv2_w"].T, 2), "scale1": I["L0_attn_scale1"][:, None],
        "scale2": I["L0_attn_scale2"][:, None], "conv1_b": I["L0_attn_conv1_b"].reshape(2, P).T,
        "rw": I["L0_ffn_router_w"], "wq": experts(I["L0_ffn_wq"]), "wk": experts(I["L0_ffn_wk"]),
        "wv": experts(I["L0_ffn_wv"]), "wo": experts(I["L0_ffn_wo"]), "bq": I["L0_ffn_bq"].T, "bk": I["L0_ffn_bk"].T,
        "W_outT": I["L1_xattn_W_out"].T, "WqT": I["L1_attn_Wq"].T, "WkT": I["L1_attn_Wk"].T,
        "WvT": I["L1_attn_Wv"].T, "WoT": I["L1_attn_Wo"].T, "bq1": I["L1_attn_bq"][:, None],
        "bk1": I["L1_attn_bk"][:, None], "relT": np.tile(I["L1_attn_rel_emb"][192:320].T, (16, 1)),
        "q5T": qkv5[:, 0:16].reshape(P, D).T, "k5T": np.repeat(qkv5[:, 16:24], 2, axis=0).reshape(P, D).T,
        "v5T": np.repeat(qkv5[:, 24:32], 2, axis=0).reshape(P, D).T, "proj5T": I["L1_ffn_proj_weight"].T,
        "rw5": I["L1_ffn_router_weight"],
    }
    for n, width in PACK:
        assert pack[n].shape == (P, width), (n, pack[n].shape)
    rows = {"bO": "L0_xattn_bO", "gamma": "L0_attn_gamma", "proj_b": "L0_attn_proj_b", "conv2_b": "L0_attn_conv2_b",
            "rb": "L0_ffn_router_b", "bv": "L0_ffn_bv", "bo": "L0_ffn_bo", "b_out": "L1_xattn_b_out",
            "bv1": "L1_attn_bv", "bo1": "L1_attn_bo", "ln1w": "L1_ffn_ln1_weight", "ln1b": "L1_ffn_ln1_bias",
            "ln2w": "L1_ffn_ln2_weight", "ln2b": "L1_ffn_ln2_bias"}
    arrays = {
        "x": I["x"].reshape(TILES, P, D), "ctx": I["ctx_1024"], "ctxT": I["ctx_1024"].transpose(0, 2, 1),
        "ctxS": I["ctx_1024"].reshape(TILES, TB, KEYS, 2, D // 2).transpose(1, 4, 0, 3, 2).reshape(P, TILES, 2, KEYS),
        "mask": I["mask_Bx1xSxS2_ik1"].reshape(TILES, P, KEYS),
        "w1": I["L1_ffn_moe_w1"], "w2": I["L1_ffn_moe_w2"].reshape(E1, FFN // P, P, D).transpose(0, 2, 1, 3),
        "wpack": np.concatenate([pack[n] for n, _ in PACK], 1),
        "rpack": np.concatenate([I[rows[n]].reshape(-1) for n, _ in ROWS]),
    }
    arrays = {k: np.ascontiguousarray(v) for k, v in arrays.items()}
    nc = bacc.Bacc("TRN2", target_bir_lowering=False, num_devices=1)
    aps = {k: nc.dram_tensor(f"in_{k}", v.shape, mybir.dt.from_np(v.dtype), kind="ExternalInput").ap()
           for k, v in arrays.items()}
    out = nc.dram_tensor("out_x", (B, S, D), F32, kind="ExternalOutput").ap()
    build(nc, aps, out)
    r = run(nc, [{f"in_{k}": v for k, v in arrays.items()}], core_ids=[0])
    return r.results[0]["out_x"]
```
